# Optimizing a Trainium2 kernel written in Bass

```python
import numpy as np
import jax
import jax.numpy as jnp

def _softmax(x, axis=-1):
    return jax.nn.softmax(x, axis=axis)

def _gelu(x):
    return jax.nn.gelu(x, approximate=True)

def _silu(x):
    return jax.nn.silu(x)

def _sigmoid(x):
    return jax.nn.sigmoid(x)

def _layernorm(x, axis=-1, eps=1e-05):
    m = jnp.mean(x, axis=axis, keepdims=True)
    v = jnp.var(x, axis=axis, keepdims=True)
    return (x - m) / jnp.sqrt(v + eps)

def _scatter_add(tgt, idx, src, axis=0):
    return tgt.at[idx].add(src)

def _segment_sum(src, seg, n):
    return jax.ops.segment_sum(src, seg, n)
kernel_name = 'mk_sandwich_d2_jaxref_r8_bbb123'

def setup_inputs(seed: int=0):
    np.random.seed(seed)
    _w = jnp.asarray

    def _L0_attn_setup():
        import jax, jax.numpy as jnp
        import numpy as np
        B, T, D, H = (4, 256, 128, 16)
        HD = D // H
        NEG = -np.finfo(np.float32).max
        key = jax.random.key(seed)
        ks = jax.random.split(key, 9)
        s = 1.0 / np.sqrt(D)
        return {'x': jax.random.normal(ks[0], (B, T, D), jnp.float32), 'wq': jax.random.normal(ks[1], (D, D), jnp.float32) * s, 'bq': jax.random.normal(ks[2], (D,), jnp.float32) * 0.02, 'wk': jax.random.normal(ks[3], (D, D), jnp.float32) * s, 'bk': jax.random.normal(ks[4], (D,), jnp.float32) * 0.02, 'wv': jax.random.normal(ks[5], (D, D), jnp.float32) * s, 'bv': jax.random.normal(ks[6], (D,), jnp.float32) * 0.02, 'wo': jax.random.normal(ks[7], (D, D), jnp.float32) * s, 'bo': jax.random.normal(ks[8], (D,), jnp.float32) * 0.02}
    _L0_attn_in = _L0_attn_setup()

    def _L0_ffn_setup():
        import jax, jax.numpy as jnp
        import numpy as np
        EPS = 1e-06
        LN_EPS = 1e-05

        def _absmean_core(W):
            gamma = jnp.mean(jnp.abs(W)) + EPS
            Ws = W / gamma
            Wq = jnp.sign(Ws) * jnp.minimum(jnp.round(jnp.abs(Ws)), 1.0)
            return (Wq, gamma)

        @jax.custom_vjp
        def absmean(W):
            return _absmean_core(W)[0]

        def _absmean_fwd(W):
            Wq, gamma = _absmean_core(W)
            return (Wq, gamma)

        def _absmean_bwd(gamma, g):
            return (g / gamma,)
        absmean.defvjp(_absmean_fwd, _absmean_bwd)

        def layernorm(x, w, b, eps=LN_EPS):
            mu = jnp.mean(x, axis=-1, keepdims=True)
            var = jnp.mean((x - mu) ** 2, axis=-1, keepdims=True)
            return (x - mu) * jax.lax.rsqrt(var + eps) * w + b
        key = jax.random.key(seed)
        k1, k2, k3 = jax.random.split(key, 3)
        d, h = (128, 512)
        B, T = (8, 256)
        return {'x': jax.random.normal(k1, (B, T, d), jnp.float32), 'W_fc': jax.random.normal(k2, (h, d), jnp.float32), 'ln_w': jnp.ones((h,), jnp.float32), 'ln_b': jnp.zeros((h,), jnp.float32), 'W_proj': jax.random.normal(k3, (d, h), jnp.float32)}
    _L0_ffn_in = _L0_ffn_setup()

    def _L1_attn_setup():
        import jax, jax.numpy as jnp
        import numpy as np
        N_EMBD = 128
        N_HEAD = 16
        HEAD_SIZE = 64
        LN_EPS = 0.001
        key = jax.random.key(seed)
        ks = jax.random.split(key, 7)
        B, S, D, H, E = (4, 256, N_EMBD, N_HEAD, HEAD_SIZE)
        x = jax.random.normal(ks[0], (B, S, D), dtype=jnp.float32)
        scale = 1.0 / np.sqrt(D)
        Wq = jax.random.normal(ks[1], (H, D, E), dtype=jnp.float32) * scale
        Wk = jax.random.normal(ks[2], (H, D, E), dtype=jnp.float32) * scale
        Wv = jax.random.normal(ks[3], (H, D, E), dtype=jnp.float32) * scale
        Wo = jax.random.normal(ks[4], (H * E, D), dtype=jnp.float32) * scale
        gamma = jnp.ones((D,), dtype=jnp.float32)
        beta = jnp.zeros((D,), dtype=jnp.float32)
        return {'x': x, 'Wq': Wq, 'Wk': Wk, 'Wv': Wv, 'Wo': Wo, 'gamma': gamma, 'beta': beta}
    _L1_attn_in = _L1_attn_setup()

    def _L1_ffn_setup():
        import jax, jax.numpy as jnp
        import numpy as np
        D_MODEL = 128
        N_HEAD = 16
        HEAD_DIM = D_MODEL // N_HEAD
        D_FF = 512
        N_EXPERTS = 4
        EPS = 1e-05

        def _layer_norm(x, gamma, beta):
            mu = jnp.mean(x, axis=-1, keepdims=True)
            var = jnp.mean((x - mu) ** 2, axis=-1, keepdims=True)
            return (x - mu) / jnp.sqrt(var + EPS) * gamma + beta
        key = jax.random.key(seed)
        ks = jax.random.split(key, 20)
        f32 = jnp.float32
        sc = 1.0 / np.sqrt(D_MODEL)
        scf = 1.0 / np.sqrt(D_FF)
        return {'src': jax.random.normal(ks[0], (4, 64, D_MODEL), f32), 'Wq': jax.random.normal(ks[1], (D_MODEL, D_MODEL), f32) * sc, 'bq': jnp.zeros((D_MODEL,), f32), 'Wk': jax.random.normal(ks[2], (D_MODEL, D_MODEL), f32) * sc, 'bk': jnp.zeros((D_MODEL,), f32), 'Wv': jax.random.normal(ks[3], (D_MODEL, D_MODEL), f32) * sc, 'bv': jnp.zeros((D_MODEL,), f32), 'Wo': jax.random.normal(ks[4], (D_MODEL, D_MODEL), f32) * sc, 'bo': jnp.zeros((D_MODEL,), f32), 'router_w': jax.random.normal(ks[5], (D_MODEL, 1), f32) * 0.05, 'router_b': jnp.zeros((1,), f32), 'W1': jax.random.normal(ks[6], (N_EXPERTS, D_MODEL, D_FF), f32) * sc, 'b1': jnp.zeros((N_EXPERTS, D_FF), f32), 'W2': jax.random.normal(ks[7], (N_EXPERTS, D_FF, D_MODEL), f32) * scf, 'b2': jnp.zeros((N_EXPERTS, D_MODEL), f32), 'ln1_g': jnp.ones((D_MODEL,), f32), 'ln1_b': jnp.zeros((D_MODEL,), f32), 'ln2_g': jnp.ones((D_MODEL,), f32), 'ln2_b': jnp.zeros((D_MODEL,), f32)}
    _L1_ffn_in = _L1_ffn_setup()
    _d = {'L0_attn_x': _L0_attn_in['x'], 'L0_attn_wq': _L0_attn_in['wq'], 'L0_attn_bq': _L0_attn_in['bq'], 'L0_attn_wk': _L0_attn_in['wk'], 'L0_attn_bk': _L0_attn_in['bk'], 'L0_attn_wv': _L0_attn_in['wv'], 'L0_attn_bv': _L0_attn_in['bv'], 'L0_attn_wo': _L0_attn_in['wo'], 'L0_attn_bo': _L0_attn_in['bo'], 'L0_ffn_W_fc': _L0_ffn_in['W_fc'], 'L0_ffn_ln_w': _L0_ffn_in['ln_w'], 'L0_ffn_ln_b': _L0_ffn_in['ln_b'], 'L0_ffn_W_proj': _L0_ffn_in['W_proj'], 'L1_attn_Wq': _L1_attn_in['Wq'], 'L1_attn_Wk': _L1_attn_in['Wk'], 'L1_attn_Wv': _L1_attn_in['Wv'], 'L1_attn_Wo': _L1_attn_in['Wo'], 'L1_attn_gamma': _L1_attn_in['gamma'], 'L1_attn_beta': _L1_attn_in['beta'], 'L1_ffn_Wq': _L1_ffn_in['Wq'], 'L1_ffn_bq': _L1_ffn_in['bq'], 'L1_ffn_Wk': _L1_ffn_in['Wk'], 'L1_ffn_bk': _L1_ffn_in['bk'], 'L1_ffn_Wv': _L1_ffn_in['Wv'], 'L1_ffn_bv': _L1_ffn_in['bv'], 'L1_ffn_Wo': _L1_ffn_in['Wo'], 'L1_ffn_bo': _L1_ffn_in['bo'], 'L1_ffn_router_w': _L1_ffn_in['router_w'], 'L1_ffn_router_b': _L1_ffn_in['router_b'], 'L1_ffn_W1': _L1_ffn_in['W1'], 'L1_ffn_b1': _L1_ffn_in['b1'], 'L1_ffn_W2': _L1_ffn_in['W2'], 'L1_ffn_b2': _L1_ffn_in['b2'], 'L1_ffn_ln1_g': _L1_ffn_in['ln1_g'], 'L1_ffn_ln1_b': _L1_ffn_in['ln1_b'], 'L1_ffn_ln2_g': _L1_ffn_in['ln2_g'], 'L1_ffn_ln2_b': _L1_ffn_in['ln2_b']}
    _x0 = _d['L0_attn_x']
    _d['L0_attn_x'] = jax.random.normal(jax.random.fold_in(jax.random.key(seed), 1), (8, 512, 128), dtype=_x0.dtype)
    del _x0
    return _d

def reference(L0_attn_x, L0_attn_wq, L0_attn_bq, L0_attn_wk, L0_attn_bk, L0_attn_wv, L0_attn_bv, L0_attn_wo, L0_attn_bo, L0_ffn_W_fc, L0_ffn_ln_w, L0_ffn_ln_b, L0_ffn_W_proj, L1_attn_Wq, L1_attn_Wk, L1_attn_Wv, L1_attn_Wo, L1_attn_gamma, L1_attn_beta, L1_ffn_Wq, L1_ffn_bq, L1_ffn_Wk, L1_ffn_bk, L1_ffn_Wv, L1_ffn_bv, L1_ffn_Wo, L1_ffn_bo, L1_ffn_router_w, L1_ffn_router_b, L1_ffn_W1, L1_ffn_b1, L1_ffn_W2, L1_ffn_b2, L1_ffn_ln1_g, L1_ffn_ln1_b, L1_ffn_ln2_g, L1_ffn_ln2_b):

    def _L0_attn_ref(x, wq, bq, wk, bk, wv, bv, wo, bo):
        import jax, jax.numpy as jnp
        import numpy as np
        B, T, D, H = (4, 256, 128, 16)
        HD = D // H
        NEG = -np.finfo(np.float32).max
        b, t, d = x.shape

        def proj(w, bias):
            y = x @ w + bias
            return y.reshape(b, t, H, HD).transpose(0, 2, 1, 3)
        q = proj(wq, bq)
        k = proj(wk, bk)
        v = proj(wv, bv)
        scale = 1.0 / np.sqrt(HD).astype(np.float32)
        scores = jnp.einsum('bhqd,bhkd->bhqk', q, k) * scale
        mask = jnp.triu(jnp.full((t, t), NEG, jnp.float32), k=1)
        attn = jax.nn.softmax(scores + mask, axis=-1)
        out = jnp.einsum('bhqk,bhkd->bhqd', attn, v)
        out = out.transpose(0, 2, 1, 3).reshape(b, t, d)
        return out @ wo + bo

    def _L0_ffn_ref(x, W_fc, ln_w, ln_b, W_proj):
        import jax, jax.numpy as jnp
        import numpy as np
        EPS = 1e-06
        LN_EPS = 1e-05

        def _absmean_core(W):
            gamma = jnp.mean(jnp.abs(W)) + EPS
            Ws = W / gamma
            Wq = jnp.sign(Ws) * jnp.minimum(jnp.round(jnp.abs(Ws)), 1.0)
            return (Wq, gamma)

        @jax.custom_vjp
        def absmean(W):
            return _absmean_core(W)[0]

        def _absmean_fwd(W):
            Wq, gamma = _absmean_core(W)
            return (Wq, gamma)

        def _absmean_bwd(gamma, g):
            return (g / gamma,)
        absmean.defvjp(_absmean_fwd, _absmean_bwd)

        def layernorm(x, w, b, eps=LN_EPS):
            mu = jnp.mean(x, axis=-1, keepdims=True)
            var = jnp.mean((x - mu) ** 2, axis=-1, keepdims=True)
            return (x - mu) * jax.lax.rsqrt(var + eps) * w + b
        h = jnp.einsum('btd,hd->bth', x, absmean(W_fc))
        h = jax.nn.gelu(h, approximate=False)
        h = layernorm(h, ln_w, ln_b)
        return jnp.einsum('bth,dh->btd', h, absmean(W_proj))

    def _L1_attn_ref(x, Wq, Wk, Wv, Wo, gamma, beta):
        import jax, jax.numpy as jnp
        import numpy as np
        N_EMBD = 128
        N_HEAD = 16
        HEAD_SIZE = 64
        LN_EPS = 0.001
        B, S, D = x.shape
        H, _, E = Wq.shape
        q = jnp.einsum('bsd,hde->bhse', x, Wq)
        k = jnp.einsum('bsd,hde->bhse', x, Wk)
        v = jnp.einsum('bsd,hde->bhse', x, Wv)
        scores = jnp.einsum('bhse,bhte->bhst', q, k)
        causal = jnp.tril(jnp.ones((S, S), dtype=bool))
        scores = jnp.where(causal, scores / jnp.sqrt(jnp.float32(E)), jnp.float32(-jnp.inf))
        attn = jax.nn.softmax(scores, axis=-1)
        out = jnp.einsum('bhst,bhte->bhse', attn, v)
        heads = out.transpose(0, 2, 1, 3).reshape(B, S, H * E)
        y = x + heads @ Wo
        mu = jnp.mean(y, axis=-1, keepdims=True)
        var = jnp.mean(jnp.square(y - mu), axis=-1, keepdims=True)
        y = (y - mu) * jax.lax.rsqrt(var + LN_EPS) * gamma + beta
        return y

    def _L1_ffn_ref(src, Wq, bq, Wk, bk, Wv, bv, Wo, bo, router_w, router_b, W1, b1, W2, b2, ln1_g, ln1_b, ln2_g, ln2_b):
        import jax, jax.numpy as jnp
        import numpy as np
        D_MODEL = 128
        N_HEAD = 16
        HEAD_DIM = D_MODEL // N_HEAD
        D_FF = 512
        N_EXPERTS = 4
        EPS = 1e-05

        def _layer_norm(x, gamma, beta):
            mu = jnp.mean(x, axis=-1, keepdims=True)
            var = jnp.mean((x - mu) ** 2, axis=-1, keepdims=True)
            return (x - mu) / jnp.sqrt(var + EPS) * gamma + beta
        B, T, _ = src.shape
        q = (src @ Wq + bq).reshape(B, T, N_HEAD, HEAD_DIM)
        k = (src @ Wk + bk).reshape(B, T, N_HEAD, HEAD_DIM)
        v = (src @ Wv + bv).reshape(B, T, N_HEAD, HEAD_DIM)
        scale = HEAD_DIM ** (-0.5)
        scores = jnp.einsum('bqhd,bkhd->bhqk', q, k) * scale
        probs = jax.nn.softmax(scores, axis=-1)
        attn = jnp.einsum('bhqk,bkhd->bqhd', probs, v).reshape(B, T, D_MODEL)
        attn = attn @ Wo + bo
        x = _layer_norm(src + attn, ln1_g, ln1_b)
        keys = (x @ router_w + router_b)[..., 0]
        expert_idx = jnp.remainder(jnp.floor(keys).astype(jnp.int32), N_EXPERTS)
        ff_out = jnp.zeros_like(x)
        for e in range(N_EXPERTS):
            h = jax.nn.relu(x @ W1[e] + b1[e])
            y = h @ W2[e] + b2[e]
            ff_out = ff_out + jnp.where((expert_idx == e)[..., None], y, 0.0)
        return _layer_norm(x + ff_out, ln2_g, ln2_b)
    x = L0_attn_x
    x = x + _layernorm(_L0_attn_ref(_layernorm(x, axis=-1), L0_attn_wq, L0_attn_bq, L0_attn_wk, L0_attn_bk, L0_attn_wv, L0_attn_bv, L0_attn_wo, L0_attn_bo), axis=-1)
    x = x + _layernorm(_L0_ffn_ref(_layernorm(x, axis=-1), L0_ffn_W_fc, L0_ffn_ln_w, L0_ffn_ln_b, L0_ffn_W_proj), axis=-1)
    x = x + _layernorm(_L1_attn_ref(_layernorm(x, axis=-1), L1_attn_Wq, L1_attn_Wk, L1_attn_Wv, L1_attn_Wo, L1_attn_gamma, L1_attn_beta), axis=-1)
    x = x + _layernorm(_L1_ffn_ref(_layernorm(x, axis=-1), L1_ffn_Wq, L1_ffn_bq, L1_ffn_Wk, L1_ffn_bk, L1_ffn_Wv, L1_ffn_bv, L1_ffn_Wo, L1_ffn_bo, L1_ffn_router_w, L1_ffn_router_b, L1_ffn_W1, L1_ffn_b1, L1_ffn_W2, L1_ffn_b2, L1_ffn_ln1_g, L1_ffn_ln1_b, L1_ffn_ln2_g, L1_ffn_ln2_b), axis=-1)
    return x

_drawn_inputs = setup_inputs


def setup_inputs(seed=0):
    import zlib

    import numpy as np

    out = dict(_drawn_inputs(seed))
    spreads = {'L0_ffn_ln_w': (1.0, 0.2),
     'L0_ffn_ln_b': (0.0, 0.1),
     'L1_attn_gamma': (1.0, 0.2),
     'L1_attn_beta': (0.0, 0.1),
     'L1_ffn_bq': (0.0, 0.639),
     'L1_ffn_bk': (0.0, 0.8),
     'L1_ffn_bv': (0.0, 0.1),
     'L1_ffn_bo': (0.0, 0.1),
     'L1_ffn_b1': (0.0, 0.447),
     'L1_ffn_b2': (0.0, 0.305),
     'L1_ffn_ln1_g': (1.0, 0.2),
     'L1_ffn_ln1_b': (0.0, 0.1),
     'L1_ffn_ln2_g': (1.0, 0.2),
     'L1_ffn_ln2_b': (0.0, 0.1)}
    factors = {'L0_attn_bk': 8.0}
    for name, (base, spread) in spreads.items():
        noise = np.random.default_rng([zlib.crc32(name.encode()), seed]).standard_normal(out[name].shape)
        drawn = base * np.exp(spread * noise) if base else spread * noise
        out[name] = jnp.asarray(drawn.astype(out[name].dtype))
    for name, factor in factors.items():
        out[name] = (out[name] * factor).astype(out[name].dtype)
    return out
```

```python
from contextlib import ExitStack

import concourse.bass as bass
from concourse import mybir

F32 = mybir.dt.float32
BF16 = mybir.dt.bfloat16
ALU = mybir.AluOpType
ACT = mybir.ActivationFunctionType
AX = mybir.AxisListType

P = 128
BATCH, SEQ, D = 8, 512, 128
TILES = SEQ // P
ALL_TILES = BATCH * TILES
HEADS = 16
HD8 = D // HEADS
QUAD = 32
GROUPS = HEADS * QUAD // P
GH = HEADS // GROUPS
HD64 = 64
PAIRS = HEADS // 2
FF = 512
FC = FF // P
EXPERTS = 4
MASKED = -3.0e38


class Signal:

    def __init__(self, sem, per_turn):
        self.sem, self.per_turn = sem, per_turn

    def at(self, turn, k):
        return turn * self.per_turn + k


class Core:

    def __init__(self, nc, ctx):
        self.nc, self.ctx = nc, ctx

    def sbuf(self, name, shape, dtype=F32, ctx=None):
        return (ctx or self.ctx).enter_context(self.nc.sbuf_tensor(name, shape, dtype))

    def semaphore(self, name, per_turn=1):
        return Signal(self.ctx.enter_context(self.nc.semaphore(name)), per_turn)


def make_link(dve, signal, turn):
    count = [0]

    def link(instruction):
        count[0] += 1
        instruction.then_inc(signal.sem, 1)
        dve.wait_ge(signal.sem, signal.at(turn, count[0]))

    def finish():
        assert count[0] == signal.per_turn, (count[0], signal.per_turn)

    return link, finish


def norm_statistics(nc, link, s, source, tiles, width):
    for c in range(tiles):
        last = nc.vector.bn_stats(s.stats[:, c, :], source(c))
    link(last)
    nc.vector.tensor_copy(s.carrier[:, :], s.stats[:, 0, 0:1])
    for c in range(tiles):
        last = nc.vector.bn_aggr(s.mean_var[:, c, :], s.stats[:, c, :])
    link(last)


def normalise(nc, dve, link, s, turn, k, source, target, eps, done=None):
    norm_statistics(nc, link, s, source, TILES, D)
    nc.vector.tensor_scalar(s.var_eps[:, :], s.mean_var[:, :, 1], eps, None, ALU.add).then_inc(s.var_ready.sem, 1)
    dve.wait_ge(s.rstd_ready.sem, s.rstd_ready.at(turn, k + 1))
    for c in range(TILES):
        last = nc.vector.tensor_scalar(target(c), source(c), s.mean_var[:, c, 0:1], s.rstd[:, c:c + 1],
                                       ALU.subtract, ALU.mult)
        if done is not None:
            last.then_inc(done.sem, 1)
    return last


def inverse_roots(nc, pool, s, turn, ks):
    for k in ks:
        pool.wait_ge(s.var_ready.sem, s.var_ready.at(turn, k + 1))
        nc.gpsimd.tensor_tensor(s.rstd[:, :], s.var_eps[:, :], s.minus_half[:, :], ALU.pow).then_inc(
            s.rstd_ready.sem, 1)


class Narrow:

    def __init__(self, core, name, tag, causal, ctx):
        sb = lambda n, shape, dtype=F32: core.sbuf(f"{name}_{n}", shape, dtype, ctx)
        self.stats = sb("stats", [P, TILES, 6])
        self.mean_var = sb("mean_var", [P, TILES, 2])
        self.carrier = sb("carrier", [P, 1])
        self.var_eps = sb("var_eps", [P, TILES])
        self.rstd = sb("rstd", [P, TILES])
        self.minus_half = core.minus_half
        self.pool_carrier = sb("pool_carrier", [P, 1])
        self.xn = sb("xn", [P, TILES, D])
        self.xt = sb("xt", [P, SEQ])
        self.qk = sb("qk", [P, TILES, 2, D])
        self.v = sb("v", [P, TILES, HEADS, HD8 + 1])
        self.q_parts = sb("q_parts", [P, TILES, HEADS, QUAD], BF16)
        self.k_parts = sb("k_parts", [P, TILES, HEADS, QUAD], BF16)
        self.qkt = sb("qkt", [P, GROUPS, 2, SEQ], BF16)
        self.q_alone = sb("q_alone", [P, HEADS, SEQ], BF16)
        self.neg_max = sb("neg_max", [P, GROUPS, TILES, GH])
        self.max_parts = sb("max_parts", [P, GROUPS, TILES, GH, 2], BF16)
        self.max_t = sb("max_t", [2 * GH, GROUPS, SEQ], BF16)
        self.probs = sb("probs", [P, 2 * GH, SEQ])
        self.out_t = sb("out_t", [P, GROUPS, SEQ])
        self.inverse = sb("inverse", [P, TILES, HEADS])
        self.attn = sb("attn", [P, TILES, D])
        self.attn_t = sb("attn_t", [P, SEQ])
        self.y = sb("y", [P, TILES, D])
        self.y_norm = sb("y_norm", [P, TILES, D])
        if causal:
            self.units = [[(0, 0, 0, 512)], [(1, 128, 0, 384), (3, 384, 384, 128)], [(2, 256, 0, 256)]]
        else:
            self.units = [[(k, 0, 0, SEQ)] for k in range(TILES)]
        self.causal = causal
        units = GROUPS * len(self.units)
        sig = lambda n, per=1: core.semaphore(f"{tag}_{n}", per)
        self.link = sig("link", 14 if causal else 16)
        self.ready = sig("ready")
        self.var_ready = sig("var_ready", 2)
        self.rstd_ready = sig("rstd_ready", 2)
        self.xn_ready = sig("xn_ready", TILES)
        self.xt_summed = sig("xt_summed")
        self.xt_ready = sig("xt_ready")
        self.qkv_summed = sig("qkv_summed", TILES)
        self.qkv_ready = sig("qkv_ready", TILES)
        self.high_ready = sig("high_ready", 4)
        self.low_ready = sig("low_ready", 2)
        self.parts_turned = sig("parts_turned", GROUPS)
        self.qkt_by_act = sig("qkt_by_act", GROUPS // 2)
        self.qkt_by_dve = sig("qkt_by_dve", GROUPS // 2)
        self.q_alone_ready = sig("q_alone_ready", 16 * GH)
        self.row_scores = sig("row_scores", GROUPS * TILES * 2)
        self.row_max = sig("row_max", GROUPS * TILES * 2)
        self.max_ready = sig("max_ready", GROUPS)
        self.max_turned = sig("max_turned", GROUPS)
        self.max_t_ready = sig("max_t_ready", GROUPS)
        self.max_placed = [sig(f"max_placed{g}", 16 * GH) for g in range(GROUPS)]
        self.scores = sig("scores", units * GH)
        self.exp_done = sig("exp_done", units * GH)
        self.masked = sig("masked", units)
        self.pv_done = sig("pv_done", units)
        self.out_t_ready = sig("out_t_ready", GROUPS)
        self.out_turned = sig("out_turned", TILES)
        self.attn_ready = sig("attn_ready", TILES)
        self.attn_turned = sig("attn_turned")
        self.attn_t_ready = sig("attn_t_ready")
        self.wo_summed = sig("wo_summed")
        self.wo_read = sig("wo_read")


def narrow_attention(core, name, tag, causal, w_qkv, b_qkv, w_o, b_o, weights, result, eps=1e-5):
    nc, X, PS = core.nc, core.X, core.PS
    PB = PS.bitcast(BF16)
    scale = float(HD8) ** -0.5
    ident, ident_b = core.ident, core.ident_b
    ST, TURN, OUT = 4, 6, 7

    with ExitStack() as ctx:
        s = Narrow(core, name, tag, causal, ctx)
        units = s.units
        nu = len(units)
        block = ctx.enter_context(nc.Block())

        @block.sync
        def _(sp):
            with sp.Fori(0, BATCH) as turn:
                sp.wait_ge(s.qkt_by_act.sem, s.qkt_by_act.at(turn, 2))
                sp.wait_ge(s.qkt_by_dve.sem, s.qkt_by_dve.at(turn, 2))
                alone = s.q_alone[:, :, :].rearrange("p (g j) t -> p g j t", j=GH)
                for j in range(GH):
                    rows = slice(QUAD * j, QUAD * (j + 1))
                    sp.dma_start(alone[rows, :, j, :], s.qkt[rows, :, 0, :]).then_inc(s.q_alone_ready.sem, 16)
                for g in range(GROUPS):
                    sp.wait_ge(s.max_t_ready.sem, s.max_t_ready.at(turn, g + 1))
                    for j in range(GH):
                        first = QUAD * j + 3 * HD8
                        sp.dma_start(s.q_alone[first:first + 2, GH * g + j, :],
                                     s.max_t[2 * j:2 * j + 2, g, :]).then_inc(s.max_placed[g].sem, 16)

        @block.gpsimd
        def _(pool):
            nc.gpsimd.memset(s.v[:, :, :, HD8:], 1.0)
            nc.gpsimd.memset(s.q_parts[:, :, :, 3 * HD8:], 0.0)
            nc.gpsimd.memset(s.k_parts[:, :, :, 3 * HD8:3 * HD8 + 2], 1.0)
            nc.gpsimd.memset(s.k_parts[:, :, :, 3 * HD8 + 2:], 0.0)
            nc.gpsimd.memset(s.q_alone[:, :, :], 0.0).then_inc(s.ready.sem, 1)
            with pool.Fori(0, BATCH) as turn:
                inverse_roots(nc, pool, s, turn, [0])
                if causal:
                    for n in range(GROUPS * nu):
                        blocks = [column for _, _, column, _ in units[n % nu]]
                        pool.wait_ge(s.exp_done.sem, s.exp_done.at(turn, GH * (n + 1)))
                        if n:
                            pool.wait_ge(s.masked.sem, s.masked.at(turn, n))
                        nc.gpsimd.tensor_tensor(s.pool_carrier[:, :], s.minus_half[:, 0:1], s.minus_half[:, 0:1],
                                                ALU.add)
                        slot = n % 2 * GH
                        for at in blocks:
                            square = s.probs[:, slot:slot + GH, at:at + P]
                            last = nc.gpsimd.affine_select(out=square, in_=square, compare_op=ALU.is_ge, fill=0.0,
                                                           base=0, pattern=[[0, GH], [1, P]], channel_multiplier=-1)
                        last.then_inc(s.masked.sem, 1)
                inverse_roots(nc, pool, s, turn, [1])

        @block.vector
        def _(dve):
            nc.vector.memset(PS[:, OUT, :], 0.0).then_inc(s.ready.sem, 1)
            dve.wait_ge(s.ready.sem, 2)
            for load in weights[1:]:
                dve.wait_ge(load.sem, load.per_turn)
            with dve.Fori(0, BATCH) as turn:
                link, finish = make_link(dve, s.link, turn)
                x = lambda c: X[:, turn * TILES + c, :]
                if tag == core.first_phase:
                    dve.wait_ge(core.x_first.sem, 16)
                normalise(nc, dve, link, s, turn, 0, x, lambda c: s.xn[:, c, :], eps, s.xn_ready)
                for c in range(TILES):
                    dve.wait_ge(s.qkv_summed.sem, s.qkv_summed.at(turn, c + 1))
                    nc.vector.tensor_tensor(s.qk[:, c, :, :].rearrange("p a d -> p (a d)"), PS[:, c, 0:2 * D],
                                            b_qkv[:, 0:2 * D], ALU.add)
                    nc.vector.tensor_tensor(s.v[:, c, :, 0:HD8],
                                            PS[:, c, 2 * D:3 * D].rearrange("p (h e) -> p h e", e=HD8),
                                            b_qkv[:, 2 * D:3 * D].rearrange("p (h e) -> p h e", e=HD8),
                                            ALU.add).then_inc(s.qkv_ready.sem, 1)
                for a, (parts, first) in enumerate(((s.q_parts, HD8), (s.k_parts, 2 * HD8))):
                    dve.wait_ge(s.high_ready.sem, s.high_ready.at(turn, 2 * a + 1))
                    nc.vector.tensor_tensor(parts[:, :, :, first:first + HD8],
                                            s.qk[:, :, a, :].rearrange("p c (h e) -> p c h e", e=HD8),
                                            parts[:, :, :, 0:HD8], ALU.subtract).then_inc(s.low_ready.sem, 1)
                for g in (0, 2):
                    dve.wait_ge(s.parts_turned.sem, s.parts_turned.at(turn, g + 1))
                    nc.vector.tensor_copy(s.qkt[:, g, :, :].rearrange("p a t -> p (a t)"),
                                          PB[:, ST + g, :]).then_inc(s.qkt_by_dve.sem, 1)
                for g in range(GROUPS):
                    for c in range(TILES):
                        keys = P * (c + 1) if causal else SEQ
                        for half in range(2):
                            n = (g * TILES + c) * 2 + half
                            dve.wait_ge(s.row_scores.sem, s.row_scores.at(turn, n + 1))
                            bank = n % 2 * 2
                            nc.vector.tensor_reduce(s.neg_max[:, g, c, 2 * half:2 * half + 2],
                                                    PS[:, bank:bank + 2, 0:keys], AX.X, ALU.max,
                                                    negate=True).then_inc(s.row_max.sem, 1)
                    dve.wait_ge(s.row_max.sem, s.row_max.at(turn, (g + 1) * TILES * 2))
                    maxima = s.neg_max[:, g, :, :]
                    link(nc.vector.tensor_copy(s.max_parts[:, g, :, :, 0], maxima))
                    nc.vector.tensor_tensor(s.max_parts[:, g, :, :, 1], maxima, s.max_parts[:, g, :, :, 0],
                                            ALU.subtract).then_inc(s.max_ready.sem, 1)
                for c in range(TILES):
                    dve.wait_ge(s.out_turned.sem, s.out_turned.at(turn, c + 1))
                    heads = PS[:, c, :].rearrange("p (h r) -> p h r", r=QUAD)
                    link(nc.vector.reciprocal(s.inverse[:, c, :], heads[:, :, HD8]))
                    nc.vector.tensor_tensor(s.attn[:, c, :].rearrange("p (h e) -> p h e", e=HD8), heads[:, :, 0:HD8],
                                            s.inverse[:, c, :].unsqueeze(2).to_broadcast([P, HEADS, HD8]),
                                            ALU.mult).then_inc(s.attn_ready.sem, 1)
                dve.wait_ge(s.wo_summed.sem, s.wo_summed.at(turn, 1))
                ins = nc.vector.tensor_tensor(s.y[:, :, :], PS[:, 5, :].rearrange("p (c d) -> p c d", d=D),
                                              b_o[:, :].unsqueeze(1).to_broadcast([P, TILES, D]), ALU.add)
                ins.then_inc(s.wo_read.sem, 1)
                dve.wait_ge(s.wo_read.sem, s.wo_read.at(turn, 1))
                result(nc, dve, link, s, turn, x)
                finish()
                if tag == core.first_phase:
                    dve.wait_ge(core.x_rest.sem, 16)

        @block.scalar
        def _(act):
            act.wait_ge(s.ready.sem, 2)
            with act.Fori(0, BATCH) as turn:
                act.wait_ge(s.xt_summed.sem, s.xt_summed.at(turn, 1))
                nc.scalar.activation(s.xt[:, :], PS[:, ST, :], ACT.Copy).then_inc(s.xt_ready.sem, 1)
                act.wait_ge(s.qkv_ready.sem, s.qkv_ready.at(turn, TILES))
                for a, (parts, copies) in enumerate(((s.q_parts, (0, 2 * HD8)), (s.k_parts, (0, HD8)))):
                    for first in copies:
                        nc.scalar.activation(parts[:, :, :, first:first + HD8],
                                             s.qk[:, :, a, :].rearrange("p c (h e) -> p c h e", e=HD8),
                                             ACT.Copy).then_inc(s.high_ready.sem, 1)
                for g in (1, 3):
                    act.wait_ge(s.parts_turned.sem, s.parts_turned.at(turn, g + 1))
                    nc.scalar.activation(s.qkt[:, g, :, :].rearrange("p a t -> p (a t)"), PB[:, ST + g, :],
                                         ACT.Copy).then_inc(s.qkt_by_act.sem, 1)

                def keep_maxima(g):
                    act.wait_ge(s.max_turned.sem, s.max_turned.at(turn, g + 1))
                    nc.scalar.activation(s.max_t[:, g, :], PB[0:2 * GH, TURN, 0:SEQ], ACT.Copy).then_inc(
                        s.max_t_ready.sem, 1)

                def exps(n):
                    width = sum(w for _, _, _, w in units[n % nu])
                    for j in range(GH):
                        i = GH * n + j
                        if n >= 2:
                            act.wait_ge(s.pv_done.sem, s.pv_done.at(turn, n - 1))
                        act.wait_ge(s.scores.sem, s.scores.at(turn, i + 1))
                        nc.scalar.activation(s.probs[:, n % 2 * GH + j, 0:width], PS[:, ST + i % 2, 0:width],
                                             ACT.Exp, scale=scale).then_inc(s.exp_done.sem, 1)

                def keep_products(g):
                    act.wait_ge(s.pv_done.sem, s.pv_done.at(turn, nu * (g + 1)))
                    nc.scalar.activation(s.out_t[:, g, :], PS[:, OUT, :], ACT.Copy).then_inc(s.out_t_ready.sem, 1)

                keep_maxima(0)
                for n in range(GROUPS * nu):
                    exps(n)
                    if n % nu == 0:
                        if n:
                            keep_products(n // nu - 1)
                        if n // nu + 1 < GROUPS:
                            keep_maxima(n // nu + 1)
                keep_products(GROUPS - 1)
                act.wait_ge(s.attn_turned.sem, s.attn_turned.at(turn, 1))
                nc.scalar.activation(s.attn_t[:, :], PS[:, ST, :], ACT.Copy).then_inc(s.attn_t_ready.sem, 1)

        @block.tensor
        def _(pe):
            pe.wait_ge(s.ready.sem, 2)
            pe.wait_ge(core.constants_ready.sem, core.constants_ready.per_turn)
            pe.wait_ge(weights[0].sem, weights[0].per_turn)
            with pe.Fori(0, BATCH) as turn:
                for c in range(TILES):
                    pe.wait_ge(s.xn_ready.sem, s.xn_ready.at(turn, c + 1))
                    last = nc.tensor.transpose(PS[:, ST, c * P:(c + 1) * P], s.xn[:, c, :], ident[:, :])
                last.then_inc(s.xt_summed.sem, 1)
                pe.wait_ge(s.xt_ready.sem, s.xt_ready.at(turn, 1))
                for c in range(TILES):
                    nc.tensor.matmul(PS[:, c, 0:3 * D], s.xt[:, c * P:(c + 1) * P], w_qkv[:, :], start=True,
                                     stop=True).then_inc(s.qkv_summed.sem, 1)
                pe.wait_ge(s.high_ready.sem, s.high_ready.at(turn, 4))
                pe.wait_ge(s.low_ready.sem, s.low_ready.at(turn, 2))
                for g in range(GROUPS):
                    for a, parts in enumerate((s.q_parts, s.k_parts)):
                        for c in range(TILES):
                            at = a * SEQ + c * P
                            last = nc.tensor.transpose(
                                PB[:, ST + g, at:at + P],
                                parts[:, c, GH * g:GH * (g + 1), :].rearrange("p h r -> p (h r)"), ident_b[:, :])
                    last.then_inc(s.parts_turned.sem, 1)
                pe.wait_ge(s.qkt_by_act.sem, s.qkt_by_act.at(turn, 2))
                pe.wait_ge(s.qkt_by_dve.sem, s.qkt_by_dve.at(turn, 2))
                pe.wait_ge(s.q_alone_ready.sem, s.q_alone_ready.at(turn, 16 * GH))

                def row_scores(n):
                    g, c, half = n // (2 * TILES), n // 2 % TILES, n % 2
                    if n >= 2:
                        pe.wait_ge(s.row_max.sem, s.row_max.at(turn, n - 1))
                    keys = P * (c + 1) if causal else SEQ
                    for h in range(2):
                        bank = n % 2 * 2 + h
                        last = nc.tensor.matmul(PS[:, bank, 0:keys],
                                                s.q_alone[:, GH * g + 2 * half + h, c * P:(c + 1) * P],
                                                s.qkt[:, g, 1, 0:keys], start=True, stop=not causal)
                        if causal:
                            last = nc.tensor.matmul(PS[:, bank, keys - P:keys], ident_b[:, :], core.mask[:, :],
                                                    start=False, stop=True)
                    last.then_inc(s.row_scores.sem, 1)

                def turn_maxima(g):
                    pe.wait_ge(s.max_ready.sem, s.max_ready.at(turn, g + 1))
                    for c in range(TILES):
                        last = nc.tensor.transpose(PB[0:2 * GH, TURN, c * P:(c + 1) * P],
                                                   s.max_parts[:, g, c, :, :].rearrange("p j r -> p (j r)"),
                                                   ident_b[:, :])
                    last.then_inc(s.max_turned.sem, 1)

                def products(n):
                    g, u = n // nu, n % nu
                    if causal:
                        pe.wait_ge(s.masked.sem, s.masked.at(turn, n + 1))
                    else:
                        pe.wait_ge(s.exp_done.sem, s.exp_done.at(turn, GH * (n + 1)))
                    if u == 0 and g:
                        pe.wait_ge(s.out_t_ready.sem, s.out_t_ready.at(turn, g))
                    for i, (k, q0, at, width) in enumerate(units[u]):
                        for j in range(GH):
                            last = nc.tensor.matmul(PS[QUAD * j:QUAD * j + HD8 + 1, OUT, q0:q0 + width],
                                                    s.v[:, k, GH * g + j, :],
                                                    s.probs[:, n % 2 * GH + j, at:at + width],
                                                    start=u == 0 and i == 0, stop=u == nu - 1 and i == len(units[u]) - 1)
                    last.then_inc(s.pv_done.sem, 1)

                fills = GROUPS * TILES * 2
                for n in range(2 * 2 * TILES):
                    row_scores(n)
                done = 2 * 2 * TILES
                turn_maxima(0)
                for n in range(GROUPS * nu):
                    g, u = n // nu, n % nu
                    if u == 0:
                        pe.wait_ge(s.max_placed[g].sem, s.max_placed[g].at(turn, 16 * GH))
                    for j in range(GH):
                        i = GH * n + j
                        if i >= 2:
                            pe.wait_ge(s.exp_done.sem, s.exp_done.at(turn, i - 1))
                        for k, q0, at, width in units[u]:
                            last = nc.tensor.matmul(PS[:, ST + i % 2, at:at + width],
                                                    s.qkt[:, g, 1, k * P:(k + 1) * P],
                                                    s.q_alone[:, GH * g + j, q0:q0 + width], start=True, stop=True)
                        last.then_inc(s.scores.sem, 1)
                        due = 2 * 2 * TILES + (i + 1) * 2 * TILES // (GH * nu)
                        while done < min(due, fills):
                            row_scores(done)
                            done += 1
                    if n:
                        products(n - 1)
                    if u == 0 and g + 1 < GROUPS:
                        turn_maxima(g + 1)
                products(GROUPS * nu - 1)
                pe.wait_ge(s.out_t_ready.sem, s.out_t_ready.at(turn, GROUPS))
                for c in range(TILES):
                    for g in range(GROUPS):
                        last = nc.tensor.transpose(PS[:, c, g * P:(g + 1) * P], s.out_t[:, g, c * P:(c + 1) * P],
                                                   ident[:, :])
                    last.then_inc(s.out_turned.sem, 1)
                for c in range(TILES):
                    pe.wait_ge(s.attn_ready.sem, s.attn_ready.at(turn, c + 1))
                    last = nc.tensor.transpose(PS[:, ST, c * P:(c + 1) * P], s.attn[:, c, :], ident[:, :])
                last.then_inc(s.attn_turned.sem, 1)
                pe.wait_ge(s.attn_t_ready.sem, s.attn_t_ready.at(turn, 1))
                for c in range(TILES):
                    last = nc.tensor.matmul(PS[:, 5, c * P:(c + 1) * P], s.attn_t[:, c * P:(c + 1) * P], w_o[:, :],
                                            start=True, stop=True)
                last.then_inc(s.wo_summed.sem, 1)
                pe.wait_ge(s.wo_read.sem, s.wo_read.at(turn, 1))


def scale_shift(nc, link, target, source, gain, offset):
    rows = [P, TILES, D]
    link(nc.vector.tensor_tensor(target[:, :, :], source[:, :, :], gain[:, :].unsqueeze(1).to_broadcast(rows), ALU.mult))
    link(nc.vector.tensor_tensor(target[:, :, :], target[:, :, :], offset[:, :].unsqueeze(1).to_broadcast(rows), ALU.add))


def add_normalised(nc, dve, link, s, turn, x):
    link(normalise(nc, dve, link, s, turn, 1, lambda c: s.y[:, c, :], lambda c: s.y_norm[:, c, :], 1e-5))
    for c in range(TILES):
        last = nc.vector.tensor_tensor(x(c), x(c), s.y_norm[:, c, :], ALU.add)
    link(last)


def keep_norm1(core):
    def result(nc, dve, link, s, turn, x):
        link(nc.vector.tensor_tensor(s.y[:, :, :], s.y[:, :, :], s.xn[:, :, :], ALU.add))
        link(normalise(nc, dve, link, s, turn, 1, lambda c: s.y[:, c, :], lambda c: s.y_norm[:, c, :], 1e-5))
        rows = [P, TILES, D]
        gain, offset = core.ln1_g[:, :].unsqueeze(1), core.ln1_b[:, :].unsqueeze(1)
        link(nc.vector.tensor_tensor(s.y[:, :, :], s.y_norm[:, :, :], gain.to_broadcast(rows), ALU.mult))
        link(nc.vector.tensor_tensor(core.X1[:, bass.ds(turn * TILES, TILES), :], s.y[:, :, :],
                                     offset.to_broadcast(rows), ALU.add))
    return result


class Norms:

    def __init__(self, core, name, tag, links, norms, ctx):
        sb = lambda n, shape, dtype=F32: core.sbuf(f"{name}_{n}", shape, dtype, ctx)
        self.stats = sb("stats", [P, TILES, 6])
        self.mean_var = sb("mean_var", [P, TILES, 2])
        self.carrier = sb("carrier", [P, 1])
        self.var_eps = sb("var_eps", [P, TILES])
        self.rstd = sb("rstd", [P, TILES])
        self.minus_half = core.minus_half
        self.constants = core.constants_ready
        sig = lambda n, per=1: core.semaphore(f"{tag}_{n}", per)
        self.ready = sig("ready")
        self.link = sig("link", links)
        self.var_ready = sig("var_ready", norms)
        self.rstd_ready = sig("rstd_ready", norms)


def gelu_ffn(core, name, tag):
    nc, X, PS, ident = core.nc, core.X, core.PS, core.ident
    DOWN = 0
    with ExitStack() as ctx:
        sb = lambda n, shape, dtype=F32: core.sbuf(f"{name}_{n}", shape, dtype, ctx)
        s = Norms(core, name, tag, 2 + 2 + 3 + 1, 3, ctx)
        sig = lambda n, per=1: core.semaphore(f"{tag}_{n}", per)
        row_sums = sb("row_sums", [P, 2])
        threshold = sb("threshold", [P, 2, 2])
        above, below = sb("above", [P, 2, FF]), sb("below", [P, 2, FF])
        w_up, w_down = sb("w_up", [P, FF]), sb("w_down", [P, FC, D])
        xn, xt = sb("xn", [P, TILES, D]), sb("xt", [P, SEQ])
        hidden, hidden_n = sb("hidden", [P, TILES, FF]), sb("hidden_n", [P, TILES, FF])
        hidden_t = sb("hidden_t", [P, FC, SEQ])
        y, y_norm = sb("y", [P, TILES, D]), sb("y_norm", [P, TILES, D])
        setup = sig("setup", 5)
        sums_spread, turned_w, weights_ready = sig("sums_spread"), sig("turned_w"), sig("weights_ready", 2)
        xn_ready, xt_summed, xt_ready = sig("xn_ready", TILES), sig("xt_summed"), sig("xt_ready")
        up_summed, gelu_done, hidden_ready = sig("up_summed", TILES), sig("gelu_done", TILES), sig("hidden_ready", TILES)
        hidden_turned, hidden_t_ready = sig("hidden_turned", FC), sig("hidden_t_ready", FC)
        down_summed, y_read = sig("down_summed"), sig("y_read")
        block = ctx.enter_context(nc.Block())

        @block.gpsimd
        def _(pool):
            with pool.Fori(0, BATCH) as turn:
                inverse_roots(nc, pool, s, turn, [0, 1, 2])

        @block.vector
        def _(dve):
            dve.wait_ge(core.weights_b.sem, core.weights_b.per_turn)
            raw = (core.w_fc[:, :, :], core.w_proj[:, :, :])
            for i, weight in enumerate(raw):
                nc.vector.tensor_reduce(row_sums[:, i:i + 1], weight, AX.XY, ALU.add,
                                        apply_absolute_value=True).then_inc(setup.sem, 1)
            dve.wait_ge(sums_spread.sem, 1)
            for i, sign in enumerate((0.5, -0.5)):
                nc.vector.tensor_scalar(threshold[:, :, i], PS[:, 0, 0:2], sign / (D * FF), sign * 1e-6, ALU.mult,
                                        ALU.add).then_inc(setup.sem, 1)
            dve.wait_ge(setup.sem, 4)
            for i, weight in enumerate(raw):
                flat = weight.rearrange("p a d -> p (a d)")
                nc.vector.tensor_scalar(above[:, i, :], flat, threshold[:, i, 0:1], None, ALU.is_gt)
                last = nc.vector.tensor_scalar(below[:, i, :], flat, threshold[:, i, 1:2], None, ALU.is_lt)
            last.then_inc(setup.sem, 1)
            dve.wait_ge(setup.sem, 5)
            nc.vector.tensor_tensor(above[:, :, :], above[:, :, :], below[:, :, :], ALU.subtract).then_inc(
                weights_ready.sem, 1)
            with dve.Fori(0, BATCH) as turn:
                link, finish = make_link(dve, s.link, turn)
                x = lambda c: X[:, turn * TILES + c, :]
                if tag == core.first_phase:
                    dve.wait_ge(core.x_first.sem, 16)
                    dve.wait_ge(core.x_rest.sem, 16)
                normalise(nc, dve, link, s, turn, 0, x, lambda c: xn[:, c, :], 1e-5, xn_ready)
                dve.wait_ge(xt_summed.sem, xt_summed.at(turn, 1))
                nc.vector.tensor_copy(xt[:, :], PS[:, 0, :]).then_inc(xt_ready.sem, 1)
                dve.wait_ge(gelu_done.sem, gelu_done.at(turn, TILES))
                norm_statistics(nc, link, s, lambda c: hidden[:, c, :], TILES, FF)
                nc.vector.tensor_scalar(s.var_eps[:, :], s.mean_var[:, :, 1], 1e-5, None, ALU.add).then_inc(
                    s.var_ready.sem, 1)
                dve.wait_ge(s.rstd_ready.sem, s.rstd_ready.at(turn, 2))
                for c in range(TILES):
                    nc.vector.tensor_scalar(hidden_n[:, c, :], hidden[:, c, :], s.mean_var[:, c, 0:1],
                                            s.rstd[:, c:c + 1], ALU.subtract, ALU.mult).then_inc(hidden_ready.sem, 1)
                for f in range(FC):
                    dve.wait_ge(hidden_turned.sem, hidden_turned.at(turn, f + 1))
                    nc.vector.tensor_scalar(hidden_t[:, f, :], PS[:, 4 + f, :], core.ln_w[:, f:f + 1],
                                            core.ln_b[:, f:f + 1], ALU.mult, ALU.add).then_inc(hidden_t_ready.sem, 1)
                dve.wait_ge(down_summed.sem, down_summed.at(turn, 1))
                nc.vector.tensor_copy(y[:, :, :].rearrange("p c d -> p (c d)"), PS[:, DOWN, :]).then_inc(y_read.sem, 1)
                dve.wait_ge(y_read.sem, y_read.at(turn, 1))
                link(normalise(nc, dve, link, s, turn, 2, lambda c: y[:, c, :], lambda c: y_norm[:, c, :], 1e-5))
                for c in range(TILES):
                    last = nc.vector.tensor_tensor(x(c), x(c), y_norm[:, c, :], ALU.add)
                link(last)
                finish()

        @block.scalar
        def _(act):
            act.wait_ge(turned_w.sem, 1)
            nc.scalar.activation(w_up[:, :], PS[:, 1, :], ACT.Copy)
            nc.scalar.activation(w_down[:, :, :].rearrange("p a d -> p (a d)"), PS[:, 2, :], ACT.Copy).then_inc(
                weights_ready.sem, 1)
            with act.Fori(0, BATCH) as turn:
                for c in range(TILES):
                    act.wait_ge(up_summed.sem, up_summed.at(turn, c + 1))
                    nc.scalar.activation(hidden[:, c, :], PS[:, c, :], ACT.Gelu).then_inc(gelu_done.sem, 1)

        @block.tensor
        def _(pe):
            pe.wait_ge(core.constants_ready.sem, core.constants_ready.per_turn)
            pe.wait_ge(setup.sem, 2)
            nc.tensor.matmul(PS[:, 0, 0:2], core.ones[:, :], row_sums[:, :], start=True, stop=True).then_inc(
                sums_spread.sem, 1)
            pe.wait_ge(weights_ready.sem, 1)
            for i in range(2):
                for a in range(FC):
                    last = nc.tensor.transpose(PS[:, 1 + i, a * P:(a + 1) * P], above[:, i, a * P:(a + 1) * P],
                                               ident[:, :])
            last.then_inc(turned_w.sem, 1)
            pe.wait_ge(weights_ready.sem, 2)
            with pe.Fori(0, BATCH) as turn:
                for c in range(TILES):
                    pe.wait_ge(xn_ready.sem, xn_ready.at(turn, c + 1))
                    last = nc.tensor.transpose(PS[:, 0, c * P:(c + 1) * P], xn[:, c, :], ident[:, :])
                last.then_inc(xt_summed.sem, 1)
                pe.wait_ge(xt_ready.sem, xt_ready.at(turn, 1))
                for c in range(TILES):
                    nc.tensor.matmul(PS[:, c, :], xt[:, c * P:(c + 1) * P], w_up[:, :], start=True,
                                     stop=True).then_inc(up_summed.sem, 1)
                pe.wait_ge(hidden_ready.sem, hidden_ready.at(turn, TILES))
                for f in range(FC):
                    for c in range(TILES):
                        last = nc.tensor.transpose(PS[:, 4 + f, c * P:(c + 1) * P], hidden_n[:, c, f * P:(f + 1) * P],
                                                   ident[:, :])
                    last.then_inc(hidden_turned.sem, 1)
                pe.wait_ge(hidden_t_ready.sem, hidden_t_ready.at(turn, FC))
                for c in range(TILES):
                    for f in range(FC):
                        last = nc.tensor.matmul(PS[:, DOWN, c * P:(c + 1) * P], hidden_t[:, f, c * P:(c + 1) * P],
                                                w_down[:, f, :], start=f == 0, stop=f == FC - 1)
                last.then_inc(down_summed.sem, 1)
                pe.wait_ge(y_read.sem, y_read.at(turn, 1))


def expert_ffn(core, name, tag, stored, out):
    nc, X, X1, PS, ident = core.nc, core.X, core.X1, core.PS, core.ident
    with ExitStack() as ctx:
        sb = lambda n, shape, dtype=F32: core.sbuf(f"{name}_{n}", shape, dtype, ctx)
        s = Norms(core, name, tag, 29, 2, ctx)
        sig = lambda n, per=1: core.semaphore(f"{tag}_{n}", per)
        now, xt = sb("now", [P, TILES, D]), sb("xt", [P, SEQ])
        key_terms, keys = sb("key_terms", [P, TILES, D]), sb("keys", [P, TILES])
        whole, rounded = sb("whole", [P, TILES], mybir.dt.int32), sb("rounded", [P, TILES])
        over, floor, chosen = sb("over", [P, TILES]), sb("floor", [P, TILES]), sb("chosen", [P, TILES])
        gate = sb("gate", [P, EXPERTS, TILES])
        hidden = sb("hidden", [P, 4, SEQ])
        experts = sb("experts", [P, TILES, EXPERTS, D])
        total = sb("total", [P, TILES, D])
        normed, scaled = sb("normed", [P, TILES, D]), sb("scaled", [P, TILES, D])
        y_norm = sb("y_norm", [P, TILES, D])
        xt_summed, xt_ready = sig("xt_summed"), sig("xt_ready")
        up_summed, hidden_used = sig("up_summed", EXPERTS * FC), sig("hidden_used", EXPERTS * FC)
        hidden_by = sig("hidden_by_act", EXPERTS * FC // 2), sig("hidden_by_dve", EXPERTS * FC // 2)
        down_read = sig("down_read")
        block = ctx.enter_context(nc.Block())

        @block.sync
        def _(sp):
            with sp.Fori(0, BATCH) as turn:
                sp.wait_ge(s.link.sem, s.link.at(turn, s.link.per_turn))
                sp.dma_start(out[bass.ds(turn, 1)].rearrange("b (c p) d -> p (b c) d", p=P),
                             X[:, bass.ds(turn * TILES, TILES), :]).then_inc(stored.sem, 16)
            sp.wait_ge(stored.sem, 16 * BATCH)

        @block.gpsimd
        def _(pool):
            with pool.Fori(0, BATCH) as turn:
                inverse_roots(nc, pool, s, turn, [0, 1])

        @block.vector
        def _(dve):
            dve.wait_ge(core.weights_e.sem, core.weights_e.per_turn)
            with dve.Fori(0, BATCH) as turn:
                link, finish = make_link(dve, s.link, turn)
                x = lambda c: X[:, turn * TILES + c, :]
                link(nc.vector.tensor_copy(now[:, :, :], X1[:, bass.ds(turn * TILES, TILES), :]))
                x1 = lambda c: now[:, c, :]
                for c in range(TILES):
                    last = nc.vector.tensor_tensor(key_terms[:, c, :], x1(c), core.router_w[:, :], ALU.mult)
                link(last)
                link(nc.vector.tensor_reduce(keys[:, :], key_terms[:, :, :], AX.X, ALU.add))
                link(nc.vector.tensor_scalar(keys[:, :], keys[:, :], core.router_b[:, 0:1], None, ALU.add))

                def take_floor(value):
                    link(nc.vector.tensor_copy(whole[:, :], value))
                    link(nc.vector.tensor_copy(rounded[:, :], whole[:, :]))
                    link(nc.vector.tensor_tensor(over[:, :], rounded[:, :], value, ALU.is_gt))

                take_floor(keys[:, :])
                link(nc.vector.tensor_tensor(floor[:, :], rounded[:, :], over[:, :], ALU.subtract))
                link(nc.vector.tensor_scalar(keys[:, :], floor[:, :], 1.0 / EXPERTS, None, ALU.mult))
                take_floor(keys[:, :])
                link(nc.vector.tensor_tensor(chosen[:, :], rounded[:, :], over[:, :], ALU.subtract))
                link(nc.vector.tensor_scalar(chosen[:, :], chosen[:, :], float(EXPERTS), None, ALU.mult))
                link(nc.vector.tensor_tensor(chosen[:, :], floor[:, :], chosen[:, :], ALU.subtract))
                for e in range(EXPERTS):
                    last = nc.vector.tensor_scalar(gate[:, e, :], chosen[:, :], float(e), None, ALU.is_equal)
                link(last)
                for n in range(1, EXPERTS * FC, 2):
                    dve.wait_ge(up_summed.sem, up_summed.at(turn, n + 1))
                    nc.vector.tensor_scalar(hidden[:, n % 4, :], PS[:, n % 4, :], core.b1[:, n:n + 1], 0.0, ALU.add,
                                            ALU.max).then_inc(hidden_by[1].sem, 1)
                dve.wait_ge(hidden_used.sem, hidden_used.at(turn, EXPERTS * FC))
                for c in range(TILES):
                    last = nc.vector.tensor_tensor(experts[:, c, :, :].rearrange("p e d -> p (e d)"), PS[:, 4 + c, :],
                                                   core.b2[:, :], ALU.add)
                last.then_inc(down_read.sem, 1)
                dve.wait_ge(down_read.sem, down_read.at(turn, 1))
                for e in range(EXPERTS):
                    for c in range(TILES):
                        last = nc.vector.scalar_tensor_tensor(
                            out=total[:, c, :], in0=experts[:, c, e, :], scalar=gate[:, e, c:c + 1],
                            in1=x1(c) if e == 0 else total[:, c, :], op0=ALU.mult, op1=ALU.add)
                    link(last)
                link(normalise(nc, dve, link, s, turn, 0, lambda c: total[:, c, :], lambda c: normed[:, c, :], 1e-5))
                scale_shift(nc, link, scaled, normed, core.ln2_g, core.ln2_b)
                link(normalise(nc, dve, link, s, turn, 1, lambda c: scaled[:, c, :], lambda c: y_norm[:, c, :], 1e-5))
                for c in range(TILES):
                    last = nc.vector.tensor_tensor(x(c), x(c), y_norm[:, c, :], ALU.add)
                link(last)
                finish()

        @block.scalar
        def _(act):
            act.wait_ge(core.weights_e.sem, core.weights_e.per_turn)
            with act.Fori(0, BATCH) as turn:
                act.wait_ge(xt_summed.sem, xt_summed.at(turn, 1))
                nc.scalar.activation(xt[:, :], PS[:, 0, :], ACT.Copy).then_inc(xt_ready.sem, 1)
                for n in range(0, EXPERTS * FC, 2):
                    act.wait_ge(up_summed.sem, up_summed.at(turn, n + 1))
                    nc.scalar.activation(hidden[:, n % 4, :], PS[:, n % 4, :], ACT.Relu,
                                         bias=core.b1[:, n:n + 1]).then_inc(hidden_by[0].sem, 1)

        @block.tensor
        def _(pe):
            pe.wait_ge(core.weights_e.sem, core.weights_e.per_turn)
            with pe.Fori(0, BATCH) as turn:
                pe.wait_ge(s.link.sem, s.link.at(turn, 1))
                for c in range(TILES):
                    last = nc.tensor.transpose(PS[:, 0, c * P:(c + 1) * P], now[:, c, :], ident[:, :])
                last.then_inc(xt_summed.sem, 1)
                pe.wait_ge(xt_ready.sem, xt_ready.at(turn, 1))

                def up(n):
                    nc.tensor.matmul(PS[:, n % 4, :], core.w1[:, n // FC, n % FC * P:(n % FC + 1) * P], xt[:, :],
                                     start=True, stop=True).then_inc(up_summed.sem, 1)

                def down(n):
                    e, f = n // FC, n % FC
                    ready = hidden_by[n % 2]
                    pe.wait_ge(ready.sem, ready.at(turn, n // 2 + 1))
                    for c in range(TILES):
                        last = nc.tensor.matmul(PS[:, 4 + c, e * D:(e + 1) * D], hidden[:, n % 4, c * P:(c + 1) * P],
                                                core.w2[:, e, f, :], start=f == 0, stop=f == FC - 1)
                    last.then_inc(hidden_used.sem, 1)

                up(0)
                up(1)
                for n in range(EXPERTS * FC):
                    if n + 2 < EXPERTS * FC:
                        up(n + 2)
                    down(n)
                pe.wait_ge(down_read.sem, down_read.at(turn, 1))


def wide_attention(core, name, tag):
    nc, X, PS, ident, ident_b = core.nc, core.X, core.PS, core.ident, core.ident_b
    PB = PS.bitcast(BF16)
    w_q, w_k, w_v = core.wide_w
    scale = float(HD64) ** -0.5
    ROWS, TURN, ST, OUT, SUMS = 3, 3, 4, 6, 7
    units = [[(0, 0, 0, 512)], [(1, 128, 0, 384), (3, 384, 384, 128)], [(2, 256, 0, 256)]]
    nu = len(units)
    GRAIN = 2
    KEPT = 2 * GRAIN
    low, high = slice(0, HD64), slice(HD64, P)

    with ExitStack() as ctx:
        sb = lambda n, shape, dtype=F32: core.sbuf(f"{name}_{n}", shape, dtype, ctx)
        s = Norms(core, name, tag, 2 + 2 * PAIRS + 3 + 2 + 3 + 1, 3, ctx)
        sig = lambda n, per=1: core.semaphore(f"{tag}_{n}", per)
        xn, xt = sb("xn", [P, TILES, D]), sb("xt", [P, SEQ])
        v = sb("v", [P, TILES, HEADS, HD64])
        part_high, part_low = sb("part_high", [P, 2, KEPT, SEQ], BF16), sb("part_low", [P, 2, KEPT, SEQ], BF16)
        q1, k1 = sb("q1", [P, HEADS, SEQ], BF16), sb("k1", [P, HEADS, SEQ], BF16)
        q2, k2 = sb("q2", [P, HEADS, SEQ], BF16), sb("k2", [P, HEADS, SEQ], BF16)
        neg_max = sb("neg_max", [P, PAIRS, TILES, 2])
        max_parts = sb("max_parts", [P, PAIRS, TILES, 2, 2], BF16)
        max_t = sb("max_t", [4, PAIRS, SEQ], BF16)
        probs = sb("probs", [P, 4, SEQ])
        inverse = sb("inverse", [P, SEQ])
        out_t = core.X1[:, :, :].rearrange("p (a c) d -> p a (c d)", a=PAIRS)
        pool_carrier = sb("pool_carrier", [P, 1])
        y, y_norm = sb("y", [P, TILES, D]), sb("y_norm", [P, TILES, D])
        cleared = sig("cleared")
        xn_ready, xt_summed, xt_ready = sig("xn_ready", TILES), sig("xt_summed"), sig("xt_ready")
        v_summed, v_ready = sig("v_summed", 2 * TILES), sig("v_ready", 2 * TILES)
        qk_summed, high_ready, low_ready = (sig(n, 2 * PAIRS) for n in ("qk_summed", "high_ready", "low_ready"))
        placed = [sig(f"placed{i}", 12 * 16) for i in range(PAIRS // GRAIN)]
        row_scores_ready, row_max = sig("row_scores", PAIRS * TILES * 2), sig("row_max", PAIRS * TILES * 2)
        max_ready, max_turned, max_t_ready = (sig(n, PAIRS) for n in ("max_ready", "max_turned", "max_t_ready"))
        max_placed = [sig(f"max_placed{p}", 32) for p in range(PAIRS)]
        scores, exp_done = sig("scores", PAIRS * nu * 2), sig("exp_done", PAIRS * nu * 2)
        masked, pv_done = sig("masked", PAIRS * nu), sig("pv_done", PAIRS * nu)
        out_t_ready, wo_summed, y_read = sig("out_t_ready", PAIRS), sig("wo_summed"), sig("y_read")
        block = ctx.enter_context(nc.Block())

        @block.sync
        def _(sp):
            even = lambda t, i: t[:, :, :].rearrange("p (a b) t -> p a b t", b=2)[:, i * GRAIN:(i + 1) * GRAIN, 0, :]
            odd = lambda t, i: t[:, :, :].rearrange("p (a b) t -> p a b t", b=2)[:, i * GRAIN:(i + 1) * GRAIN, 1, :]
            with sp.Fori(0, BATCH) as turn:
                for i in range(PAIRS // GRAIN):
                    sp.wait_ge(high_ready.sem, high_ready.at(turn, 2 * GRAIN * (i + 1)))
                    sp.wait_ge(low_ready.sem, low_ready.at(turn, 2 * GRAIN * (i + 1)))
                    of = slice(i % 2 * GRAIN, (i % 2 + 1) * GRAIN)
                    qh, ql = part_high[:, 0, of, :], part_low[:, 0, of, :]
                    kh, kl = part_high[:, 1, of, :], part_low[:, 1, of, :]
                    for target, rows, source, source_rows in (
                            (even(q1, i), low, qh, low), (even(q1, i), high, ql, low),
                            (odd(q1, i), low, ql, high), (odd(q1, i), high, qh, high),
                            (even(k1, i), low, kh, low), (even(k1, i), high, kh, low),
                            (odd(k1, i), low, kh, high), (odd(k1, i), high, kh, high),
                            (even(q2, i), low, qh, low), (odd(q2, i), high, qh, high),
                            (even(k2, i), low, kl, low), (odd(k2, i), high, kl, high)):
                        sp.dma_start(target[rows], source[source_rows]).then_inc(placed[i].sem, 16)
                for p in range(PAIRS):
                    sp.wait_ge(max_t_ready.sem, max_t_ready.at(turn, p + 1))
                    sp.dma_start(q2[HD64:HD64 + 2, 2 * p, :], max_t[0:2, p, :]).then_inc(max_placed[p].sem, 16)
                    sp.dma_start(q2[0:2, 2 * p + 1, :], max_t[2:4, p, :]).then_inc(max_placed[p].sem, 16)

        @block.gpsimd
        def _(pool):
            nc.gpsimd.memset(q2[:, :, :], 0.0)
            nc.gpsimd.memset(k2[:, :, :], 0.0).then_inc(cleared.sem, 1)
            pool.wait_ge(cleared.sem, 1)
            heads = k2[:, :, :].rearrange("p (a b) t -> p a b t", b=2)
            nc.gpsimd.memset(heads[HD64:HD64 + 2, :, 0, :], 1.0).then_inc(cleared.sem, 1)
            pool.wait_ge(cleared.sem, 2)
            nc.gpsimd.memset(heads[0:2, :, 1, :], 1.0).then_inc(s.ready.sem, 1)
            pool.wait_ge(s.ready.sem, 1)
            with pool.Fori(0, BATCH) as turn:
                inverse_roots(nc, pool, s, turn, [0])
                for n in range(PAIRS * nu):
                    pool.wait_ge(exp_done.sem, exp_done.at(turn, 2 * (n + 1)))
                    if n:
                        pool.wait_ge(masked.sem, masked.at(turn, n))
                    nc.gpsimd.tensor_tensor(pool_carrier[:, :], s.minus_half[:, 0:1], s.minus_half[:, 0:1], ALU.add)
                    slot = n % 2 * 2
                    for _, _, at, _ in units[n % nu]:
                        square = probs[:, slot:slot + 2, at:at + P]
                        last = nc.gpsimd.affine_select(out=square, in_=square, compare_op=ALU.is_ge, fill=0.0,
                                                       base=0, pattern=[[0, 2], [1, P]], channel_multiplier=-1)
                    last.then_inc(masked.sem, 1)
                inverse_roots(nc, pool, s, turn, [1, 2])

        @block.vector
        def _(dve):
            dve.wait_ge(core.weights_c.sem, core.weights_c.per_turn)
            with dve.Fori(0, BATCH) as turn:
                link, finish = make_link(dve, s.link, turn)
                x = lambda c: X[:, turn * TILES + c, :]
                if tag == core.first_phase:
                    dve.wait_ge(core.x_first.sem, 16)
                    dve.wait_ge(core.x_rest.sem, 16)
                normalise(nc, dve, link, s, turn, 0, x, lambda c: xn[:, c, :], 1e-5, xn_ready)
                for n in range(2 * PAIRS):
                    dve.wait_ge(high_ready.sem, high_ready.at(turn, n + 1))
                    nc.vector.tensor_tensor(part_low[:, n % 2, n // 2 % KEPT, :], PS[:, 4 + n % 4, :],
                                            part_high[:, n % 2, n // 2 % KEPT, :], ALU.subtract).then_inc(low_ready.sem, 1)

                def keep_products(p):
                    dve.wait_ge(pv_done.sem, pv_done.at(turn, nu * (p + 1)))
                    link(nc.vector.reciprocal(inverse[:, :], PS[:, SUMS, :]))
                    nc.vector.tensor_tensor(out_t[:, p, :], PS[:, OUT, :], inverse[:, :], ALU.mult).then_inc(
                        out_t_ready.sem, 1)

                for p in range(PAIRS):
                    for c in range(TILES):
                        for a in range(2):
                            n = (p * TILES + c) * 2 + a
                            if p >= 3 and n % (2 * TILES) == 3:
                                keep_products(p - 3)
                            dve.wait_ge(row_scores_ready.sem, row_scores_ready.at(turn, n + 1))
                            nc.vector.tensor_reduce(neg_max[:, p, c, a:a + 1], PS[:, n % ROWS, 0:P * (c + 1)], AX.X,
                                                    ALU.max, negate=True).then_inc(row_max.sem, 1)
                    dve.wait_ge(row_max.sem, row_max.at(turn, (p + 1) * TILES * 2))
                    link(nc.vector.tensor_copy(max_parts[:, p, :, :, 0], neg_max[:, p, :, :]))
                    nc.vector.tensor_tensor(max_parts[:, p, :, :, 1], neg_max[:, p, :, :], max_parts[:, p, :, :, 0],
                                            ALU.subtract).then_inc(max_ready.sem, 1)
                for p in range(PAIRS - 3, PAIRS):
                    keep_products(p)
                dve.wait_ge(wo_summed.sem, wo_summed.at(turn, 1))
                nc.vector.tensor_tensor(y[:, :, :], PS[:, ST, :].rearrange("p (c d) -> p c d", d=D), xn[:, :, :],
                                        ALU.add).then_inc(y_read.sem, 1)
                dve.wait_ge(y_read.sem, y_read.at(turn, 1))
                link(normalise(nc, dve, link, s, turn, 1, lambda c: y[:, c, :], lambda c: y_norm[:, c, :], 1e-3))
                scale_shift(nc, link, y, y_norm, core.wide_gamma, core.wide_beta)
                link(normalise(nc, dve, link, s, turn, 2, lambda c: y[:, c, :], lambda c: y_norm[:, c, :], 1e-5))
                for c in range(TILES):
                    last = nc.vector.tensor_tensor(x(c), x(c), y_norm[:, c, :], ALU.add)
                link(last)
                finish()

        @block.scalar
        def _(act):
            act.wait_ge(s.ready.sem, 1)
            with act.Fori(0, BATCH) as turn:
                act.wait_ge(xt_summed.sem, xt_summed.at(turn, 1))
                nc.scalar.activation(xt[:, :], PS[:, 4, :], ACT.Copy).then_inc(xt_ready.sem, 1)
                for n in range(2 * PAIRS):
                    if n >= 2 * KEPT and n % (2 * GRAIN) == 0:
                        i = n // (2 * GRAIN) - 2
                        act.wait_ge(placed[i].sem, placed[i].at(turn, 12 * 16))
                    act.wait_ge(qk_summed.sem, qk_summed.at(turn, n + 1))
                    nc.scalar.activation(part_high[:, n % 2, n // 2 % KEPT, :], PS[:, 4 + n % 4, :], ACT.Copy).then_inc(
                        high_ready.sem, 1)
                    if n % 2:
                        m = n // 2
                        act.wait_ge(v_summed.sem, v_summed.at(turn, m + 1))
                        nc.scalar.activation(v[:, m // 2, :, :].rearrange("p h e -> p (h e)")[:, m % 2 * 512:][:, 0:512],
                                             PS[:, m % 4, :], ACT.Copy).then_inc(v_ready.sem, 1)

                def keep_maxima(p):
                    act.wait_ge(max_turned.sem, max_turned.at(turn, p + 1))
                    nc.scalar.activation(max_t[:, p, :], PB[0:4, TURN, 0:SEQ], ACT.Copy).then_inc(max_t_ready.sem, 1)

                keep_maxima(0)
                for n in range(PAIRS * nu):
                    width = sum(w for _, _, _, w in units[n % nu])
                    for a in range(2):
                        i = 2 * n + a
                        if n >= 2:
                            act.wait_ge(pv_done.sem, pv_done.at(turn, n - 1))
                        act.wait_ge(scores.sem, scores.at(turn, i + 1))
                        nc.scalar.activation(probs[:, n % 2 * 2 + a, 0:width], PS[:, ST + i % 2, 0:width], ACT.Exp,
                                             scale=scale).then_inc(exp_done.sem, 1)
                    if n % nu == 0 and n // nu + 1 < PAIRS:
                        keep_maxima(n // nu + 1)

        @block.tensor
        def _(pe):
            pe.wait_ge(s.ready.sem, 1)
            pe.wait_ge(core.constants_ready.sem, core.constants_ready.per_turn)
            pe.wait_ge(core.weights_c.sem, core.weights_c.per_turn)
            with pe.Fori(0, BATCH) as turn:
                for c in range(TILES):
                    pe.wait_ge(xn_ready.sem, xn_ready.at(turn, c + 1))
                    last = nc.tensor.transpose(PS[:, 4, c * P:(c + 1) * P], xn[:, c, :], ident[:, :])
                last.then_inc(xt_summed.sem, 1)
                pe.wait_ge(xt_ready.sem, xt_ready.at(turn, 1))
                for n in range(2 * PAIRS):
                    if n >= 4:
                        pe.wait_ge(low_ready.sem, low_ready.at(turn, n - 3))
                    weight = (w_q, w_k)[n % 2][:, n // 2 * 2:n // 2 * 2 + 2, :].rearrange("p h e -> p (h e)")
                    nc.tensor.matmul(PS[:, 4 + n % 4, :], weight, xt[:, :], start=True, stop=True).then_inc(
                        qk_summed.sem, 1)
                    if n % 2:
                        m = n // 2
                        if m >= 4:
                            pe.wait_ge(v_ready.sem, v_ready.at(turn, m - 3))
                        columns = w_v[:, :, :].rearrange("p h e -> p (h e)")[:, m % 2 * 512:][:, 0:512]
                        nc.tensor.matmul(PS[:, m % 4, :], xt[:, m // 2 * P:(m // 2 + 1) * P], columns, start=True,
                                         stop=True).then_inc(v_summed.sem, 1)
                pe.wait_ge(v_ready.sem, v_ready.at(turn, 2 * TILES))
                pe.wait_ge(low_ready.sem, low_ready.at(turn, 2 * PAIRS))

                def row_scores(n):
                    p, c, a = n // (2 * TILES), n // 2 % TILES, n % 2
                    if n % (2 * TILES * GRAIN) == 0:
                        i = p // GRAIN
                        pe.wait_ge(placed[i].sem, placed[i].at(turn, 12 * 16))
                    if n >= ROWS:
                        pe.wait_ge(row_max.sem, row_max.at(turn, n - ROWS + 1))
                    keys, head = P * (c + 1), 2 * p + a
                    nc.tensor.matmul(PS[:, n % ROWS, 0:keys], q1[:, head, c * P:(c + 1) * P], k1[:, head, 0:keys],
                                     start=True, stop=False)
                    nc.tensor.matmul(PS[:, n % ROWS, keys - P:keys], ident_b[:, :], core.mask[:, :], start=False,
                                     stop=True).then_inc(row_scores_ready.sem, 1)

                def turn_maxima(p):
                    pe.wait_ge(max_ready.sem, max_ready.at(turn, p + 1))
                    for c in range(TILES):
                        last = nc.tensor.transpose(PB[0:4, TURN, c * P:(c + 1) * P],
                                                   max_parts[:, p, c, :, :].rearrange("p a r -> p (a r)"), ident_b[:, :])
                    last.then_inc(max_turned.sem, 1)

                def products(n):
                    p, u = n // nu, n % nu
                    pe.wait_ge(masked.sem, masked.at(turn, n + 1))
                    if u == 0 and p:
                        pe.wait_ge(out_t_ready.sem, out_t_ready.at(turn, p))
                    for i, (k, q0, at, width) in enumerate(units[u]):
                        first, final = u == 0 and i == 0, u == nu - 1 and i == len(units[u]) - 1
                        for bank in (OUT, SUMS):
                            for a in range(2):
                                lhs = v[:, k, 2 * p + a, :] if bank == OUT else core.ones[:, 0:HD64]
                                last = nc.tensor.matmul(PS[HD64 * a:HD64 * (a + 1), bank, q0:q0 + width], lhs,
                                                        probs[:, n % 2 * 2 + a, at:at + width], start=first, stop=final)
                    last.then_inc(pv_done.sem, 1)

                fills, done = PAIRS * TILES * 2, 0
                while done < 2 * 2 * TILES:
                    row_scores(done)
                    done += 1
                turn_maxima(0)
                for n in range(PAIRS * nu):
                    p, u = n // nu, n % nu
                    if u == 0:
                        pe.wait_ge(max_placed[p].sem, max_placed[p].at(turn, 32))
                    for a in range(2):
                        i, head = 2 * n + a, 2 * p + a
                        if i >= 2:
                            pe.wait_ge(exp_done.sem, exp_done.at(turn, i - 1))
                        for k, q0, at, width in units[u]:
                            bank = PS[:, ST + i % 2, at:at + width]
                            keys, queries = slice(k * P, (k + 1) * P), slice(q0, q0 + width)
                            nc.tensor.matmul(bank, k1[:, head, keys], q1[:, head, queries], start=True, stop=False)
                            last = nc.tensor.matmul(bank, k2[:, head, keys], q2[:, head, queries], start=False,
                                                    stop=True)
                        last.then_inc(scores.sem, 1)
                        due = 2 * 2 * TILES + (i + 1) * 2 * TILES // (2 * nu)
                        while done < min(due, fills):
                            row_scores(done)
                            done += 1
                    if n:
                        products(n - 1)
                    if u == 0 and p + 1 < PAIRS:
                        turn_maxima(p + 1)
                products(PAIRS * nu - 1)
                pe.wait_ge(out_t_ready.sem, out_t_ready.at(turn, PAIRS))
                for c in range(TILES):
                    for p in range(PAIRS):
                        last = nc.tensor.matmul(PS[:, ST, c * P:(c + 1) * P], out_t[:, p, c * P:(c + 1) * P],
                                                core.wide_wo[:, p, :], start=p == 0, stop=p == PAIRS - 1)
                last.then_inc(wo_summed.sem, 1)
                pe.wait_ge(y_read.sem, y_read.at(turn, 1))


def broadcast_rows(vector):
    return vector.rearrange("(a n) -> a n", a=1).to_broadcast([P, vector.shape[0]])


class Net(Core):

    def __init__(self, nc, ctx, w, x_dram):
        super().__init__(nc, ctx)
        self.w, self.x_dram = w, x_dram
        self.PS = ctx.enter_context(nc.psum_tensor("banks", [P, 8, 512], F32))[:, :, :]
        self.X1 = self.sbuf("tokens1", [P, ALL_TILES, D])
        self.X = self.sbuf("tokens", [P, BATCH * TILES, D])
        self.ident = self.sbuf("ident", [P, P])
        self.ident_b = self.sbuf("ident_b", [P, P], BF16)
        self.mask = self.sbuf("mask", [P, P], BF16)
        self.minus_half = self.sbuf("minus_half", [P, TILES])
        self.constants_made = self.semaphore("constants_made")
        self.constants_ready = self.semaphore("constants_ready", 4)
        self.x_first = self.semaphore("x_first")
        self.x_rest = self.semaphore("x_rest")
        self.loads = []

        def load(signal, target, source):
            self.loads.append((target, source, signal))
            signal.per_turn += 16

        self.weights_a, self.biases_a = self.semaphore("weights_a", 0), self.semaphore("biases_a", 0)
        self.weights_b, self.weights_c = self.semaphore("weights_b", 0), self.semaphore("weights_c", 0)
        self.weights_d, self.biases_d = self.semaphore("weights_d", 0), self.semaphore("biases_d", 0)
        self.weights_e = self.semaphore("weights_e", 0)

        def narrow(tag, prefix, names, weights, biases):
            w_qkv = self.sbuf(f"w_qkv_{tag}", [P, 3 * D])
            b_qkv = self.sbuf(f"b_qkv_{tag}", [P, 3 * D])
            w_o, b_o = self.sbuf(f"w_o_{tag}", [P, D]), self.sbuf(f"b_o_{tag}", [P, D])
            for i, letter in enumerate("qkv"):
                load(weights, w_qkv[:, i * D:(i + 1) * D], w[f"{prefix}_{names[0]}{letter}"])
            load(weights, w_o[:, :], w[f"{prefix}_{names[0]}o"])
            for i, letter in enumerate("qkv"):
                load(biases, b_qkv[:, i * D:(i + 1) * D], broadcast_rows(w[f"{prefix}_b{letter}"]))
            load(biases, b_o[:, :], broadcast_rows(w[f"{prefix}_bo"]))
            return w_qkv, b_qkv, w_o, b_o

        self.ones = self.sbuf("ones", [P, P])
        self.narrow_a = narrow("a", "L0_attn", "w", self.weights_a, self.biases_a)
        self.w_fc = self.sbuf("w_fc", [P, FC, D])
        load(self.weights_b, self.w_fc[:, :, :], w["L0_ffn_W_fc"].rearrange("(a p) d -> p a d", p=P))
        self.w_proj = self.sbuf("w_proj", [P, FC, P])
        load(self.weights_b, self.w_proj[:, :, :], w["L0_ffn_W_proj"].rearrange("d (a p) -> d a p", p=P))
        self.ln_w, self.ln_b = self.sbuf("ln_w", [P, FC]), self.sbuf("ln_b", [P, FC])
        for tile, key in ((self.ln_w, "L0_ffn_ln_w"), (self.ln_b, "L0_ffn_ln_b")):
            load(self.weights_b, tile[:, :], w[key].rearrange("(a p) -> p a", p=P))
        self.wide_w = []
        for letter in "qkv":
            self.wide_w.append(self.sbuf(f"wide_w{letter}", [P, HEADS, HD64]))
            load(self.weights_c, self.wide_w[-1][:, :, :], w[f"L1_attn_W{letter}"].rearrange("h d e -> d h e"))
        self.wide_wo = self.sbuf("wide_wo", [P, PAIRS, D])
        load(self.weights_c, self.wide_wo[:, :, :], w["L1_attn_Wo"].rearrange("(a p) d -> p a d", p=P))
        self.wide_gamma, self.wide_beta = self.sbuf("wide_gamma", [P, D]), self.sbuf("wide_beta", [P, D])
        load(self.weights_c, self.wide_gamma[:, :], broadcast_rows(w["L1_attn_gamma"]))
        load(self.weights_c, self.wide_beta[:, :], broadcast_rows(w["L1_attn_beta"]))
        self.narrow_d = narrow("d", "L1_ffn", "W", self.weights_d, self.biases_d)
        self.ln1_g, self.ln1_b = self.sbuf("ln1_g", [P, D]), self.sbuf("ln1_b", [P, D])
        load(self.biases_d, self.ln1_g[:, :], broadcast_rows(w["L1_ffn_ln1_g"]))
        load(self.biases_d, self.ln1_b[:, :], broadcast_rows(w["L1_ffn_ln1_b"]))
        self.w1 = self.sbuf("w1", [P, EXPERTS, FF])
        load(self.weights_e, self.w1[:, :, :], w["L1_ffn_W1"].rearrange("e d f -> d e f"))
        self.w2 = self.sbuf("w2", [P, EXPERTS, FC, D])
        load(self.weights_e, self.w2[:, :, :, :], w["L1_ffn_W2"].rearrange("e (a p) d -> p e a d", p=P))
        self.b1 = self.sbuf("b1", [P, EXPERTS * FC])
        load(self.weights_e, self.b1[:, :], w["L1_ffn_b1"].rearrange("e (a p) -> p (e a)", p=P))
        self.b2 = self.sbuf("b2", [P, EXPERTS * D])
        load(self.weights_e, self.b2[:, :], broadcast_rows(w["L1_ffn_b2"].rearrange("e d -> (e d)")))
        self.router_w, self.router_b = self.sbuf("router_w", [P, D]), self.sbuf("router_b", [P, 1])
        load(self.weights_e, self.router_w[:, :], broadcast_rows(w["L1_ffn_router_w"].rearrange("d o -> (d o)")))
        load(self.weights_e, self.router_b[:, :], broadcast_rows(w["L1_ffn_router_b"]))
        self.ln2_g, self.ln2_b = self.sbuf("ln2_g", [P, D]), self.sbuf("ln2_b", [P, D])
        load(self.weights_e, self.ln2_g[:, :], broadcast_rows(w["L1_ffn_ln2_g"]))
        load(self.weights_e, self.ln2_b[:, :], broadcast_rows(w["L1_ffn_ln2_b"]))

    def start_loads(self, sp):
        x = self.x_dram.rearrange("b (c p) d -> p b c d", p=P)
        tokens = self.X[:, :, :].rearrange("p (b c) d -> p b c d", c=TILES)
        sp.dma_start(tokens[:, 0], x[:, 0]).then_inc(self.x_first.sem, 16)
        for n, (target, source, signal) in enumerate(self.loads):
            with self.nc.allow_non_contiguous_dma(reason="short vectors laid out by feature"):
                sp.dma_start(target, source).then_inc(signal.sem, 16)
            if n == 7:
                sp.dma_start(tokens[:, 1:].rearrange("p b c d -> p (b c) d"),
                             x[:, 1:].rearrange("p b c d -> p (b c) d")).then_inc(self.x_rest.sem, 16)

    def make_constants(self, pool):
        nc = self.nc
        nc.gpsimd.memset(self.ident[:, :], 0.0)
        nc.gpsimd.memset(self.ident_b[:, :], 0.0)
        nc.gpsimd.memset(self.mask[:, :], 0.0).then_inc(self.constants_made.sem, 1)
        pool.wait_ge(self.constants_made.sem, 1)
        for tile in (self.ident, self.ident_b):
            nc.gpsimd.affine_select(out=tile[:, :], in_=tile[:, :], compare_op=ALU.not_equal, fill=1.0, base=0,
                                    pattern=[[-1, P]], channel_multiplier=1).then_inc(self.constants_ready.sem, 1)
        nc.gpsimd.affine_select(out=self.mask[:, :], in_=self.mask[:, :], compare_op=ALU.is_ge, fill=MASKED, base=0,
                                pattern=[[-1, P]], channel_multiplier=1).then_inc(self.constants_ready.sem, 1)
        nc.gpsimd.memset(self.ones[:, :], 1.0)
        nc.gpsimd.memset(self.minus_half[:, :], -0.5).then_inc(self.constants_ready.sem, 1)


def build(nc, w, x_dram, out, phases="abcde"):
    with ExitStack() as ctx:
        core = Net(nc, ctx, w, x_dram)
        core.first_phase = phases[0]
        stored = core.semaphore("stored")
        with nc.Block() as block:
            @block.sync
            def _(sp):
                core.start_loads(sp)

            @block.gpsimd
            def _(pool):
                core.make_constants(pool)

        if "a" in phases:
            narrow_attention(core, "first", "a", True, *core.narrow_a, (core.weights_a, core.biases_a), add_normalised)
        if "b" in phases:
            gelu_ffn(core, "rounded", "b")
        if "c" in phases:
            wide_attention(core, "wide", "c")
        if "d" in phases:
            narrow_attention(core, "last", "d", False, *core.narrow_d, (core.weights_d, core.biases_d),
                             keep_norm1(core))
            expert_ffn(core, "experts", "e", stored, out)
        else:
            with nc.Block() as block:
                @block.sync
                def _(sp):
                    sp.dma_start(out.rearrange("b (c p) d -> p (b c) d", p=P), core.X[:, 0:4*BATCH, :]).then_inc(stored.sem, 16)
                    sp.wait_ge(stored.sem, 16)


def kernel(**inputs):
    import numpy as _np
    import concourse.bacc as _bacc
    from concourse import mybir as _mybir
    from concourse.bass_utils import run_bass_kernel_spmd as _run

    nc = _bacc.Bacc("TRN2", target_bir_lowering=False, num_devices=1)
    arrays, handles = {}, {}
    for name, value in inputs.items():
        a = _np.ascontiguousarray(value)
        arrays[f"in_{name}"] = a
        handles[name] = nc.dram_tensor(f"in_{name}", a.shape, _mybir.dt.from_np(a.dtype), kind="ExternalInput").ap()
    out = nc.dram_tensor("out", (BATCH, SEQ, D), F32, kind="ExternalOutput").ap()
    build(nc, handles, handles["L0_attn_x"], out)
    r = _run(nc, [arrays], core_ids=[0])
    return r.results[0]["out"]
```

```python
from contextlib import ExitStack

import concourse.bass as bass
from concourse import mybir

F32 = mybir.dt.float32
BF16 = mybir.dt.bfloat16
ALU = mybir.AluOpType
ACT = mybir.ActivationFunctionType
AX = mybir.AxisListType

P = 128
BATCH, SEQ, D = 8, 512, 128
TILES = SEQ // P
ALL_TILES = BATCH * TILES
HEADS = 16
HD8 = D // HEADS
QUAD = 32
GROUPS = HEADS * QUAD // P
GH = HEADS // GROUPS
HD64 = 64
PAIRS = HEADS // 2
FF = 512
FC = FF // P
EXPERTS = 4
MASKED = -3.0e38


class Signal:

    def __init__(self, sem, per_turn):
        self.sem, self.per_turn = sem, per_turn

    def at(self, turn, k):
        return turn * self.per_turn + k


class Core:

    def __init__(self, nc, ctx):
        self.nc, self.ctx = nc, ctx

    def sbuf(self, name, shape, dtype=F32, ctx=None):
        return (ctx or self.ctx).enter_context(self.nc.sbuf_tensor(name, shape, dtype))

    def semaphore(self, name, per_turn=1):
        return Signal(self.ctx.enter_context(self.nc.semaphore(name)), per_turn)


def make_link(dve, signal, turn):
    count = [0]

    def link(instruction):
        count[0] += 1
        instruction.then_inc(signal.sem, 1)
        dve.wait_ge(signal.sem, signal.at(turn, count[0]))

    def finish():
        assert count[0] == signal.per_turn, (count[0], signal.per_turn)

    return link, finish


def norm_statistics(nc, link, s, source, tiles, width):
    for c in range(tiles):
        last = nc.vector.bn_stats(s.stats[:, c, :], source(c))
    link(last)
    nc.vector.tensor_copy(s.carrier[:, :], s.stats[:, 0, 0:1])
    for c in range(tiles):
        last = nc.vector.bn_aggr(s.mean_var[:, c, :], s.stats[:, c, :])
    link(last)


def normalise(nc, dve, link, s, turn, k, source, target, eps, done=None):
    norm_statistics(nc, link, s, source, TILES, D)
    nc.vector.tensor_scalar(s.var_eps[:, :], s.mean_var[:, :, 1], eps, None, ALU.add).then_inc(s.var_ready.sem, 1)
    dve.wait_ge(s.rstd_ready.sem, s.rstd_ready.at(turn, k + 1))
    for c in range(TILES):
        last = nc.vector.tensor_scalar(target(c), source(c), s.mean_var[:, c, 0:1], s.rstd[:, c:c + 1],
                                       ALU.subtract, ALU.mult)
        if done is not None:
            last.then_inc(done.sem, 1)
    return last


def inverse_roots(nc, pool, s, turn, ks):
    for k in ks:
        pool.wait_ge(s.var_ready.sem, s.var_ready.at(turn, k + 1))
        nc.gpsimd.tensor_tensor(s.rstd[:, :], s.var_eps[:, :], s.minus_half[:, :], ALU.pow).then_inc(
            s.rstd_ready.sem, 1)


class Stage:

    def __init__(self, written, read, names, base):
        self.written, self.read, self.names, self.base = written, read, names, base

    def fill(self, pe, name):
        k = self.names.index(name)
        if not (isinstance(self.base, int) and self.base + k == 0):
            pe.wait_ge(self.read.sem, self.base + k)

    def drain(self, engine, name):
        engine.wait_ge(self.written.sem, self.base + self.names.index(name) + 1)

    def after(self, engine, name):
        engine.wait_ge(self.read.sem, self.base + self.names.index(name) + 1)


class Chain:

    def __init__(self, dve, signal, base):
        self.dve, self.raised, self.base, self.count = dve, signal, base, 0

    def link(self, instruction):
        self.count += 1
        instruction.then_inc(self.raised.sem, 1)
        self.dve.wait_ge(self.raised.sem, self.base + self.count)


class NormState:

    def __init__(self, core, sb, sig, name):
        self.stats = sb(f"{name}_stats", [P, TILES, 6])
        self.mean_var = sb(f"{name}_mean_var", [P, TILES, 2])
        self.carrier = sb(f"{name}_carrier", [P, 1])
        self.var_eps = sb(f"{name}_var_eps", [P, TILES])
        self.rstd = sb(f"{name}_rstd", [P, TILES])
        self.minus_half = core.minus_half
        self.var_ready = sig(f"{name}_var_ready")
        self.rstd_ready = sig(f"{name}_rstd_ready")

    def statistics(self, nc, link, source, eps, width=D):
        norm_statistics(nc, link, self, source, TILES, width)
        nc.vector.tensor_scalar(self.var_eps[:, :], self.mean_var[:, :, 1], eps, None, ALU.add).then_inc(
            self.var_ready.sem, 1)

    def power(self, nc, pool, t):
        pool.wait_ge(self.var_ready.sem, self.var_ready.at(t, 1))
        nc.gpsimd.tensor_tensor(self.rstd[:, :], self.var_eps[:, :], self.minus_half[:, :], ALU.pow).then_inc(
            self.rstd_ready.sem, 1)

    def apply(self, nc, dve, t, source, target):
        dve.wait_ge(self.rstd_ready.sem, self.rstd_ready.at(t, 1))
        for c in range(TILES):
            last = nc.vector.tensor_scalar(target(c), source(c), self.mean_var[:, c, 0:1], self.rstd[:, c:c + 1],
                                           ALU.subtract, ALU.mult)
        return last


class Narrow:

    def __init__(self, core, name, tag, causal, ctx):
        sb = lambda n, shape, dtype=F32: core.sbuf(f"{name}_{n}", shape, dtype, ctx)
        sig = lambda n, per=1: core.semaphore(f"{tag}_{n}", per)
        self.front_norm = NormState(core, sb, sig, "front")
        self.tail_norm = NormState(core, sb, sig, "tail")
        self.pool_carrier = sb("pool_carrier", [P, 1])
        self.xn = sb("xn", [P, 2, TILES, D])
        self.xt = sb("xt", [P, SEQ])
        self.qk = sb("qk", [P, TILES, 2, D])
        self.v = sb("v", [P, 2, TILES, HEADS, HD8 + 1])
        self.q_parts = sb("q_parts", [P, TILES, HEADS, QUAD], BF16)
        self.k_parts = sb("k_parts", [P, TILES, HEADS, QUAD], BF16)
        self.qkt = sb("qkt", [P, 2, GROUPS, 2, SEQ], BF16)
        self.q_alone = sb("q_alone", [P, 2, HEADS, SEQ], BF16)
        self.neg_max = sb("neg_max", [P, GROUPS, TILES, GH])
        self.max_parts = sb("max_parts", [P, GROUPS, TILES, GH, 2], BF16)
        self.max_t = sb("max_t", [2 * GH, GROUPS, SEQ], BF16)
        self.probs = sb("probs", [P, 2 * GH, SEQ])
        self.out_t = sb("out_t", [P, 2, GROUPS, SEQ])
        self.inverse = sb("inverse", [P, TILES, HEADS])
        self.attn = sb("attn", [P, TILES, D])
        self.attn_t = sb("attn_t", [P, SEQ])
        self.y = sb("y", [P, TILES, D])
        self.y_norm = sb("y_norm", [P, TILES, D])
        if causal:
            self.units = [[(0, 0, 0, 512)], [(1, 128, 0, 384), (3, 384, 384, 128)], [(2, 256, 0, 256)]]
            self.steps = {0: "norm", 1: "xn xt proj0", 2: "proj1 proj2 proj3 high", 3: "low parts0 parts1",
                          4: "parts2 parts3 place", 6: "out0 out1", 7: "out2 out3", 8: "attn", 9: "wo",
                          10: "y_norm", 11: "y_add"}
        else:
            self.units = [[(k, 0, 0, SEQ)] for k in range(TILES)]
            self.steps = {0: "norm", 1: "xn xt", 2: "proj0 proj1", 3: "proj2 proj3 high", 4: "low parts0",
                          5: "parts1 parts2", 6: "parts3 place", 8: "out0", 9: "out1", 10: "out2", 11: "out3",
                          12: "attn", 13: "wo", 14: "y_norm", 15: "y_add"}
        self.nu = len(self.units)
        self.n_units = n = GROUPS * self.nu
        self.links = 2 + 4 + 4 + 2 + (2 if causal else 4)
        self.link = sig("link")
        self.ready = sig("ready")
        self.stage_written, self.stage_read = sig("stage_written"), sig("stage_read")
        self.xn_ready = sig("xn_ready")
        self.xn_kept = sig("xn_kept")
        self.high_ready = sig("high_ready", 4)
        self.low_ready = sig("low_ready", 2)
        self.q_alone_ready = sig("q_alone_ready", 16 * GH)
        self.row_scores = sig("row_scores", GROUPS * TILES * 2)
        self.row_max = sig("row_max", GROUPS * TILES * 2)
        self.max_ready = sig("max_ready", GROUPS)
        self.max_placed = [sig(f"max_placed{g}", 16 * GH) for g in range(GROUPS)]
        self.scores = sig("scores", n * GH)
        self.exp_done = sig("exp_done", n * GH)
        self.masked = sig("masked", n)
        self.pv_done = sig("pv_done", n)
        self.out_t_ready = sig("out_t_ready", GROUPS)

    FRONT = "norm xn xt proj0 proj1 proj2 proj3 high low parts0 parts1 parts2 parts3 place".split()
    TAIL = "out0 out1 out2 out3 attn wo y_norm y_add".split()
    UNSTAGED = "norm xn high low place y_norm y_add".split()

    def slot(self, n, kind):
        g, names = n // self.nu, []
        if n % self.nu == 0 and not (g == GROUPS - 1 and kind == "last"):
            names.append(f"max{(g + 1) % GROUPS}")
        for name in self.steps.get(n, "").split():
            if (kind != "last" or name not in self.FRONT) and (kind != "first" or name not in self.TAIL):
                names.append(name)
        return names

    def staged(self, kind):
        if kind == "before":
            names = self.FRONT + ["max0"]
        elif kind == "after":
            names = self.TAIL
        else:
            names = [name for n in range(self.n_units) for name in self.slot(n, kind)]
        return [name for name in names if name not in self.UNSTAGED]

    def fills(self, n):
        per_group = 2 * TILES
        due = lambda i: 2 * per_group + i * per_group // (GH * self.nu)
        return [range(due(GH * n + j), due(GH * n + j + 1)) for j in range(GH)]

    def stage(self, kind, t):
        count = lambda k: len(self.staged(k))
        if kind == "before":
            base = 0
        elif kind == "first":
            base = count("before")
        else:
            base = count("before") + count("first") + (t - 1) * count("mid")
            if kind == "after":
                base = base - count("mid") + count("last")
        return Stage(self.stage_written, self.stage_read, self.staged(kind), base)


def over_turns(engine, before, turn, after):
    before()
    turn(0, 0, "first")
    with engine.Fori(0, (BATCH - 2) // 2) as i:
        turn(2 * i + 1, 1, "mid")
        turn(2 * i + 2, 0, "mid")
    turn(BATCH - 1, 1, "last")
    after()


def narrow_attention(core, name, tag, causal, w_qkv, b_qkv, w_o, b_o, weights, result):
    nc, X, PS = core.nc, core.X, core.PS
    PB = PS.bitcast(BF16)
    scale = float(HD8) ** -0.5
    ident, ident_b = core.ident, core.ident_b
    ST, STAGE, OUT = 4, 6, 7
    ROWS = GROUPS * TILES * 2

    with ExitStack() as ctx:
        s = Narrow(core, name, tag, causal, ctx)
        units, nu, N = s.units, s.nu, s.n_units
        block = ctx.enter_context(nc.Block())

        @block.sync
        def _(sp):
            def step(stage, name, t, b):
                if name == "place":
                    stage.after(sp, "parts3")
                    alone = s.q_alone[:, b, :, :].rearrange("p (g j) t -> p g j t", j=GH)
                    for j in range(GH):
                        rows = slice(QUAD * j, QUAD * (j + 1))
                        sp.dma_start(alone[rows, :, j, :], s.qkt[rows, b, :, 0, :]).then_inc(s.q_alone_ready.sem, 16)
                elif name[:3] == "max":
                    g = int(name[3:])
                    stage.after(sp, name)
                    for j in range(GH):
                        first = QUAD * j + 3 * HD8
                        sp.dma_start(s.q_alone[first:first + 2, b, GH * g + j, :],
                                     s.max_t[2 * j:2 * j + 2, g, :]).then_inc(s.max_placed[g].sem, 16)

            def before():
                stage = s.stage("before", 0)
                step(stage, "place", 0, 0)
                step(stage, "max0", 0, 0)

            def turn(t, b, kind):
                stage = s.stage(kind, t)
                for n in range(N):
                    for name in s.slot(n, kind):
                        ahead = name == "place" or name == "max0"
                        step(stage, name, t + 1 if ahead else t, 1 - b if ahead else b)

            over_turns(sp, before, turn, lambda: None)

        @block.gpsimd
        def _(pool):
            nc.gpsimd.memset(s.v[:, :, :, :, HD8:], 1.0)
            nc.gpsimd.memset(s.q_parts[:, :, :, 3 * HD8:], 0.0)
            nc.gpsimd.memset(s.k_parts[:, :, :, 3 * HD8:3 * HD8 + 2], 1.0)
            nc.gpsimd.memset(s.k_parts[:, :, :, 3 * HD8 + 2:], 0.0)
            nc.gpsimd.memset(s.q_alone[:, :, :, :], 0.0).then_inc(s.ready.sem, 1)

            def turn(t, b, kind):
                for n in range(N):
                    if causal:
                        pool.wait_ge(s.exp_done.sem, s.exp_done.at(t, GH * (n + 1)))
                        if n or kind != "first":
                            pool.wait_ge(s.masked.sem, s.masked.at(t, n))
                        nc.gpsimd.tensor_tensor(s.pool_carrier[:, :], core.minus_half[:, 0:1],
                                                core.minus_half[:, 0:1], ALU.add)
                        slot = n % 2 * GH
                        for _, _, at, _ in units[n % nu]:
                            square = s.probs[:, slot:slot + GH, at:at + P]
                            last = nc.gpsimd.affine_select(out=square, in_=square, compare_op=ALU.is_ge, fill=0.0,
                                                           base=0, pattern=[[0, GH], [1, P]], channel_multiplier=-1)
                        last.then_inc(s.masked.sem, 1)
                    for name in s.slot(n, kind):
                        if name == "norm":
                            s.front_norm.power(nc, pool, t + 1)
                        elif name == "xn" and not causal:
                            keep_xn(t + 1, 1 - b)
                        elif name == "y_norm":
                            s.tail_norm.power(nc, pool, t - 1)

            def keep_xn(t, b):
                pool.wait_ge(s.xn_ready.sem, s.xn_ready.at(t, 1))
                nc.gpsimd.tensor_copy(core.X1[:, bass.ds(t * TILES, TILES), :], s.xn[:, b, :, :]).then_inc(
                    s.xn_kept.sem, 1)

            def before():
                s.front_norm.power(nc, pool, 0)
                if not causal:
                    keep_xn(0, 0)

            over_turns(pool, before, turn,
                       lambda: s.tail_norm.power(nc, pool, BATCH - 1))

        @block.vector
        def _(dve):
            nc.vector.memset(PS[:, OUT, :], 0.0).then_inc(s.ready.sem, 1)
            dve.wait_ge(s.ready.sem, 2)
            for load in weights[1:]:
                dve.wait_ge(load.sem, load.per_turn)

            def row_max(t, n):
                g, c, half = n // (2 * TILES), n // 2 % TILES, n % 2
                keys = P * (c + 1) if causal else SEQ
                dve.wait_ge(s.row_scores.sem, s.row_scores.at(t, n + 1))
                bank = n % 2 * 2
                nc.vector.tensor_reduce(s.neg_max[:, g, c, 2 * half:2 * half + 2], PS[:, bank:bank + 2, 0:keys], AX.X,
                                        ALU.max, negate=True).then_inc(s.row_max.sem, 1)

            def split_maxima(chain, t, g):
                dve.wait_ge(s.row_max.sem, s.row_max.at(t, (g + 1) * TILES * 2))
                maxima = s.neg_max[:, g, :, :]
                chain.link(nc.vector.tensor_copy(s.max_parts[:, g, :, :, 0], maxima))
                nc.vector.tensor_tensor(s.max_parts[:, g, :, :, 1], maxima, s.max_parts[:, g, :, :, 0],
                                        ALU.subtract).then_inc(s.max_ready.sem, 1)

            def step(chain, stage, name, t, b):
                x = lambda c: X[:, t * TILES + c, :]
                if name == "norm":
                    s.front_norm.statistics(nc, chain.link, x, 1e-5)
                elif name == "xn":
                    if not causal and not (isinstance(t, int) and t < 2):
                        dve.wait_ge(s.xn_kept.sem, s.xn_kept.at(t, -1))
                    s.front_norm.apply(nc, dve, t, x, lambda c: s.xn[:, b, c, :]).then_inc(s.xn_ready.sem, 1)
                elif name[:4] == "proj":
                    c = int(name[4:])
                    stage.drain(dve, name)
                    nc.vector.tensor_tensor(s.qk[:, c, :, :].rearrange("p a d -> p (a d)"), PS[:, STAGE, 0:2 * D],
                                            b_qkv[:, 0:2 * D], ALU.add)
                    nc.vector.tensor_tensor(s.v[:, b, c, :, 0:HD8],
                                            PS[:, STAGE, 2 * D:3 * D].rearrange("p (h e) -> p h e", e=HD8),
                                            b_qkv[:, 2 * D:3 * D].rearrange("p (h e) -> p h e", e=HD8),
                                            ALU.add).then_inc(s.stage_read.sem, 1)
                elif name == "low":
                    for a, (parts, first) in enumerate(((s.q_parts, HD8), (s.k_parts, 2 * HD8))):
                        dve.wait_ge(s.high_ready.sem, s.high_ready.at(t, 2 * a + 1))
                        nc.vector.tensor_tensor(parts[:, :, :, first:first + HD8],
                                                s.qk[:, :, a, :].rearrange("p c (h e) -> p c h e", e=HD8),
                                                parts[:, :, :, 0:HD8], ALU.subtract).then_inc(s.low_ready.sem, 1)
                elif name[:5] == "parts":
                    g = int(name[5:])
                    stage.drain(dve, name)
                    nc.vector.tensor_copy(s.qkt[:, b, g, :, :].rearrange("p a t -> p (a t)"),
                                          PB[:, STAGE, :]).then_inc(s.stage_read.sem, 1)
                elif name[:3] == "out":
                    c = int(name[3:])
                    stage.drain(dve, name)
                    heads = PS[:, STAGE, :].rearrange("p (h r) -> p h r", r=QUAD)
                    chain.link(nc.vector.reciprocal(s.inverse[:, c, :], heads[:, :, HD8]))
                    nc.vector.tensor_tensor(s.attn[:, c, :].rearrange("p (h e) -> p h e", e=HD8), heads[:, :, 0:HD8],
                                            s.inverse[:, c, :].unsqueeze(2).to_broadcast([P, HEADS, HD8]),
                                            ALU.mult).then_inc(s.stage_read.sem, 1)
                elif name == "wo":
                    stage.drain(dve, name)
                    nc.vector.tensor_tensor(s.y[:, :, :], PS[:, STAGE, :].rearrange("p (c d) -> p c d", d=D),
                                            b_o[:, :].unsqueeze(1).to_broadcast([P, TILES, D]),
                                            ALU.add).then_inc(s.stage_read.sem, 1)
                elif name == "y_norm":
                    stage.after(dve, "wo")
                    if not causal:
                        dve.wait_ge(s.xn_kept.sem, s.xn_kept.at(t, 1))
                        chain.link(nc.vector.tensor_tensor(s.y[:, :, :], s.y[:, :, :],
                                                           core.X1[:, bass.ds(t * TILES, TILES), :], ALU.add))
                    s.tail_norm.statistics(nc, chain.link, lambda c: s.y[:, c, :], 1e-5)
                elif name == "y_add":
                    chain.link(s.tail_norm.apply(nc, dve, t, lambda c: s.y[:, c, :], lambda c: s.y_norm[:, c, :]))
                    result(nc, chain.link, s, t, x)

            links = [0]

            def before():
                chain = Chain(dve, s.link, 0)
                stage = s.stage("before", 0)
                if tag == core.first_phase:
                    dve.wait_ge(core.x_first.sem, 16)
                for name in s.FRONT:
                    step(chain, stage, name, 0, 0)
                if tag == core.first_phase:
                    dve.wait_ge(core.x_rest.sem, 16)
                for n in range(2 * 2 * TILES):
                    row_max(0, n)
                    if n % (2 * TILES) == 2 * TILES - 1:
                        split_maxima(chain, 0, n // (2 * TILES))
                links[0] = chain.count

            def turn(t, b, kind):
                first = links[0] if kind == "first" else links[0] + (t - 1) * s.links
                chain = Chain(dve, s.link, first)
                stage = s.stage(kind, t)
                for n in range(N):
                    for fills in s.fills(n):
                        for m in fills:
                            if m < ROWS or kind != "last":
                                t_rows = t if m < ROWS else t + 1
                                row_max(t_rows, m % ROWS)
                                if m % (2 * TILES) == 2 * TILES - 1:
                                    split_maxima(chain, t_rows, m % ROWS // (2 * TILES))
                    for name in s.slot(n, kind):
                        if name in s.FRONT:
                            step(chain, stage, name, t + 1, 1 - b)
                        elif name in s.TAIL:
                            step(chain, stage, name, t - 1, 1 - b)
                if kind == "first":
                    links[0] += chain.count
                else:
                    assert kind == "last" or chain.count == s.links, (chain.count, s.links)
                last_links[0] = chain.count

            last_links = [0]

            def after():
                chain = Chain(dve, s.link, links[0] + (BATCH - 2) * s.links + last_links[0])
                stage = s.stage("after", BATCH)
                for name in s.TAIL:
                    step(chain, stage, name, BATCH - 1, 1)

            over_turns(dve, before, turn, after)

        @block.scalar
        def _(act):
            act.wait_ge(s.ready.sem, 2)

            def exps(t, n, kind):
                width = sum(w for _, _, _, w in units[n % nu])
                for j in range(GH):
                    if n >= 2 or kind != "first":
                        act.wait_ge(s.pv_done.sem, s.pv_done.at(t, n - 1))
                    act.wait_ge(s.scores.sem, s.scores.at(t, GH * n + j + 1))
                    nc.scalar.activation(s.probs[:, n % 2 * GH + j, 0:width], PS[:, ST + j % 2, 0:width],
                                         ACT.Exp, scale=scale).then_inc(s.exp_done.sem, 1)

            def keep_products(t, b, g):
                act.wait_ge(s.pv_done.sem, s.pv_done.at(t, nu * (g + 1)))
                nc.scalar.activation(s.out_t[:, b, g, :], PS[:, OUT, :], ACT.Copy).then_inc(s.out_t_ready.sem, 1)

            def step(stage, name, t):
                if name == "xt":
                    stage.drain(act, name)
                    nc.scalar.activation(s.xt[:, :], PS[:, STAGE, :], ACT.Copy).then_inc(s.stage_read.sem, 1)
                elif name == "high":
                    stage.after(act, "proj3")
                    for a, (parts, copies) in enumerate(((s.q_parts, (0, 2 * HD8)), (s.k_parts, (0, HD8)))):
                        for first in copies:
                            nc.scalar.activation(parts[:, :, :, first:first + HD8],
                                                 s.qk[:, :, a, :].rearrange("p c (h e) -> p c h e", e=HD8),
                                                 ACT.Copy).then_inc(s.high_ready.sem, 1)
                elif name[:3] == "max":
                    stage.drain(act, name)
                    nc.scalar.activation(s.max_t[:, int(name[3:]), :], PB[0:2 * GH, STAGE, 0:SEQ],
                                         ACT.Copy).then_inc(s.stage_read.sem, 1)
                elif name == "attn":
                    stage.drain(act, name)
                    nc.scalar.activation(s.attn_t[:, :], PS[:, STAGE, :], ACT.Copy).then_inc(s.stage_read.sem, 1)

            def before():
                stage = s.stage("before", 0)
                for name in s.FRONT + ["max0"]:
                    step(stage, name, 0)

            def turn(t, b, kind):
                stage = s.stage(kind, t)
                for n in range(N):
                    exps(t, n, kind)
                    if n % nu == 0 and n:
                        keep_products(t, b, n // nu - 1)
                    elif n == 0 and kind != "first":
                        keep_products(t - 1, 1 - b, GROUPS - 1)
                    for name in s.slot(n, kind):
                        step(stage, name, t + 1 if name in s.FRONT else t - 1)

            def after():
                keep_products(BATCH - 1, 1, GROUPS - 1)
                step(s.stage("after", BATCH), "attn", BATCH - 1)

            over_turns(act, before, turn, after)

        @block.tensor
        def _(pe):
            pe.wait_ge(s.ready.sem, 2)
            pe.wait_ge(core.constants_ready.sem, core.constants_ready.per_turn)
            pe.wait_ge(weights[0].sem, weights[0].per_turn)

            def row_scores(t, b, n, first):
                g, c, half = n // (2 * TILES), n // 2 % TILES, n % 2
                if n == 0:
                    pe.wait_ge(s.q_alone_ready.sem, s.q_alone_ready.at(t, 16 * GH))
                if n >= 2 or not first:
                    pe.wait_ge(s.row_max.sem, s.row_max.at(t, n - 1))
                keys = P * (c + 1) if causal else SEQ
                for h in range(2):
                    bank = n % 2 * 2 + h
                    last = nc.tensor.matmul(PS[:, bank, 0:keys],
                                            s.q_alone[:, b, GH * g + 2 * half + h, c * P:(c + 1) * P],
                                            s.qkt[:, b, g, 1, 0:keys], start=True, stop=not causal)
                    if causal:
                        last = nc.tensor.matmul(PS[:, bank, keys - P:keys], ident_b[:, :], core.mask[:, :],
                                                start=False, stop=True)
                last.then_inc(s.row_scores.sem, 1)

            def products(t, b, n):
                g, u = n // nu, n % nu
                if causal:
                    pe.wait_ge(s.masked.sem, s.masked.at(t, n + 1))
                else:
                    pe.wait_ge(s.exp_done.sem, s.exp_done.at(t, GH * (n + 1)))
                if u == 0 and not (g == 0 and isinstance(t, int) and t == 0):
                    pe.wait_ge(s.out_t_ready.sem, s.out_t_ready.at(t, g))
                for i, (k, q0, at, width) in enumerate(units[u]):
                    for j in range(GH):
                        last = nc.tensor.matmul(PS[QUAD * j:QUAD * j + HD8 + 1, OUT, q0:q0 + width],
                                                s.v[:, b, k, GH * g + j, :],
                                                s.probs[:, n % 2 * GH + j, at:at + width],
                                                start=u == 0 and i == 0, stop=u == nu - 1 and i == len(units[u]) - 1)
                last.then_inc(s.pv_done.sem, 1)

            def step(stage, name, t, b):
                if name in s.UNSTAGED:
                    return
                stage.fill(pe, name)
                if name == "xt":
                    pe.wait_ge(s.xn_ready.sem, s.xn_ready.at(t, 1))
                    for c in range(TILES):
                        last = nc.tensor.transpose(PS[:, STAGE, c * P:(c + 1) * P], s.xn[:, b, c, :], ident[:, :])
                elif name[:4] == "proj":
                    c = int(name[4:])
                    last = nc.tensor.matmul(PS[:, STAGE, 0:3 * D], s.xt[:, c * P:(c + 1) * P], w_qkv[:, :],
                                            start=True, stop=True)
                elif name[:5] == "parts":
                    g = int(name[5:])
                    if g == 0:
                        pe.wait_ge(s.high_ready.sem, s.high_ready.at(t, 4))
                        pe.wait_ge(s.low_ready.sem, s.low_ready.at(t, 2))
                    for a, parts in enumerate((s.q_parts, s.k_parts)):
                        for c in range(TILES):
                            at = a * SEQ + c * P
                            last = nc.tensor.transpose(
                                PB[:, STAGE, at:at + P],
                                parts[:, c, GH * g:GH * (g + 1), :].rearrange("p h r -> p (h r)"), ident_b[:, :])
                elif name[:3] == "max":
                    g = int(name[3:])
                    pe.wait_ge(s.max_ready.sem, s.max_ready.at(t, g + 1))
                    for c in range(TILES):
                        last = nc.tensor.transpose(PB[0:2 * GH, STAGE, c * P:(c + 1) * P],
                                                   s.max_parts[:, g, c, :, :].rearrange("p j r -> p (j r)"),
                                                   ident_b[:, :])
                elif name[:3] == "out":
                    c = int(name[3:])
                    if c == 0:
                        pe.wait_ge(s.out_t_ready.sem, s.out_t_ready.at(t, GROUPS))
                    for g in range(GROUPS):
                        last = nc.tensor.transpose(PS[:, STAGE, g * P:(g + 1) * P],
                                                   s.out_t[:, b, g, c * P:(c + 1) * P], ident[:, :])
                elif name == "attn":
                    for c in range(TILES):
                        last = nc.tensor.transpose(PS[:, STAGE, c * P:(c + 1) * P], s.attn[:, c, :], ident[:, :])
                elif name == "wo":
                    for c in range(TILES):
                        last = nc.tensor.matmul(PS[:, STAGE, c * P:(c + 1) * P], s.attn_t[:, c * P:(c + 1) * P],
                                                w_o[:, :], start=True, stop=True)
                last.then_inc(s.stage_written.sem, 1)

            def before():
                stage = s.stage("before", 0)
                for name in s.FRONT:
                    step(stage, name, 0, 0)
                for n in range(2 * 2 * TILES):
                    row_scores(0, 0, n, True)
                step(stage, "max0", 0, 0)

            def turn(t, b, kind):
                stage = s.stage(kind, t)
                for n in range(N):
                    g, u = n // nu, n % nu
                    if u == 0:
                        pe.wait_ge(s.max_placed[g].sem, s.max_placed[g].at(t, 16 * GH))
                    for j, fills in enumerate(s.fills(n)):
                        i = GH * n + j
                        if i >= 2 or kind != "first":
                            pe.wait_ge(s.exp_done.sem, s.exp_done.at(t, i - 1))
                        for k, q0, at, width in units[u]:
                            last = nc.tensor.matmul(PS[:, ST + j % 2, at:at + width],
                                                    s.qkt[:, b, g, 1, k * P:(k + 1) * P],
                                                    s.q_alone[:, b, GH * g + j, q0:q0 + width], start=True, stop=True)
                        last.then_inc(s.scores.sem, 1)
                        for m in fills:
                            if m < ROWS:
                                row_scores(t, b, m, False)
                            elif kind != "last":
                                row_scores(t + 1, 1 - b, m - ROWS, False)
                    if n:
                        products(t, b, n - 1)
                    elif kind != "first":
                        products(t - 1, 1 - b, N - 1)
                    for name in s.slot(n, kind):
                        ahead = name in s.FRONT or name == "max0"
                        if ahead:
                            step(stage, name, t + 1, 1 - b)
                        elif name in s.TAIL:
                            step(stage, name, t - 1, 1 - b)
                        else:
                            step(stage, name, t, b)

            def after():
                products(BATCH - 1, 1, N - 1)
                stage = s.stage("after", BATCH)
                for name in s.TAIL:
                    step(stage, name, BATCH - 1, 1)

            over_turns(pe, before, turn, after)


def scale_shift(nc, link, target, source, gain, offset):
    rows = [P, TILES, D]
    link(nc.vector.tensor_tensor(target[:, :, :], source[:, :, :], gain[:, :].unsqueeze(1).to_broadcast(rows), ALU.mult))
    link(nc.vector.tensor_tensor(target[:, :, :], target[:, :, :], offset[:, :].unsqueeze(1).to_broadcast(rows), ALU.add))


def add_normalised(nc, link, s, turn, x):
    for c in range(TILES):
        last = nc.vector.tensor_tensor(x(c), x(c), s.y_norm[:, c, :], ALU.add)
    link(last)


def keep_norm1(core):
    def result(nc, link, s, turn, x):
        rows = [P, TILES, D]
        gain, offset = core.ln1_g[:, :].unsqueeze(1), core.ln1_b[:, :].unsqueeze(1)
        link(nc.vector.tensor_tensor(s.y[:, :, :], s.y_norm[:, :, :], gain.to_broadcast(rows), ALU.mult))
        link(nc.vector.tensor_tensor(core.X1[:, bass.ds(turn * TILES, TILES), :], s.y[:, :, :],
                                     offset.to_broadcast(rows), ALU.add))
    return result


class Norms:

    def __init__(self, core, name, tag, links, norms, ctx):
        sb = lambda n, shape, dtype=F32: core.sbuf(f"{name}_{n}", shape, dtype, ctx)
        self.stats = sb("stats", [P, TILES, 6])
        self.mean_var = sb("mean_var", [P, TILES, 2])
        self.carrier = sb("carrier", [P, 1])
        self.var_eps = sb("var_eps", [P, TILES])
        self.rstd = sb("rstd", [P, TILES])
        self.minus_half = core.minus_half
        self.constants = core.constants_ready
        sig = lambda n, per=1: core.semaphore(f"{tag}_{n}", per)
        self.ready = sig("ready")
        self.link = sig("link", links)
        self.var_ready = sig("var_ready", norms)
        self.rstd_ready = sig("rstd_ready", norms)


def gelu_ffn(core, name, tag):
    nc, X, PS, ident = core.nc, core.X, core.PS, core.ident
    DOWN = 0
    with ExitStack() as ctx:
        sb = lambda n, shape, dtype=F32: core.sbuf(f"{name}_{n}", shape, dtype, ctx)
        s = Norms(core, name, tag, 2 + 2 + 3 + 1, 3, ctx)
        sig = lambda n, per=1: core.semaphore(f"{tag}_{n}", per)
        row_sums = sb("row_sums", [P, 2])
        threshold = sb("threshold", [P, 2, 2])
        above, below = sb("above", [P, 2, FF]), sb("below", [P, 2, FF])
        w_up, w_down = sb("w_up", [P, FF]), sb("w_down", [P, FC, D])
        xn, xt = sb("xn", [P, TILES, D]), sb("xt", [P, SEQ])
        hidden, hidden_n = sb("hidden", [P, TILES, FF]), sb("hidden_n", [P, TILES, FF])
        hidden_t = sb("hidden_t", [P, FC, SEQ])
        y, y_norm = sb("y", [P, TILES, D]), sb("y_norm", [P, TILES, D])
        setup = sig("setup", 5)
        sums_spread, turned_w, weights_ready = sig("sums_spread"), sig("turned_w"), sig("weights_ready", 2)
        xn_ready, xt_summed, xt_ready = sig("xn_ready", TILES), sig("xt_summed"), sig("xt_ready")
        up_summed, gelu_done, hidden_ready = sig("up_summed", TILES), sig("gelu_done", TILES), sig("hidden_ready", TILES)
        hidden_turned, hidden_t_ready = sig("hidden_turned", FC), sig("hidden_t_ready", FC)
        down_summed, y_read = sig("down_summed"), sig("y_read")
        block = ctx.enter_context(nc.Block())

        @block.gpsimd
        def _(pool):
            with pool.Fori(0, BATCH) as turn:
                inverse_roots(nc, pool, s, turn, [0, 1, 2])

        @block.vector
        def _(dve):
            dve.wait_ge(core.weights_b.sem, core.weights_b.per_turn)
            raw = (core.w_fc[:, :, :], core.w_proj[:, :, :])
            for i, weight in enumerate(raw):
                nc.vector.tensor_reduce(row_sums[:, i:i + 1], weight, AX.XY, ALU.add,
                                        apply_absolute_value=True).then_inc(setup.sem, 1)
            dve.wait_ge(sums_spread.sem, 1)
            for i, sign in enumerate((0.5, -0.5)):
                nc.vector.tensor_scalar(threshold[:, :, i], PS[:, 0, 0:2], sign / (D * FF), sign * 1e-6, ALU.mult,
                                        ALU.add).then_inc(setup.sem, 1)
            dve.wait_ge(setup.sem, 4)
            for i, weight in enumerate(raw):
                flat = weight.rearrange("p a d -> p (a d)")
                nc.vector.tensor_scalar(above[:, i, :], flat, threshold[:, i, 0:1], None, ALU.is_gt)
                last = nc.vector.tensor_scalar(below[:, i, :], flat, threshold[:, i, 1:2], None, ALU.is_lt)
            last.then_inc(setup.sem, 1)
            dve.wait_ge(setup.sem, 5)
            nc.vector.tensor_tensor(above[:, :, :], above[:, :, :], below[:, :, :], ALU.subtract).then_inc(
                weights_ready.sem, 1)
            with dve.Fori(0, BATCH) as turn:
                link, finish = make_link(dve, s.link, turn)
                x = lambda c: X[:, turn * TILES + c, :]
                if tag == core.first_phase:
                    dve.wait_ge(core.x_first.sem, 16)
                    dve.wait_ge(core.x_rest.sem, 16)
                normalise(nc, dve, link, s, turn, 0, x, lambda c: xn[:, c, :], 1e-5, xn_ready)
                dve.wait_ge(xt_summed.sem, xt_summed.at(turn, 1))
                nc.vector.tensor_copy(xt[:, :], PS[:, 0, :]).then_inc(xt_ready.sem, 1)
                dve.wait_ge(gelu_done.sem, gelu_done.at(turn, TILES))
                norm_statistics(nc, link, s, lambda c: hidden[:, c, :], TILES, FF)
                nc.vector.tensor_scalar(s.var_eps[:, :], s.mean_var[:, :, 1], 1e-5, None, ALU.add).then_inc(
                    s.var_ready.sem, 1)
                dve.wait_ge(s.rstd_ready.sem, s.rstd_ready.at(turn, 2))
                for c in range(TILES):
                    nc.vector.tensor_scalar(hidden_n[:, c, :], hidden[:, c, :], s.mean_var[:, c, 0:1],
                                            s.rstd[:, c:c + 1], ALU.subtract, ALU.mult).then_inc(hidden_ready.sem, 1)
                for f in range(FC):
                    dve.wait_ge(hidden_turned.sem, hidden_turned.at(turn, f + 1))
                    nc.vector.tensor_scalar(hidden_t[:, f, :], PS[:, 4 + f, :], core.ln_w[:, f:f + 1],
                                            core.ln_b[:, f:f + 1], ALU.mult, ALU.add).then_inc(hidden_t_ready.sem, 1)
                dve.wait_ge(down_summed.sem, down_summed.at(turn, 1))
                nc.vector.tensor_copy(y[:, :, :].rearrange("p c d -> p (c d)"), PS[:, DOWN, :]).then_inc(y_read.sem, 1)
                dve.wait_ge(y_read.sem, y_read.at(turn, 1))
                link(normalise(nc, dve, link, s, turn, 2, lambda c: y[:, c, :], lambda c: y_norm[:, c, :], 1e-5))
                for c in range(TILES):
                    last = nc.vector.tensor_tensor(x(c), x(c), y_norm[:, c, :], ALU.add)
                link(last)
                finish()

        @block.scalar
        def _(act):
            act.wait_ge(turned_w.sem, 1)
            nc.scalar.activation(w_up[:, :], PS[:, 1, :], ACT.Copy)
            nc.scalar.activation(w_down[:, :, :].rearrange("p a d -> p (a d)"), PS[:, 2, :], ACT.Copy).then_inc(
                weights_ready.sem, 1)
            with act.Fori(0, BATCH) as turn:
                for c in range(TILES):
                    act.wait_ge(up_summed.sem, up_summed.at(turn, c + 1))
                    nc.scalar.activation(hidden[:, c, :], PS[:, c, :], ACT.Gelu).then_inc(gelu_done.sem, 1)

        @block.tensor
        def _(pe):
            pe.wait_ge(core.constants_ready.sem, core.constants_ready.per_turn)
            pe.wait_ge(setup.sem, 2)
            nc.tensor.matmul(PS[:, 0, 0:2], core.ones[:, :], row_sums[:, :], start=True, stop=True).then_inc(
                sums_spread.sem, 1)
            pe.wait_ge(weights_ready.sem, 1)
            for i in range(2):
                for a in range(FC):
                    last = nc.tensor.transpose(PS[:, 1 + i, a * P:(a + 1) * P], above[:, i, a * P:(a + 1) * P],
                                               ident[:, :])
            last.then_inc(turned_w.sem, 1)
            pe.wait_ge(weights_ready.sem, 2)
            with pe.Fori(0, BATCH) as turn:
                for c in range(TILES):
                    pe.wait_ge(xn_ready.sem, xn_ready.at(turn, c + 1))
                    last = nc.tensor.transpose(PS[:, 0, c * P:(c + 1) * P], xn[:, c, :], ident[:, :])
                last.then_inc(xt_summed.sem, 1)
                pe.wait_ge(xt_ready.sem, xt_ready.at(turn, 1))
                for c in range(TILES):
                    nc.tensor.matmul(PS[:, c, :], xt[:, c * P:(c + 1) * P], w_up[:, :], start=True,
                                     stop=True).then_inc(up_summed.sem, 1)
                pe.wait_ge(hidden_ready.sem, hidden_ready.at(turn, TILES))
                for f in range(FC):
                    for c in range(TILES):
                        last = nc.tensor.transpose(PS[:, 4 + f, c * P:(c + 1) * P], hidden_n[:, c, f * P:(f + 1) * P],
                                                   ident[:, :])
                    last.then_inc(hidden_turned.sem, 1)
                pe.wait_ge(hidden_t_ready.sem, hidden_t_ready.at(turn, FC))
                for c in range(TILES):
                    for f in range(FC):
                        last = nc.tensor.matmul(PS[:, DOWN, c * P:(c + 1) * P], hidden_t[:, f, c * P:(c + 1) * P],
                                                w_down[:, f, :], start=f == 0, stop=f == FC - 1)
                last.then_inc(down_summed.sem, 1)
                pe.wait_ge(y_read.sem, y_read.at(turn, 1))


def expert_ffn(core, name, tag, stored, out):
    nc, X, X1, PS, ident = core.nc, core.X, core.X1, core.PS, core.ident
    with ExitStack() as ctx:
        sb = lambda n, shape, dtype=F32: core.sbuf(f"{name}_{n}", shape, dtype, ctx)
        s = Norms(core, name, tag, 29, 2, ctx)
        sig = lambda n, per=1: core.semaphore(f"{tag}_{n}", per)
        now, xt = sb("now", [P, TILES, D]), sb("xt", [P, SEQ])
        key_terms, keys = sb("key_terms", [P, TILES, D]), sb("keys", [P, TILES])
        whole, rounded = sb("whole", [P, TILES], mybir.dt.int32), sb("rounded", [P, TILES])
        over, floor, chosen = sb("over", [P, TILES]), sb("floor", [P, TILES]), sb("chosen", [P, TILES])
        gate = sb("gate", [P, EXPERTS, TILES])
        hidden = sb("hidden", [P, 4, SEQ])
        experts = sb("experts", [P, TILES, EXPERTS, D])
        total = sb("total", [P, TILES, D])
        normed, scaled = sb("normed", [P, TILES, D]), sb("scaled", [P, TILES, D])
        y_norm = sb("y_norm", [P, TILES, D])
        xt_summed, xt_ready = sig("xt_summed"), sig("xt_ready")
        up_summed, hidden_used = sig("up_summed", EXPERTS * FC), sig("hidden_used", EXPERTS * FC)
        hidden_by = sig("hidden_by_act", EXPERTS * FC // 2), sig("hidden_by_dve", EXPERTS * FC // 2)
        down_read = sig("down_read")
        block = ctx.enter_context(nc.Block())

        @block.sync
        def _(sp):
            with sp.Fori(0, BATCH) as turn:
                sp.wait_ge(s.link.sem, s.link.at(turn, s.link.per_turn))
                sp.dma_start(out[bass.ds(turn, 1)].rearrange("b (c p) d -> p (b c) d", p=P),
                             X[:, bass.ds(turn * TILES, TILES), :]).then_inc(stored.sem, 16)
            sp.wait_ge(stored.sem, 16 * BATCH)

        @block.gpsimd
        def _(pool):
            with pool.Fori(0, BATCH) as turn:
                inverse_roots(nc, pool, s, turn, [0, 1])

        @block.vector
        def _(dve):
            dve.wait_ge(core.weights_e.sem, core.weights_e.per_turn)
            with dve.Fori(0, BATCH) as turn:
                link, finish = make_link(dve, s.link, turn)
                x = lambda c: X[:, turn * TILES + c, :]
                link(nc.vector.tensor_copy(now[:, :, :], X1[:, bass.ds(turn * TILES, TILES), :]))
                x1 = lambda c: now[:, c, :]
                for c in range(TILES):
                    last = nc.vector.tensor_tensor(key_terms[:, c, :], x1(c), core.router_w[:, :], ALU.mult)
                link(last)
                link(nc.vector.tensor_reduce(keys[:, :], key_terms[:, :, :], AX.X, ALU.add))
                link(nc.vector.tensor_scalar(keys[:, :], keys[:, :], core.router_b[:, 0:1], None, ALU.add))

                def take_floor(value):
                    link(nc.vector.tensor_copy(whole[:, :], value))
                    link(nc.vector.tensor_copy(rounded[:, :], whole[:, :]))
                    link(nc.vector.tensor_tensor(over[:, :], rounded[:, :], value, ALU.is_gt))

                take_floor(keys[:, :])
                link(nc.vector.tensor_tensor(floor[:, :], rounded[:, :], over[:, :], ALU.subtract))
                link(nc.vector.tensor_scalar(keys[:, :], floor[:, :], 1.0 / EXPERTS, None, ALU.mult))
                take_floor(keys[:, :])
                link(nc.vector.tensor_tensor(chosen[:, :], rounded[:, :], over[:, :], ALU.subtract))
                link(nc.vector.tensor_scalar(chosen[:, :], chosen[:, :], float(EXPERTS), None, ALU.mult))
                link(nc.vector.tensor_tensor(chosen[:, :], floor[:, :], chosen[:, :], ALU.subtract))
                for e in range(EXPERTS):
                    last = nc.vector.tensor_scalar(gate[:, e, :], chosen[:, :], float(e), None, ALU.is_equal)
                link(last)
                for n in range(1, EXPERTS * FC, 2):
                    dve.wait_ge(up_summed.sem, up_summed.at(turn, n + 1))
                    nc.vector.tensor_scalar(hidden[:, n % 4, :], PS[:, n % 4, :], core.b1[:, n:n + 1], 0.0, ALU.add,
                                            ALU.max).then_inc(hidden_by[1].sem, 1)
                dve.wait_ge(hidden_used.sem, hidden_used.at(turn, EXPERTS * FC))
                for c in range(TILES):
                    last = nc.vector.tensor_tensor(experts[:, c, :, :].rearrange("p e d -> p (e d)"), PS[:, 4 + c, :],
                                                   core.b2[:, :], ALU.add)
                last.then_inc(down_read.sem, 1)
                dve.wait_ge(down_read.sem, down_read.at(turn, 1))
                for e in range(EXPERTS):
                    for c in range(TILES):
                        last = nc.vector.scalar_tensor_tensor(
                            out=total[:, c, :], in0=experts[:, c, e, :], scalar=gate[:, e, c:c + 1],
                            in1=x1(c) if e == 0 else total[:, c, :], op0=ALU.mult, op1=ALU.add)
                    link(last)
                link(normalise(nc, dve, link, s, turn, 0, lambda c: total[:, c, :], lambda c: normed[:, c, :], 1e-5))
                scale_shift(nc, link, scaled, normed, core.ln2_g, core.ln2_b)
                link(normalise(nc, dve, link, s, turn, 1, lambda c: scaled[:, c, :], lambda c: y_norm[:, c, :], 1e-5))
                for c in range(TILES):
                    last = nc.vector.tensor_tensor(x(c), x(c), y_norm[:, c, :], ALU.add)
                link(last)
                finish()

        @block.scalar
        def _(act):
            act.wait_ge(core.weights_e.sem, core.weights_e.per_turn)
            with act.Fori(0, BATCH) as turn:
                act.wait_ge(xt_summed.sem, xt_summed.at(turn, 1))
                nc.scalar.activation(xt[:, :], PS[:, 0, :], ACT.Copy).then_inc(xt_ready.sem, 1)
                for n in range(0, EXPERTS * FC, 2):
                    act.wait_ge(up_summed.sem, up_summed.at(turn, n + 1))
                    nc.scalar.activation(hidden[:, n % 4, :], PS[:, n % 4, :], ACT.Relu,
                                         bias=core.b1[:, n:n + 1]).then_inc(hidden_by[0].sem, 1)

        @block.tensor
        def _(pe):
            pe.wait_ge(core.weights_e.sem, core.weights_e.per_turn)
            with pe.Fori(0, BATCH) as turn:
                pe.wait_ge(s.link.sem, s.link.at(turn, 1))
                for c in range(TILES):
                    last = nc.tensor.transpose(PS[:, 0, c * P:(c + 1) * P], now[:, c, :], ident[:, :])
                last.then_inc(xt_summed.sem, 1)
                pe.wait_ge(xt_ready.sem, xt_ready.at(turn, 1))

                def up(n):
                    nc.tensor.matmul(PS[:, n % 4, :], core.w1[:, n // FC, n % FC * P:(n % FC + 1) * P], xt[:, :],
                                     start=True, stop=True).then_inc(up_summed.sem, 1)

                def down(n):
                    e, f = n // FC, n % FC
                    ready = hidden_by[n % 2]
                    pe.wait_ge(ready.sem, ready.at(turn, n // 2 + 1))
                    for c in range(TILES):
                        last = nc.tensor.matmul(PS[:, 4 + c, e * D:(e + 1) * D], hidden[:, n % 4, c * P:(c + 1) * P],
                                                core.w2[:, e, f, :], start=f == 0, stop=f == FC - 1)
                    last.then_inc(hidden_used.sem, 1)

                up(0)
                up(1)
                for n in range(EXPERTS * FC):
                    if n + 2 < EXPERTS * FC:
                        up(n + 2)
                    down(n)
                pe.wait_ge(down_read.sem, down_read.at(turn, 1))


class Wide:
    NU = 3
    SUBS = 2 * NU
    HELD = 4
    AHEAD = 3
    UNITS = [[(0, 0, 0, 512)], [(1, 128, 0, 384), (3, 384, 384, 128)], [(2, 256, 0, 256)]]

    def __init__(self, core, name, tag, ctx):
        sb = lambda n, shape, dtype=F32: core.sbuf(f"{name}_{n}", shape, dtype, ctx)
        sig = lambda n, per=1: core.semaphore(f"{tag}_{n}", per)
        held, nu = self.HELD, self.NU
        self.norm = NormState(core, sb, sig, "front")
        self.norm1, self.norm2 = NormState(core, sb, sig, "tail1"), NormState(core, sb, sig, "tail2")
        self.pool_carrier = sb("pool_carrier", [P, 1])
        self.xn, self.xt, self.residual = sb("xn", [P, TILES, D]), sb("xt", [P, SEQ]), sb("residual", [P, TILES, D])
        self.v = sb("v", [P, held, TILES, 2, HD64])
        self.part_high, self.part_low = sb("part_high", [P, 2, 2, SEQ], BF16), sb("part_low", [P, 2, 2, SEQ], BF16)
        self.q = sb("q", [P, 2, held, 2, SEQ], BF16)
        self.k = sb("k", [P, 2, held, 2, SEQ], BF16)
        self.neg_max = sb("neg_max", [P, PAIRS, TILES, 2])
        self.max_parts = sb("max_parts", [P, PAIRS, TILES, 2, 2], BF16)
        self.max_t = sb("max_t", [4, PAIRS, SEQ], BF16)
        self.probs = sb("probs", [P, nu * 2, SEQ])
        self.sums = sb("sums", [P, 2, 2, SEQ])
        self.inverse = sb("inverse", [P, SEQ])
        self.y, self.y_norm = sb("y", [P, TILES, D]), sb("y_norm", [P, TILES, D])
        self.cleared, self.ready = sig("cleared"), sig("ready")
        self.link = sig("link")
        self.links = PAIRS + 3 + 2 + 3 + 2 + 2
        self.stage_written, self.stage_read = sig("stage_written"), sig("stage_read")
        self.xn_ready = sig("xn_ready")
        self.high_ready = sig("high_ready", 2 * PAIRS)
        self.placed = [sig(f"placed{p}", 10 * 16) for p in range(PAIRS)]
        self.row_scores, self.row_max = sig("row_scores", PAIRS * TILES * 2), sig("row_max", PAIRS * TILES * 2)
        self.max_ready = sig("max_ready", PAIRS)
        self.max_placed = [sig(f"max_placed{p}", 32) for p in range(PAIRS)]
        self.scores, self.exp_done = sig("scores", PAIRS * nu * 2), sig("exp_done", PAIRS * nu * 2)
        self.added, self.sums_done = sig("added", PAIRS * 4), sig("sums_done", PAIRS)
        self.masked, self.pv_done = sig("masked", PAIRS * nu), sig("pv_done", PAIRS * nu)
        self.inverted, self.out_t_ready = sig("inverted", PAIRS * TILES), sig("out_t_ready", PAIRS)

    NORMS = {(1, 5): "y_norm1", (2, 2): "y_scale", (2, 4): "y_norm2", (3, 0): "y_add", (3, 2): "norm", (3, 5): "xn"}
    AFTER = ["wo", "y_norm1", "y_scale", "y_norm2", "y_add"]
    UNSTAGED = ["y_norm1", "y_scale", "y_norm2", "y_add", "norm", "xn"]

    def before(self):
        steps = [("norm", 0), ("xn", 0), ("xt", 0)]
        for p in range(self.AHEAD):
            steps += [("q", p), ("k", p), ("v", p)]
        return steps + [("max", 0)]

    def beside(self, p, sub, kind):
        names = []
        if sub in (0, 1, 4):
            ahead = p + self.AHEAD
            names.append(({0: "q", 1: "k", 4: "v"}[sub], ahead // PAIRS, ahead % PAIRS))
        if sub == 2:
            names.append(("max", (p + 1) // PAIRS, (p + 1) % PAIRS))
        if (p, sub) == (1, 3):
            names.append(("wo", -1, 0))
        if (p, sub) == (4, 5):
            names.append(("xt", 1, 0))
        if (p, sub) in self.NORMS:
            name = self.NORMS[p, sub]
            names.append((name, -1 if name[0] == "y" else 1, 0))
        return [s for s in names if not (s[1] < 0 and kind == "first") and not (s[1] > 0 and kind == "last")]

    def staged(self, kind):
        if kind == "before":
            steps = self.before()
        elif kind == "after":
            steps = [(name, 0) for name in self.AFTER]
        else:
            steps = [(name, p) for pair in range(PAIRS) for sub in range(self.SUBS)
                     for name, _, p in self.beside(pair, sub, kind)]
        return [name + str(p) for name, p in steps if name not in self.UNSTAGED]

    def stage(self, kind, t):
        count = lambda k: len(self.staged(k))
        base = 0
        if kind in ("mid", "last", "after"):
            base = count("before") + count("first") + (t - 1) * count("mid")
        if kind == "first":
            base = count("before")
        if kind == "after":
            base += count("last") - count("mid")
        return Stage(self.stage_written, self.stage_read, self.staged(kind), base)

    def fills(self, p, sub):
        per_pair = 2 * TILES
        due = lambda s: (p + 2) * per_pair + s * per_pair // self.SUBS
        return range(due(sub), due(sub + 1))


def one_by_one(engine, before, turn, after):
    before()
    turn(0, "first")
    with engine.Fori(0, BATCH - 2) as i:
        turn(i + 1, "mid")
    turn(BATCH - 1, "last")
    after()


def wide_attention(core, name, tag):
    nc, X, PS, ident, ident_b = core.nc, core.X, core.PS, core.ident, core.ident_b
    PB = PS.bitcast(BF16)
    w_q, w_k, w_v = core.wide_w
    scale = float(HD64) ** -0.5
    ST, OUT, SUMS, STAGE = 2, 4, 6, 7
    FILLS = PAIRS * TILES * 2
    out_t = core.X1[:, :, :].rearrange("p (a c) d -> p a (c d)", a=PAIRS)

    with ExitStack() as ctx:
        s = Wide(core, name, tag, ctx)
        units, nu, held = s.UNITS, s.NU, s.HELD
        block = ctx.enter_context(nc.Block())

        @block.sync
        def _(sp):
            halves = slice(0, HD64), slice(HD64, P)

            def place(stage, p):
                at = p % held
                stage.after(sp, f"q{p}")
                for a in range(2):
                    own, other = halves[a], halves[1 - a]
                    high, low = s.part_high[own, 0, p % 2, :], s.part_low[own, 0, p % 2, :]
                    sp.dma_start(s.q[own, :, at, a, :], high.unsqueeze(1).to_broadcast([HD64, 2, SEQ])).then_inc(
                        s.placed[p].sem, 16)
                    sp.dma_start(s.q[other, 0, at, a, :], low).then_inc(s.placed[p].sem, 16)
                stage.after(sp, f"k{p}")
                for a in range(2):
                    own, other = halves[a], halves[1 - a]
                    high, low = s.part_high[own, 1, p % 2, :], s.part_low[own, 1, p % 2, :]
                    sp.dma_start(s.k[own, 0, at, a, :], high).then_inc(s.placed[p].sem, 16)
                    sp.dma_start(s.k[other, 0, at, a, :], high).then_inc(s.placed[p].sem, 16)
                    sp.dma_start(s.k[own, 1, at, a, :], low).then_inc(s.placed[p].sem, 16)

            def step(stage, name, t, p):
                if name == "k":
                    place(stage, p)
                elif name == "max":
                    stage.after(sp, f"max{p}")
                    at = p % held
                    sp.dma_start(s.q[HD64:HD64 + 2, 1, at, 0, :], s.max_t[0:2, p, :]).then_inc(s.max_placed[p].sem, 16)
                    sp.dma_start(s.q[0:2, 1, at, 1, :], s.max_t[2:4, p, :]).then_inc(s.max_placed[p].sem, 16)

            def before():
                stage = s.stage("before", 0)
                sp.wait_ge(s.ready.sem, 1)
                for name, p in s.before():
                    step(stage, name, 0, p)

            def turn(t, kind):
                stage = s.stage(kind, t)
                for pair in range(PAIRS):
                    for sub in range(s.SUBS):
                        for name, ahead, p in s.beside(pair, sub, kind):
                            step(stage, name, t + ahead, p)

            one_by_one(sp, before, turn, lambda: None)

        @block.gpsimd
        def _(pool):
            nc.gpsimd.memset(s.q[:, 1, :, :, :], 0.0)
            nc.gpsimd.memset(s.k[:, 1, :, :, :], 0.0).then_inc(s.cleared.sem, 1)
            pool.wait_ge(s.cleared.sem, 1)
            nc.gpsimd.memset(s.k[HD64:HD64 + 2, 1, :, 0, :], 1.0).then_inc(s.cleared.sem, 1)
            pool.wait_ge(s.cleared.sem, 2)
            nc.gpsimd.memset(s.k[0:2, 1, :, 1, :], 1.0).then_inc(s.ready.sem, 1)
            pool.wait_ge(s.ready.sem, 1)

            def add_up(t, p, u, kind):
                total, probs = s.sums[:, p % 2, :, :], s.probs
                added = [(0, P)] if u == 0 else [(P, SEQ), (3 * P, SEQ)] if u == 1 else [(2 * P, SEQ)]
                sources = {0: [(0, 0)], 1: [(2, 0), (2, 3 * P)], 2: [(4, 0)]}[u]
                for k, ((first, end), (slot, at)) in enumerate(zip(added, sources)):
                    if u == 0 and not (kind == "first" and p < 2):
                        pool.wait_ge(s.sums_done.sem, s.sums_done.at(t, p - 1))
                    if u == 0:
                        nc.gpsimd.tensor_tensor(s.pool_carrier[:, :], core.minus_half[:, 0:1],
                                                core.minus_half[:, 0:1], ALU.add)
                        last = nc.gpsimd.affine_select(out=total[:, :, 0:P], in_=probs[:, 0:2, 0:P],
                                                       compare_op=ALU.is_ge, fill=0.0, base=0,
                                                       pattern=[[0, 2], [1, P]], channel_multiplier=-1)
                    else:
                        before = probs[:, 0:2, P:SEQ] if (u, k) == (1, 0) else total[:, :, first:end]
                        if (u, k) != (1, 0):
                            pool.wait_ge(s.added.sem, s.added.at(t, 4 * p + u + k))
                        last = nc.gpsimd.tensor_tensor(total[:, :, first:end], before,
                                                       probs[:, slot:slot + 2, at:at + end - first], ALU.add)
                    last.then_inc(s.added.sem, 1)

            def turn(t, kind):
                for n in range(PAIRS * nu):
                    p, u = n // nu, n % nu
                    first = n == 0 and kind == "first"
                    pool.wait_ge(s.exp_done.sem, s.exp_done.at(t, 2 * (n + 1)))
                    if not first:
                        pool.wait_ge(s.added.sem, s.added.at(t, (0, 1, 3)[u] + 4 * p))
                    nc.gpsimd.tensor_tensor(s.pool_carrier[:, :], core.minus_half[:, 0:1], core.minus_half[:, 0:1],
                                            ALU.add)
                    heads = slice(2 * u, 2 * u + 2)
                    for _, _, at, _ in units[u]:
                        square = s.probs[:, heads, at:at + P]
                        last = nc.gpsimd.affine_select(out=square, in_=square, compare_op=ALU.is_ge, fill=0.0,
                                                       base=0, pattern=[[0, 2], [1, P]], channel_multiplier=-1)
                    last.then_inc(s.masked.sem, 1)
                    pool.wait_ge(s.masked.sem, s.masked.at(t, n + 1))
                    add_up(t, p, u, kind)
                    for sub in (n % nu * 2, n % nu * 2 + 1):
                        for name, ahead, _ in s.beside(n // nu, sub, kind):
                            if name in ("norm", "y_norm1", "y_norm2"):
                                norm = {"norm": s.norm, "y_norm1": s.norm1, "y_norm2": s.norm2}[name]
                                norm.power(nc, pool, t + ahead)

            def after():
                s.norm1.power(nc, pool, BATCH - 1)
                s.norm2.power(nc, pool, BATCH - 1)

            one_by_one(pool, lambda: s.norm.power(nc, pool, 0), turn, after)

        @block.vector
        def _(dve):
            dve.wait_ge(core.weights_c.sem, core.weights_c.per_turn)
            counted = [0]

            def row_max(chain, t, n):
                p, c, a = n // (2 * TILES), n // 2 % TILES, n % 2
                dve.wait_ge(s.row_scores.sem, s.row_scores.at(t, n + 1))
                nc.vector.tensor_reduce(s.neg_max[:, p, c, a:a + 1], PS[:, n % 2, 0:P * (c + 1)], AX.X, ALU.max,
                                        negate=True).then_inc(s.row_max.sem, 1)
                if n % (2 * TILES) == 2 * TILES - 1:
                    dve.wait_ge(s.row_max.sem, s.row_max.at(t, n + 1))
                    chain.link(nc.vector.tensor_copy(s.max_parts[:, p, :, :, 0], s.neg_max[:, p, :, :]))
                    nc.vector.tensor_tensor(s.max_parts[:, p, :, :, 1], s.neg_max[:, p, :, :],
                                            s.max_parts[:, p, :, :, 0], ALU.subtract).then_inc(s.max_ready.sem, 1)

            def invert(t, p, c):
                first = isinstance(t, int) and t * PAIRS + p == 0
                if c == 0:
                    dve.wait_ge(s.sums_done.sem, s.sums_done.at(t, p + 1))
                    if not first:
                        dve.wait_ge(s.out_t_ready.sem, s.out_t_ready.at(t, p))
                nc.vector.reciprocal(s.inverse[:, c * P:(c + 1) * P], PS[:, SUMS, c * P:(c + 1) * P]).then_inc(
                    s.inverted.sem, 1)

            def keep_products(t, p):
                dve.wait_ge(s.inverted.sem, s.inverted.at(t, TILES * (p + 1)))
                nc.vector.tensor_tensor(out_t[:, p, :], PS[:, OUT + p % 2, :], s.inverse[:, :], ALU.mult).then_inc(
                    s.out_t_ready.sem, 1)

            def finish_pair(pair, sub, t, kind):
                back, c = {3: (1, 0), 4: (1, 1), 5: (1, 2), 0: (2, 3), 1: (2, TILES)}.get(sub, (0, 0))
                if back and (pair >= back or kind != "first"):
                    t_of, p = (t, pair - back) if pair >= back else (t - 1, pair - back + PAIRS)
                    if c < TILES:
                        invert(t_of, p, c)
                    else:
                        keep_products(t_of, p)

            def step(chain, stage, name, t, p):
                x = lambda c: X[:, t * TILES + c, :]
                link = chain.link
                if name == "norm":
                    if not (isinstance(t, int) and t == 0):
                        link(nc.vector.tensor_copy(s.residual[:, :, :], s.xn[:, :, :]))
                    s.norm.statistics(nc, link, x, 1e-5)
                elif name == "xn":
                    s.norm.apply(nc, dve, t, x, lambda c: s.xn[:, c, :]).then_inc(s.xn_ready.sem, 1)
                elif name in ("q", "k"):
                    n = 2 * p + (name == "k")
                    dve.wait_ge(s.high_ready.sem, s.high_ready.at(t, n + 1))
                    nc.vector.tensor_tensor(s.part_low[:, n % 2, p % 2, :], PS[:, STAGE, :],
                                            s.part_high[:, n % 2, p % 2, :], ALU.subtract).then_inc(
                                                s.stage_read.sem, 1)
                elif name == "wo":
                    stage.drain(dve, "wo0")
                    residual = s.xn if isinstance(t, int) and t == BATCH - 1 else s.residual
                    nc.vector.tensor_tensor(s.y[:, :, :], PS[:, STAGE, :].rearrange("p (c d) -> p c d", d=D),
                                            residual[:, :, :], ALU.add).then_inc(s.stage_read.sem, 1)
                elif name == "y_norm1":
                    stage.after(dve, "wo0")
                    s.norm1.statistics(nc, link, lambda c: s.y[:, c, :], 1e-3)
                elif name == "y_scale":
                    link(s.norm1.apply(nc, dve, t, lambda c: s.y[:, c, :], lambda c: s.y_norm[:, c, :]))
                    scale_shift(nc, link, s.y, s.y_norm, core.wide_gamma, core.wide_beta)
                elif name == "y_norm2":
                    s.norm2.statistics(nc, link, lambda c: s.y[:, c, :], 1e-5)
                elif name == "y_add":
                    link(s.norm2.apply(nc, dve, t, lambda c: s.y[:, c, :], lambda c: s.y_norm[:, c, :]))
                    for c in range(TILES):
                        last = nc.vector.tensor_tensor(x(c), x(c), s.y_norm[:, c, :], ALU.add)
                    link(last)

            def before():
                chain = Chain(dve, s.link, 0)
                stage = s.stage("before", 0)
                if tag == core.first_phase:
                    dve.wait_ge(core.x_first.sem, 16)
                    dve.wait_ge(core.x_rest.sem, 16)
                for name, p in s.before()[:-1]:
                    step(chain, stage, name, 0, p)
                for n in range(2 * 2 * TILES):
                    row_max(chain, 0, n)
                counted[0] = chain.count

            def turn(t, kind):
                chain = Chain(dve, s.link, counted[0] + (0 if kind == "first" else (t - 1) * s.links))
                stage = s.stage(kind, t)
                for pair in range(PAIRS):
                    for sub in range(s.SUBS):
                        for n in s.fills(pair, sub):
                            if n < FILLS:
                                row_max(chain, t, n)
                            elif kind != "last":
                                row_max(chain, t + 1, n - FILLS)
                        finish_pair(pair, sub, t, kind)
                        for name, ahead, p in s.beside(pair, sub, kind):
                            step(chain, stage, name, t + ahead, p)
                if kind == "first":
                    counted[0] += chain.count
                elif kind == "mid":
                    assert chain.count == s.links, (chain.count, s.links)
                else:
                    counted[0] += (BATCH - 2) * s.links + chain.count

            def after():
                chain = Chain(dve, s.link, counted[0])
                invert(BATCH - 1, PAIRS - 2, TILES - 1)
                keep_products(BATCH - 1, PAIRS - 2)
                for c in range(TILES):
                    invert(BATCH - 1, PAIRS - 1, c)
                keep_products(BATCH - 1, PAIRS - 1)
                for name in s.AFTER:
                    step(chain, s.stage("after", BATCH), name, BATCH - 1, 0)

            one_by_one(dve, before, turn, after)

        @block.scalar
        def _(act):
            act.wait_ge(s.ready.sem, 1)

            def step(stage, name, t, p):
                early = isinstance(t, int)
                if name == "xt":
                    stage.drain(act, "xt0")
                    nc.scalar.activation(s.xt[:, :], PS[:, STAGE, :], ACT.Copy).then_inc(s.stage_read.sem, 1)
                elif name in ("q", "k"):
                    n = 2 * p + (name == "k")
                    stage.drain(act, name + str(p))
                    if p >= 2:
                        act.wait_ge(s.placed[p - 2].sem, s.placed[p - 2].at(t, 10 * 16))
                    elif not (early and t == 0):
                        act.wait_ge(s.placed[p - 2].sem, s.placed[p - 2].at(t, 0))
                    nc.scalar.activation(s.part_high[:, n % 2, p % 2, :], PS[:, STAGE, :], ACT.Copy).then_inc(
                        s.high_ready.sem, 1)
                elif name == "v":
                    stage.drain(act, f"v{p}")
                    if not (early and t * PAIRS + p < held):
                        act.wait_ge(s.pv_done.sem, s.pv_done.at(t, nu * (p - held + 1)))
                    nc.scalar.activation(s.v[:, p % held, :, :, :].rearrange("p c a e -> p (c a e)"),
                                         PS[:, STAGE, :], ACT.Copy).then_inc(s.stage_read.sem, 1)
                elif name == "max":
                    stage.drain(act, f"max{p}")
                    nc.scalar.activation(s.max_t[:, p, :], PB[0:4, STAGE, 0:SEQ], ACT.Copy).then_inc(
                        s.stage_read.sem, 1)

            def before():
                stage = s.stage("before", 0)
                for name, p in s.before():
                    step(stage, name, 0, p)

            def turn(t, kind):
                stage = s.stage(kind, t)
                for pair in range(PAIRS):
                    for sub in range(s.SUBS):
                        n, i = pair * nu + sub // 2, pair * s.SUBS + sub
                        width = sum(w for _, _, _, w in units[n % nu])
                        if n >= nu or kind != "first":
                            act.wait_ge(s.pv_done.sem, s.pv_done.at(t, n - nu + 1))
                            act.wait_ge(s.added.sem, s.added.at(t, 4 * (pair - 1) + (3, 3, 4)[sub // 2]))
                        act.wait_ge(s.scores.sem, s.scores.at(t, i + 1))
                        nc.scalar.activation(s.probs[:, sub, 0:width], PS[:, ST + i % 2, 0:width], ACT.Exp,
                                             scale=scale).then_inc(s.exp_done.sem, 1)
                        for name, ahead, p in s.beside(pair, sub, kind):
                            step(stage, name, t + ahead, p)

            one_by_one(act, before, turn, lambda: None)

        @block.tensor
        def _(pe):
            pe.wait_ge(s.ready.sem, 1)
            pe.wait_ge(core.constants_ready.sem, core.constants_ready.per_turn)
            pe.wait_ge(core.weights_c.sem, core.weights_c.per_turn)

            def row_scores(t, n, first):
                p, c, a = n // (2 * TILES), n // 2 % TILES, n % 2
                if n % (2 * TILES) == 0:
                    pe.wait_ge(s.placed[p].sem, s.placed[p].at(t, 10 * 16))
                if n >= 2 or not first:
                    pe.wait_ge(s.row_max.sem, s.row_max.at(t, n - 1))
                keys, at = P * (c + 1), p % held
                nc.tensor.matmul(PS[:, n % 2, 0:keys], s.q[:, 0, at, a, c * P:(c + 1) * P], s.k[:, 0, at, a, 0:keys],
                                 start=True, stop=False)
                nc.tensor.matmul(PS[:, n % 2, keys - P:keys], ident_b[:, :], core.mask[:, :], start=False,
                                 stop=True).then_inc(s.row_scores.sem, 1)

            def products(t, n):
                p, u = n // nu, n % nu
                start = isinstance(t, int) and t == 0
                pe.wait_ge(s.masked.sem, s.masked.at(t, n + 1))
                if u == 0 and not (start and p < 2):
                    pe.wait_ge(s.out_t_ready.sem, s.out_t_ready.at(t, p - 1))
                for i, (k, q0, at, width) in enumerate(units[u]):
                    for a in range(2):
                        last = nc.tensor.matmul(PS[HD64 * a:HD64 * (a + 1), OUT + p % 2, q0:q0 + width],
                                                s.v[:, p % held, k, a, :], s.probs[:, u * 2 + a, at:at + width],
                                                start=u == 0 and i == 0, stop=u == nu - 1 and i == len(units[u]) - 1)
                last.then_inc(s.pv_done.sem, 1)

            def sum_rows(t, p):
                pe.wait_ge(s.added.sem, s.added.at(t, 4 * (p + 1)))
                if not (isinstance(t, int) and t == 0 and p == 0):
                    pe.wait_ge(s.inverted.sem, s.inverted.at(t, TILES * p))
                for a in range(2):
                    last = nc.tensor.matmul(PS[HD64 * a:HD64 * (a + 1), SUMS, :], core.ones[:, 0:HD64],
                                            s.sums[:, p % 2, a, :], start=True, stop=True)
                last.then_inc(s.sums_done.sem, 1)

            def step(stage, name, t, p):
                if name in s.UNSTAGED:
                    return
                stage.fill(pe, name + str(p))
                if name == "xt":
                    pe.wait_ge(s.xn_ready.sem, s.xn_ready.at(t, 1))
                    for c in range(TILES):
                        last = nc.tensor.transpose(PS[:, STAGE, c * P:(c + 1) * P], s.xn[:, c, :], ident[:, :])
                elif name in ("q", "k"):
                    weight = w_q if name == "q" else w_k
                    last = nc.tensor.matmul(PS[:, STAGE, :], weight[:, 2 * p:2 * p + 2, :].rearrange("p h e -> p (h e)"),
                                            s.xt[:, :], start=True, stop=True)
                elif name == "v":
                    for c in range(TILES):
                        last = nc.tensor.matmul(PS[:, STAGE, c * P:(c + 1) * P], s.xt[:, c * P:(c + 1) * P],
                                                w_v[:, 2 * p:2 * p + 2, :].rearrange("p h e -> p (h e)"), start=True,
                                                stop=True)
                elif name == "max":
                    pe.wait_ge(s.max_ready.sem, s.max_ready.at(t, p + 1))
                    for c in range(TILES):
                        last = nc.tensor.transpose(PB[0:4, STAGE, c * P:(c + 1) * P],
                                                   s.max_parts[:, p, c, :, :].rearrange("p a r -> p (a r)"),
                                                   ident_b[:, :])
                elif name == "wo":
                    pe.wait_ge(s.out_t_ready.sem, s.out_t_ready.at(t, PAIRS))
                    for c in range(TILES):
                        for pair in range(PAIRS):
                            last = nc.tensor.matmul(PS[:, STAGE, c * P:(c + 1) * P],
                                                    out_t[:, pair, c * P:(c + 1) * P], core.wide_wo[:, pair, :],
                                                    start=pair == 0, stop=pair == PAIRS - 1)
                last.then_inc(s.stage_written.sem, 1)

            def before():
                stage = s.stage("before", 0)
                for name, p in s.before()[:-1]:
                    step(stage, name, 0, p)
                for n in range(2 * 2 * TILES):
                    row_scores(0, n, True)
                step(stage, "max", 0, 0)

            def turn(t, kind):
                stage = s.stage(kind, t)
                for pair in range(PAIRS):
                    pe.wait_ge(s.max_placed[pair].sem, s.max_placed[pair].at(t, 32))
                    for sub in range(s.SUBS):
                        n, a, i = pair * nu + sub // 2, sub % 2, pair * s.SUBS + sub
                        if i >= 2 or kind != "first":
                            pe.wait_ge(s.exp_done.sem, s.exp_done.at(t, i - 1))
                        for k, q0, at, width in units[n % nu]:
                            bank = PS[:, ST + i % 2, at:at + width]
                            for half in range(2):
                                last = nc.tensor.matmul(bank, s.k[:, half, pair % held, a, k * P:(k + 1) * P],
                                                        s.q[:, half, pair % held, a, q0:q0 + width],
                                                        start=half == 0, stop=half == 1)
                        last.then_inc(s.scores.sem, 1)
                        for m in s.fills(pair, sub):
                            if m < FILLS:
                                row_scores(t, m, False)
                            elif kind != "last":
                                row_scores(t + 1, m - FILLS, False)
                        if sub == 2 and (pair or kind != "first"):
                            sum_rows(t if pair else t - 1, (pair - 1) % PAIRS)
                        for name, ahead, p in s.beside(pair, sub, kind):
                            step(stage, name, t + ahead, p)
                        if a:
                            if n:
                                products(t, n - 1)
                            elif kind != "first":
                                products(t - 1, PAIRS * nu - 1)

            def after():
                products(BATCH - 1, PAIRS * nu - 1)
                sum_rows(BATCH - 1, PAIRS - 1)
                step(s.stage("after", BATCH), "wo", BATCH - 1, 0)

            one_by_one(pe, before, turn, after)


def broadcast_rows(vector):
    return vector.rearrange("(a n) -> a n", a=1).to_broadcast([P, vector.shape[0]])


class Net(Core):

    def __init__(self, nc, ctx, w, x_dram):
        super().__init__(nc, ctx)
        self.w, self.x_dram = w, x_dram
        self.PS = ctx.enter_context(nc.psum_tensor("banks", [P, 8, 512], F32))[:, :, :]
        self.X1 = self.sbuf("tokens1", [P, ALL_TILES, D])
        self.X = self.sbuf("tokens", [P, BATCH * TILES, D])
        self.ident = self.sbuf("ident", [P, P])
        self.ident_b = self.sbuf("ident_b", [P, P], BF16)
        self.mask = self.sbuf("mask", [P, P], BF16)
        self.minus_half = self.sbuf("minus_half", [P, TILES])
        self.constants_made = self.semaphore("constants_made")
        self.constants_ready = self.semaphore("constants_ready", 4)
        self.x_first = self.semaphore("x_first")
        self.x_rest = self.semaphore("x_rest")
        self.loads = []

        def load(signal, target, source):
            self.loads.append((target, source, signal))
            signal.per_turn += 16

        self.weights_a, self.biases_a = self.semaphore("weights_a", 0), self.semaphore("biases_a", 0)
        self.weights_b, self.weights_c = self.semaphore("weights_b", 0), self.semaphore("weights_c", 0)
        self.weights_d, self.biases_d = self.semaphore("weights_d", 0), self.semaphore("biases_d", 0)
        self.weights_e = self.semaphore("weights_e", 0)

        def narrow(tag, prefix, names, weights, biases):
            w_qkv = self.sbuf(f"w_qkv_{tag}", [P, 3 * D])
            b_qkv = self.sbuf(f"b_qkv_{tag}", [P, 3 * D])
            w_o, b_o = self.sbuf(f"w_o_{tag}", [P, D]), self.sbuf(f"b_o_{tag}", [P, D])
            for i, letter in enumerate("qkv"):
                load(weights, w_qkv[:, i * D:(i + 1) * D], w[f"{prefix}_{names[0]}{letter}"])
            load(weights, w_o[:, :], w[f"{prefix}_{names[0]}o"])
            for i, letter in enumerate("qkv"):
                load(biases, b_qkv[:, i * D:(i + 1) * D], broadcast_rows(w[f"{prefix}_b{letter}"]))
            load(biases, b_o[:, :], broadcast_rows(w[f"{prefix}_bo"]))
            return w_qkv, b_qkv, w_o, b_o

        self.ones = self.sbuf("ones", [P, P])
        self.narrow_a = narrow("a", "L0_attn", "w", self.weights_a, self.biases_a)
        self.w_fc = self.sbuf("w_fc", [P, FC, D])
        load(self.weights_b, self.w_fc[:, :, :], w["L0_ffn_W_fc"].rearrange("(a p) d -> p a d", p=P))
        self.w_proj = self.sbuf("w_proj", [P, FC, P])
        load(self.weights_b, self.w_proj[:, :, :], w["L0_ffn_W_proj"].rearrange("d (a p) -> d a p", p=P))
        self.ln_w, self.ln_b = self.sbuf("ln_w", [P, FC]), self.sbuf("ln_b", [P, FC])
        for tile, key in ((self.ln_w, "L0_ffn_ln_w"), (self.ln_b, "L0_ffn_ln_b")):
            load(self.weights_b, tile[:, :], w[key].rearrange("(a p) -> p a", p=P))
        self.wide_w = []
        for letter in "qkv":
            self.wide_w.append(self.sbuf(f"wide_w{letter}", [P, HEADS, HD64]))
            load(self.weights_c, self.wide_w[-1][:, :, :], w[f"L1_attn_W{letter}"].rearrange("h d e -> d h e"))
        self.wide_wo = self.sbuf("wide_wo", [P, PAIRS, D])
        load(self.weights_c, self.wide_wo[:, :, :], w["L1_attn_Wo"].rearrange("(a p) d -> p a d", p=P))
        self.wide_gamma, self.wide_beta = self.sbuf("wide_gamma", [P, D]), self.sbuf("wide_beta", [P, D])
        load(self.weights_c, self.wide_gamma[:, :], broadcast_rows(w["L1_attn_gamma"]))
        load(self.weights_c, self.wide_beta[:, :], broadcast_rows(w["L1_attn_beta"]))
        self.narrow_d = narrow("d", "L1_ffn", "W", self.weights_d, self.biases_d)
        self.ln1_g, self.ln1_b = self.sbuf("ln1_g", [P, D]), self.sbuf("ln1_b", [P, D])
        load(self.biases_d, self.ln1_g[:, :], broadcast_rows(w["L1_ffn_ln1_g"]))
        load(self.biases_d, self.ln1_b[:, :], broadcast_rows(w["L1_ffn_ln1_b"]))
        self.w1 = self.sbuf("w1", [P, EXPERTS, FF])
        load(self.weights_e, self.w1[:, :, :], w["L1_ffn_W1"].rearrange("e d f -> d e f"))
        self.w2 = self.sbuf("w2", [P, EXPERTS, FC, D])
        load(self.weights_e, self.w2[:, :, :, :], w["L1_ffn_W2"].rearrange("e (a p) d -> p e a d", p=P))
        self.b1 = self.sbuf("b1", [P, EXPERTS * FC])
        load(self.weights_e, self.b1[:, :], w["L1_ffn_b1"].rearrange("e (a p) -> p (e a)", p=P))
        self.b2 = self.sbuf("b2", [P, EXPERTS * D])
        load(self.weights_e, self.b2[:, :], broadcast_rows(w["L1_ffn_b2"].rearrange("e d -> (e d)")))
        self.router_w, self.router_b = self.sbuf("router_w", [P, D]), self.sbuf("router_b", [P, 1])
        load(self.weights_e, self.router_w[:, :], broadcast_rows(w["L1_ffn_router_w"].rearrange("d o -> (d o)")))
        load(self.weights_e, self.router_b[:, :], broadcast_rows(w["L1_ffn_router_b"]))
        self.ln2_g, self.ln2_b = self.sbuf("ln2_g", [P, D]), self.sbuf("ln2_b", [P, D])
        load(self.weights_e, self.ln2_g[:, :], broadcast_rows(w["L1_ffn_ln2_g"]))
        load(self.weights_e, self.ln2_b[:, :], broadcast_rows(w["L1_ffn_ln2_b"]))

    def start_loads(self, sp):
        x = self.x_dram.rearrange("b (c p) d -> p b c d", p=P)
        tokens = self.X[:, :, :].rearrange("p (b c) d -> p b c d", c=TILES)
        sp.dma_start(tokens[:, 0], x[:, 0]).then_inc(self.x_first.sem, 16)
        for n, (target, source, signal) in enumerate(self.loads):
            with self.nc.allow_non_contiguous_dma(reason="short vectors laid out by feature"):
                sp.dma_start(target, source).then_inc(signal.sem, 16)
            if n == 7:
                sp.dma_start(tokens[:, 1:].rearrange("p b c d -> p (b c) d"),
                             x[:, 1:].rearrange("p b c d -> p (b c) d")).then_inc(self.x_rest.sem, 16)

    def make_constants(self, pool):
        nc = self.nc
        nc.gpsimd.memset(self.ident[:, :], 0.0)
        nc.gpsimd.memset(self.ident_b[:, :], 0.0)
        nc.gpsimd.memset(self.mask[:, :], 0.0).then_inc(self.constants_made.sem, 1)
        pool.wait_ge(self.constants_made.sem, 1)
        for tile in (self.ident, self.ident_b):
            nc.gpsimd.affine_select(out=tile[:, :], in_=tile[:, :], compare_op=ALU.not_equal, fill=1.0, base=0,
                                    pattern=[[-1, P]], channel_multiplier=1).then_inc(self.constants_ready.sem, 1)
        nc.gpsimd.affine_select(out=self.mask[:, :], in_=self.mask[:, :], compare_op=ALU.is_ge, fill=MASKED, base=0,
                                pattern=[[-1, P]], channel_multiplier=1).then_inc(self.constants_ready.sem, 1)
        nc.gpsimd.memset(self.ones[:, :], 1.0)
        nc.gpsimd.memset(self.minus_half[:, :], -0.5).then_inc(self.constants_ready.sem, 1)


def build(nc, w, x_dram, out, phases="abcde"):
    with ExitStack() as ctx:
        core = Net(nc, ctx, w, x_dram)
        core.first_phase = phases[0]
        stored = core.semaphore("stored")
        with nc.Block() as block:
            @block.sync
            def _(sp):
                core.start_loads(sp)

            @block.gpsimd
            def _(pool):
                core.make_constants(pool)

        if "a" in phases:
            narrow_attention(core, "first", "a", True, *core.narrow_a, (core.weights_a, core.biases_a), add_normalised)
        if "b" in phases:
            gelu_ffn(core, "rounded", "b")
        if "c" in phases:
            wide_attention(core, "wide", "c")
        if "d" in phases:
            narrow_attention(core, "last", "d", False, *core.narrow_d, (core.weights_d, core.biases_d),
                             keep_norm1(core))
            expert_ffn(core, "experts", "e", stored, out)
        else:
            with nc.Block() as block:
                @block.sync
                def _(sp):
                    sp.dma_start(out.rearrange("b (c p) d -> p (b c) d", p=P), core.X[:, 0:4*BATCH, :]).then_inc(stored.sem, 16)
                    sp.wait_ge(stored.sem, 16)


def kernel(**inputs):
    import numpy as _np
    import concourse.bacc as _bacc
    from concourse import mybir as _mybir
    from concourse.bass_utils import run_bass_kernel_spmd as _run

    nc = _bacc.Bacc("TRN2", target_bir_lowering=False, num_devices=1)
    arrays, handles = {}, {}
    for name, value in inputs.items():
        a = _np.ascontiguousarray(value)
        arrays[f"in_{name}"] = a
        handles[name] = nc.dram_tensor(f"in_{name}", a.shape, _mybir.dt.from_np(a.dtype), kind="ExternalInput").ap()
    out = nc.dram_tensor("out", (BATCH, SEQ, D), F32, kind="ExternalOutput").ap()
    build(nc, handles, handles["L0_attn_x"], out)
    r = _run(nc, [arrays], core_ids=[0])
    return r.results[0]["out"]
```

```python
from contextlib import ExitStack

import concourse.bass as bass
from concourse import mybir

F32 = mybir.dt.float32
BF16 = mybir.dt.bfloat16
ALU = mybir.AluOpType
ACT = mybir.ActivationFunctionType
AX = mybir.AxisListType

P = 128
BATCH, SEQ, D = 8, 512, 128
TILES = SEQ // P
ALL_TILES = BATCH * TILES
HEADS = 16
HD8 = D // HEADS
QUAD = 32
GROUPS = HEADS * QUAD // P
GH = HEADS // GROUPS
HD64 = 64
PAIRS = HEADS // 2
FF = 512
FC = FF // P
EXPERTS = 4
KEPT = 2
MASKED = -3.0e38


class Signal:

    def __init__(self, sem, per_turn):
        self.sem, self.per_turn = sem, per_turn

    def at(self, turn, k):
        return turn * self.per_turn + k


class Core:

    def __init__(self, nc, ctx):
        self.nc, self.ctx = nc, ctx

    def sbuf(self, name, shape, dtype=F32, ctx=None):
        return (ctx or self.ctx).enter_context(self.nc.sbuf_tensor(name, shape, dtype))

    def semaphore(self, name, per_turn=1):
        return Signal(self.ctx.enter_context(self.nc.semaphore(name)), per_turn)


def norm_statistics(nc, link, s, source, tiles, width):
    for c in range(tiles):
        last = nc.vector.bn_stats(s.stats[:, c, :], source(c))
    link(last)
    nc.vector.tensor_copy(s.carrier[:, :], s.stats[:, 0, 0:1])
    for c in range(tiles):
        last = nc.vector.bn_aggr(s.mean_var[:, c, :], s.stats[:, c, :])
    link(last)


class Stage:

    def __init__(self, written, read, names, base):
        self.written, self.read, self.names, self.base = written, read, names, base

    def fill(self, pe, name):
        k = self.names.index(name)
        if not (isinstance(self.base, int) and self.base + k == 0):
            pe.wait_ge(self.read.sem, self.base + k)

    def drain(self, engine, name):
        engine.wait_ge(self.written.sem, self.base + self.names.index(name) + 1)

    def after(self, engine, name):
        engine.wait_ge(self.read.sem, self.base + self.names.index(name) + 1)


class Chain:

    def __init__(self, dve, signal, base):
        self.dve, self.raised, self.base, self.count = dve, signal, base, 0

    def link(self, instruction):
        self.count += 1
        instruction.then_inc(self.raised.sem, 1)
        self.dve.wait_ge(self.raised.sem, self.base + self.count)


class NormState:

    def __init__(self, core, sb, sig, name):
        self.stats = sb(f"{name}_stats", [P, TILES, 6])
        self.mean_var = sb(f"{name}_mean_var", [P, TILES, 2])
        self.carrier = sb(f"{name}_carrier", [P, 1])
        self.var_eps = sb(f"{name}_var_eps", [P, TILES])
        self.rstd = sb(f"{name}_rstd", [P, TILES])
        self.minus_half = core.minus_half
        self.var_ready = sig(f"{name}_var_ready")
        self.rstd_ready = sig(f"{name}_rstd_ready")

    def statistics(self, nc, link, source, eps, width=D):
        norm_statistics(nc, link, self, source, TILES, width)
        nc.vector.tensor_scalar(self.var_eps[:, :], self.mean_var[:, :, 1], eps, None, ALU.add).then_inc(
            self.var_ready.sem, 1)

    def power(self, nc, pool, t):
        pool.wait_ge(self.var_ready.sem, self.var_ready.at(t, 1))
        nc.gpsimd.tensor_tensor(self.rstd[:, :], self.var_eps[:, :], self.minus_half[:, :], ALU.pow).then_inc(
            self.rstd_ready.sem, 1)

    def apply(self, nc, dve, t, source, target):
        dve.wait_ge(self.rstd_ready.sem, self.rstd_ready.at(t, 1))
        for c in range(TILES):
            last = nc.vector.tensor_scalar(target(c), source(c), self.mean_var[:, c, 0:1], self.rstd[:, c:c + 1],
                                           ALU.subtract, ALU.mult)
        return last


class Narrow:

    def __init__(self, core, name, tag, causal, ctx):
        sb = lambda n, shape, dtype=F32: core.sbuf(f"{name}_{n}", shape, dtype, ctx)
        sig = lambda n, per=1: core.semaphore(f"{tag}_{n}", per)
        self.front_norm = NormState(core, sb, sig, "front")
        self.tail_norm = NormState(core, sb, sig, "tail")
        self.pool_carrier = sb("pool_carrier", [P, 1])
        self.xn = sb("xn", [P, 2, TILES, D])
        self.xt = sb("xt", [P, SEQ])
        self.qk = sb("qk", [P, TILES, 2, D])
        self.v = sb("v", [P, 2, TILES, HEADS, HD8 + 1])
        self.q_parts = sb("q_parts", [P, TILES, HEADS, QUAD], BF16)
        self.k_parts = sb("k_parts", [P, TILES, HEADS, QUAD], BF16)
        self.qkt = sb("qkt", [P, 2, GROUPS, 2, SEQ], BF16)
        self.q_alone = sb("q_alone", [P, 2, HEADS, SEQ], BF16)
        self.neg_max = sb("neg_max", [P, GROUPS, TILES, GH])
        self.max_parts = sb("max_parts", [P, GROUPS, TILES, GH, 2], BF16)
        self.max_t = sb("max_t", [2 * GH, GROUPS, SEQ], BF16)
        self.probs = sb("probs", [P, KEPT * GH, SEQ])
        self.out_t = sb("out_t", [P, 2, GROUPS, SEQ])
        self.inverse = sb("inverse", [P, TILES, HEADS])
        self.attn = sb("attn", [P, TILES, D])
        self.attn_t = sb("attn_t", [P, SEQ])
        self.y = sb("y", [P, TILES, D])
        self.y_norm = sb("y_norm", [P, TILES, D])
        if causal:
            self.units = [[(0, 0, 0, 512)], [(1, 128, 0, 384), (3, 384, 384, 128)], [(2, 256, 0, 256)]]
            self.steps = {0: "norm", 3: "xn", 4: "xt", 6: "proj0", 7: "proj1", 9: "proj2", 10: "proj3", 11: "high",
                          12: "low", 14: "parts0", 15: "parts1", 17: "parts2", 18: "parts3", 19: "place",
                          26: "out0", 27: "out1", 29: "out2", 30: "out3", 32: "attn", 34: "wo", 35: "y_norm",
                          39: "y_add"}
        else:
            self.units = [[(k, 0, 0, SEQ)] for k in range(TILES)]
            self.steps = {0: "norm", 3: "xn", 6: "xt", 8: "proj0", 10: "proj1", 12: "proj2", 14: "proj3", 15: "high",
                          16: "low", 19: "parts0", 21: "parts1", 23: "parts2", 25: "parts3", 26: "place",
                          35: "out0", 38: "out1", 41: "out2", 44: "out3", 46: "attn", 51: "wo", 52: "y_norm",
                          58: "y_add"}
        self.nu = len(self.units)
        self.n_units = n = GROUPS * self.nu
        self.links = 2 + 4 + 4 + 2 + (2 if causal else 4)
        self.link = sig("link")
        self.ready = sig("ready")
        self.cleared = sig("cleared0"), sig("cleared1")
        self.stage_written, self.stage_read = sig("stage_written"), sig("stage_read")
        self.xn_ready = sig("xn_ready")
        self.xn_kept = sig("xn_kept")
        self.high_ready = sig("high_ready", 4)
        self.low_ready = sig("low_ready", 2)
        self.q_alone_ready = sig("q_alone_ready", 16 * GH)
        self.row_scores = sig("row_scores", GROUPS * TILES * 2)
        self.row_max = sig("row_max", GROUPS * TILES * 2)
        self.max_ready = sig("max_ready", GROUPS)
        self.max_placed = [sig(f"max_placed{g}", 16 * GH) for g in range(GROUPS)]
        self.scores = sig("scores", n * GH)
        self.exp_done = sig("exp_done", n * GH)
        self.masked = sig("masked", n)
        self.pv_done = sig("pv_done", n)
        self.out_t_ready = sig("out_t_ready", GROUPS)

    FRONT = "norm xn xt proj0 proj1 proj2 proj3 high low parts0 parts1 parts2 parts3 place".split()
    TAIL = "out0 out1 out2 out3 attn wo y_norm y_add".split()
    UNSTAGED = "norm xn high low place y_norm y_add".split()

    def slot(self, i, kind):
        g, names = i // (self.nu * GH), []
        if i % (self.nu * GH) == 1 and not (g == GROUPS - 1 and kind == "last"):
            names.append(f"max{(g + 1) % GROUPS}")
        if i in self.steps:
            name = self.steps[i]
            if (kind != "last" or name not in self.FRONT) and (kind != "first" or name not in self.TAIL):
                names.append(name)
        return names

    def staged(self, kind):
        if kind == "before":
            names = self.FRONT + ["max0"]
        elif kind == "after":
            names = self.TAIL
        else:
            names = [name for i in range(self.n_units * GH) for name in self.slot(i, kind)]
        return [name for name in names if name not in self.UNSTAGED]

    def fills(self, i):
        per_group = 2 * TILES
        due = lambda k: 2 * per_group + k * per_group // (GH * self.nu)
        return range(due(i), due(i + 1))

    def stage(self, kind, t):
        count = lambda k: len(self.staged(k))
        if kind == "before":
            base = 0
        elif kind == "first":
            base = count("before")
        else:
            base = count("before") + count("first") + (t - 1) * count("mid")
            if kind == "after":
                base = base - count("mid") + count("last")
        return Stage(self.stage_written, self.stage_read, self.staged(kind), base)


def over_turns(engine, before, turn, after):
    before()
    turn(0, 0, "first")
    with engine.Fori(0, (BATCH - 2) // 2) as i:
        turn(2 * i + 1, 1, "mid")
        turn(2 * i + 2, 0, "mid")
    turn(BATCH - 1, 1, "last")
    after()


def narrow_attention(core, name, tag, causal, w_qkv, b_qkv, w_o, b_o, weights, result):
    nc, X, PS = core.nc, core.X, core.PS
    PB = PS.bitcast(BF16)
    scale = float(HD8) ** -0.5
    ident, ident_b = core.ident, core.ident_b
    ST, STAGE, OUT = 4, 6, 7
    ROWS = GROUPS * TILES * 2

    with ExitStack() as ctx:
        s = Narrow(core, name, tag, causal, ctx)
        units, nu, N = s.units, s.nu, s.n_units
        block = ctx.enter_context(nc.Block())

        @block.sync
        def _(sp):
            def step(stage, name, t, b):
                if name == "place":
                    stage.after(sp, "parts3")
                    alone = s.q_alone[:, b, :, :].rearrange("p (g j) t -> p g j t", j=GH)
                    for j in range(GH):
                        rows = slice(QUAD * j, QUAD * (j + 1))
                        sp.dma_start(alone[rows, :, j, :], s.qkt[rows, b, :, 0, :]).then_inc(s.q_alone_ready.sem, 16)
                elif name[:3] == "max":
                    g = int(name[3:])
                    stage.after(sp, name)
                    for j in range(GH):
                        first = QUAD * j + 3 * HD8
                        sp.dma_start(s.q_alone[first:first + 2, b, GH * g + j, :],
                                     s.max_t[2 * j:2 * j + 2, g, :]).then_inc(s.max_placed[g].sem, 16)

            def before():
                stage = s.stage("before", 0)
                sp.wait_ge(s.cleared[0].sem, 1)
                step(stage, "place", 0, 0)
                step(stage, "max0", 0, 0)
                sp.wait_ge(s.cleared[1].sem, 1)
                if causal:
                    core.load_rest(sp)

            def turn(t, b, kind):
                stage = s.stage(kind, t)
                for i in range(N * GH):
                    for name in s.slot(i, kind):
                        ahead = name == "place" or name == "max0"
                        step(stage, name, t + 1 if ahead else t, 1 - b if ahead else b)

            over_turns(sp, before, turn, lambda: None)

        @block.gpsimd
        def _(pool):
            nc.gpsimd.memset(s.v[:, :, :, :, HD8:], 1.0)
            nc.gpsimd.memset(s.q_parts[:, :, :, 3 * HD8:], 0.0)
            nc.gpsimd.memset(s.k_parts[:, :, :, 3 * HD8:3 * HD8 + 2], 1.0)
            nc.gpsimd.memset(s.k_parts[:, :, :, 3 * HD8 + 2:], 0.0).then_inc(s.ready.sem, 1)
            nc.gpsimd.memset(s.q_alone[:, 0, :, :], 0.0).then_inc(s.cleared[0].sem, 1)

            def turn(t, b, kind):
                for n in range(N):
                    if causal:
                        pool.wait_ge(s.exp_done.sem, s.exp_done.at(t, GH * (n + 1)))
                        if n or kind != "first":
                            pool.wait_ge(s.masked.sem, s.masked.at(t, n))
                        nc.gpsimd.tensor_tensor(s.pool_carrier[:, :], core.minus_half[:, 0:1],
                                                core.minus_half[:, 0:1], ALU.add)
                        slot = n % KEPT * GH
                        for _, _, at, _ in units[n % nu]:
                            square = s.probs[:, slot:slot + GH, at:at + P]
                            last = nc.gpsimd.affine_select(out=square, in_=square, compare_op=ALU.is_ge, fill=0.0,
                                                           base=0, pattern=[[0, GH], [1, P]], channel_multiplier=-1)
                        last.then_inc(s.masked.sem, 1)
                    for name in (name for j in range(GH) for name in s.slot(GH * n + j, kind)):
                        if name == "norm":
                            s.front_norm.power(nc, pool, t + 1)
                        elif name == "xn" and not causal:
                            keep_xn(t + 1, 1 - b)
                        elif name == "y_norm":
                            s.tail_norm.power(nc, pool, t - 1)

            def keep_xn(t, b):
                pool.wait_ge(s.xn_ready.sem, s.xn_ready.at(t, 1))
                nc.gpsimd.tensor_copy(core.X1[:, bass.ds(t * TILES, TILES), :], s.xn[:, b, :, :]).then_inc(
                    s.xn_kept.sem, 1)

            def before():
                s.front_norm.power(nc, pool, 0)
                if not causal:
                    keep_xn(0, 0)

            over_turns(pool, before, turn,
                       lambda: s.tail_norm.power(nc, pool, BATCH - 1))

        @block.vector
        def _(dve):
            nc.vector.memset(PS[:, OUT, :], 0.0).then_inc(s.ready.sem, 1)
            dve.wait_ge(s.ready.sem, 2)
            for load in weights[1:]:
                dve.wait_ge(load.sem, load.per_turn)

            def row_max(t, n):
                g, c, half = n // (2 * TILES), n // 2 % TILES, n % 2
                keys = P * (c + 1) if causal else SEQ
                dve.wait_ge(s.row_scores.sem, s.row_scores.at(t, n + 1))
                bank = n % 2 * 2
                nc.vector.tensor_reduce(s.neg_max[:, g, c, 2 * half:2 * half + 2], PS[:, bank:bank + 2, 0:keys], AX.X,
                                        ALU.max, negate=True).then_inc(s.row_max.sem, 1)

            def split_maxima(chain, t, g):
                dve.wait_ge(s.row_max.sem, s.row_max.at(t, (g + 1) * TILES * 2))
                maxima = s.neg_max[:, g, :, :]
                chain.link(nc.vector.tensor_copy(s.max_parts[:, g, :, :, 0], maxima))
                nc.vector.tensor_tensor(s.max_parts[:, g, :, :, 1], maxima, s.max_parts[:, g, :, :, 0],
                                        ALU.subtract).then_inc(s.max_ready.sem, 1)

            def step(chain, stage, name, t, b):
                x = lambda c: X[:, t * TILES + c, :]
                if name == "norm":
                    s.front_norm.statistics(nc, chain.link, x, 1e-5)
                elif name == "xn":
                    if not causal and not (isinstance(t, int) and t < 2):
                        dve.wait_ge(s.xn_kept.sem, s.xn_kept.at(t, -1))
                    s.front_norm.apply(nc, dve, t, x, lambda c: s.xn[:, b, c, :]).then_inc(s.xn_ready.sem, 1)
                elif name[:4] == "proj":
                    c = int(name[4:])
                    stage.drain(dve, name)
                    nc.vector.tensor_tensor(s.qk[:, c, :, :].rearrange("p a d -> p (a d)"), PS[:, STAGE, 0:2 * D],
                                            b_qkv[:, 0:2 * D], ALU.add)
                    nc.vector.tensor_tensor(s.v[:, b, c, :, 0:HD8],
                                            PS[:, STAGE, 2 * D:3 * D].rearrange("p (h e) -> p h e", e=HD8),
                                            b_qkv[:, 2 * D:3 * D].rearrange("p (h e) -> p h e", e=HD8),
                                            ALU.add).then_inc(s.stage_read.sem, 1)
                elif name == "low":
                    for a, (parts, first) in enumerate(((s.q_parts, HD8), (s.k_parts, 2 * HD8))):
                        dve.wait_ge(s.high_ready.sem, s.high_ready.at(t, 2 * a + 1))
                        nc.vector.tensor_tensor(parts[:, :, :, first:first + HD8],
                                                s.qk[:, :, a, :].rearrange("p c (h e) -> p c h e", e=HD8),
                                                parts[:, :, :, 0:HD8], ALU.subtract).then_inc(s.low_ready.sem, 1)
                elif name[:5] == "parts":
                    stage.drain(dve, name)
                    nc.vector.tensor_copy(s.qkt[:, b, int(name[5:]), :, :].rearrange("p a t -> p (a t)"),
                                          PB[:, STAGE, :]).then_inc(s.stage_read.sem, 1)
                elif name[:3] == "out":
                    c = int(name[3:])
                    stage.drain(dve, name)
                    heads = PS[:, STAGE, :].rearrange("p (h r) -> p h r", r=QUAD)
                    chain.link(nc.vector.reciprocal(s.inverse[:, c, :], heads[:, :, HD8]))
                    nc.vector.tensor_tensor(s.attn[:, c, :].rearrange("p (h e) -> p h e", e=HD8), heads[:, :, 0:HD8],
                                            s.inverse[:, c, :].unsqueeze(2).to_broadcast([P, HEADS, HD8]),
                                            ALU.mult).then_inc(s.stage_read.sem, 1)
                elif name == "wo":
                    stage.drain(dve, name)
                    nc.vector.tensor_tensor(s.y[:, :, :], PS[:, STAGE, :].rearrange("p (c d) -> p c d", d=D),
                                            b_o[:, :].unsqueeze(1).to_broadcast([P, TILES, D]),
                                            ALU.add).then_inc(s.stage_read.sem, 1)
                elif name == "y_norm":
                    stage.after(dve, "wo")
                    if not causal:
                        dve.wait_ge(s.xn_kept.sem, s.xn_kept.at(t, 1))
                        chain.link(nc.vector.tensor_tensor(s.y[:, :, :], s.y[:, :, :],
                                                           core.X1[:, bass.ds(t * TILES, TILES), :], ALU.add))
                    s.tail_norm.statistics(nc, chain.link, lambda c: s.y[:, c, :], 1e-5)
                elif name == "y_add":
                    chain.link(s.tail_norm.apply(nc, dve, t, lambda c: s.y[:, c, :], lambda c: s.y_norm[:, c, :]))
                    result(nc, chain.link, s, t, x)

            links = [0]

            def before():
                chain = Chain(dve, s.link, 0)
                stage = s.stage("before", 0)
                if causal:
                    dve.wait_ge(core.x_first.sem, 16)
                for name in s.FRONT:
                    step(chain, stage, name, 0, 0)
                nc.vector.memset(s.q_alone[:, 1, :, :], 0.0).then_inc(s.cleared[1].sem, 1)
                if causal:
                    dve.wait_ge(core.x_rest.sem, 16)
                for n in range(2 * 2 * TILES):
                    row_max(0, n)
                    if n % (2 * TILES) == 2 * TILES - 1:
                        split_maxima(chain, 0, n // (2 * TILES))
                links[0] = chain.count

            def turn(t, b, kind):
                first = links[0] if kind == "first" else links[0] + (t - 1) * s.links
                chain = Chain(dve, s.link, first)
                stage = s.stage(kind, t)
                for i in range(N * GH):
                    for m in s.fills(i):
                        if m < ROWS or kind != "last":
                            t_rows = t if m < ROWS else t + 1
                            row_max(t_rows, m % ROWS)
                            if m % (2 * TILES) == 2 * TILES - 1:
                                split_maxima(chain, t_rows, m % ROWS // (2 * TILES))
                    for name in s.slot(i, kind):
                        if name in s.FRONT:
                            step(chain, stage, name, t + 1, 1 - b)
                        elif name in s.TAIL:
                            step(chain, stage, name, t - 1, 1 - b)
                if kind == "first":
                    links[0] += chain.count
                else:
                    assert kind == "last" or chain.count == s.links, (chain.count, s.links)
                last_links[0] = chain.count

            last_links = [0]

            def after():
                chain = Chain(dve, s.link, links[0] + (BATCH - 2) * s.links + last_links[0])
                stage = s.stage("after", BATCH)
                for name in s.TAIL:
                    step(chain, stage, name, BATCH - 1, 1)

            over_turns(dve, before, turn, after)

        @block.scalar
        def _(act):
            act.wait_ge(s.ready.sem, 2)

            def exponentials(t, n, j, kind):
                width = sum(w for _, _, _, w in units[n % nu])
                if n >= KEPT or kind != "first":
                    act.wait_ge(s.pv_done.sem, s.pv_done.at(t, n - KEPT + 1))
                act.wait_ge(s.scores.sem, s.scores.at(t, GH * n + j + 1))
                nc.scalar.activation(s.probs[:, n % KEPT * GH + j, 0:width], PS[:, ST + j % 2, 0:width],
                                     ACT.Exp, scale=scale).then_inc(s.exp_done.sem, 1)

            def keep_products(t, b, g):
                act.wait_ge(s.pv_done.sem, s.pv_done.at(t, nu * (g + 1)))
                nc.scalar.activation(s.out_t[:, b, g, :], PS[:, OUT, :], ACT.Copy).then_inc(s.out_t_ready.sem, 1)

            def step(stage, name, t):
                if name == "xt":
                    stage.drain(act, name)
                    nc.scalar.activation(s.xt[:, :], PS[:, STAGE, :], ACT.Copy).then_inc(s.stage_read.sem, 1)
                elif name == "high":
                    stage.after(act, "proj3")
                    for a, (parts, copies) in enumerate(((s.q_parts, (0, 2 * HD8)), (s.k_parts, (0, HD8)))):
                        for first in copies:
                            nc.scalar.activation(parts[:, :, :, first:first + HD8],
                                                 s.qk[:, :, a, :].rearrange("p c (h e) -> p c h e", e=HD8),
                                                 ACT.Copy).then_inc(s.high_ready.sem, 1)
                elif name[:3] == "max":
                    stage.drain(act, name)
                    nc.scalar.activation(s.max_t[:, int(name[3:]), :], PB[0:2 * GH, STAGE, 0:SEQ],
                                         ACT.Copy).then_inc(s.stage_read.sem, 1)
                elif name == "attn":
                    stage.drain(act, name)
                    nc.scalar.activation(s.attn_t[:, :], PS[:, STAGE, :], ACT.Copy).then_inc(s.stage_read.sem, 1)

            def before():
                stage = s.stage("before", 0)
                for name in s.FRONT + ["max0"]:
                    step(stage, name, 0)

            def turn(t, b, kind):
                stage = s.stage(kind, t)
                for i in range(N * GH):
                    n, j = i // GH, i % GH
                    exponentials(t, n, j, kind)
                    if n % nu == 1 and j == 1:
                        if n > nu:
                            keep_products(t, b, n // nu - 1)
                        elif kind != "first":
                            keep_products(t - 1, 1 - b, GROUPS - 1)
                    for name in s.slot(i, kind):
                        step(stage, name, t + 1 if name in s.FRONT else t - 1)

            def after():
                keep_products(BATCH - 1, 1, GROUPS - 1)
                step(s.stage("after", BATCH), "attn", BATCH - 1)

            over_turns(act, before, turn, after)

        @block.tensor
        def _(pe):
            pe.wait_ge(s.ready.sem, 2)
            pe.wait_ge(core.constants_ready.sem, core.constants_ready.per_turn)
            pe.wait_ge(weights[0].sem, weights[0].per_turn)

            def row_scores(t, b, n, first):
                g, c, half = n // (2 * TILES), n // 2 % TILES, n % 2
                if n == 0:
                    pe.wait_ge(s.q_alone_ready.sem, s.q_alone_ready.at(t, 16 * GH))
                if n >= 2 or not first:
                    pe.wait_ge(s.row_max.sem, s.row_max.at(t, n - 1))
                keys = P * (c + 1) if causal else SEQ
                for h in range(2):
                    bank = n % 2 * 2 + h
                    last = nc.tensor.matmul(PS[:, bank, 0:keys],
                                            s.q_alone[:, b, GH * g + 2 * half + h, c * P:(c + 1) * P],
                                            s.qkt[:, b, g, 1, 0:keys], start=True, stop=not causal)
                    if causal:
                        last = nc.tensor.matmul(PS[:, bank, keys - P:keys], ident_b[:, :], core.mask[:, :],
                                                start=False, stop=True)
                last.then_inc(s.row_scores.sem, 1)

            def products(t, b, n):
                g, u = n // nu, n % nu
                if causal:
                    pe.wait_ge(s.masked.sem, s.masked.at(t, n + 1))
                else:
                    pe.wait_ge(s.exp_done.sem, s.exp_done.at(t, GH * (n + 1)))
                if u == 0 and not (g == 0 and isinstance(t, int) and t == 0):
                    pe.wait_ge(s.out_t_ready.sem, s.out_t_ready.at(t, g))
                for i, (k, q0, at, width) in enumerate(units[u]):
                    for j in range(GH):
                        last = nc.tensor.matmul(PS[QUAD * j:QUAD * j + HD8 + 1, OUT, q0:q0 + width],
                                                s.v[:, b, k, GH * g + j, :],
                                                s.probs[:, n % KEPT * GH + j, at:at + width],
                                                start=u == 0 and i == 0, stop=u == nu - 1 and i == len(units[u]) - 1)
                last.then_inc(s.pv_done.sem, 1)

            def step(stage, name, t, b):
                if name in s.UNSTAGED:
                    return
                stage.fill(pe, name)
                if name == "xt":
                    pe.wait_ge(s.xn_ready.sem, s.xn_ready.at(t, 1))
                    for c in range(TILES):
                        last = nc.tensor.transpose(PS[:, STAGE, c * P:(c + 1) * P], s.xn[:, b, c, :], ident[:, :])
                elif name[:4] == "proj":
                    c = int(name[4:])
                    last = nc.tensor.matmul(PS[:, STAGE, 0:3 * D], s.xt[:, c * P:(c + 1) * P], w_qkv[:, :],
                                            start=True, stop=True)
                elif name[:5] == "parts":
                    g = int(name[5:])
                    if g == 0:
                        pe.wait_ge(s.high_ready.sem, s.high_ready.at(t, 4))
                        pe.wait_ge(s.low_ready.sem, s.low_ready.at(t, 2))
                    for a, parts in enumerate((s.q_parts, s.k_parts)):
                        for c in range(TILES):
                            at = a * SEQ + c * P
                            last = nc.tensor.transpose(
                                PB[:, STAGE, at:at + P],
                                parts[:, c, GH * g:GH * (g + 1), :].rearrange("p h r -> p (h r)"), ident_b[:, :])
                elif name[:3] == "max":
                    g = int(name[3:])
                    pe.wait_ge(s.max_ready.sem, s.max_ready.at(t, g + 1))
                    for c in range(TILES):
                        last = nc.tensor.transpose(PB[0:2 * GH, STAGE, c * P:(c + 1) * P],
                                                   s.max_parts[:, g, c, :, :].rearrange("p j r -> p (j r)"),
                                                   ident_b[:, :])
                elif name[:3] == "out":
                    c = int(name[3:])
                    if c == 0:
                        pe.wait_ge(s.out_t_ready.sem, s.out_t_ready.at(t, GROUPS))
                    for g in range(GROUPS):
                        last = nc.tensor.transpose(PS[:, STAGE, g * P:(g + 1) * P],
                                                   s.out_t[:, b, g, c * P:(c + 1) * P], ident[:, :])
                elif name == "attn":
                    for c in range(TILES):
                        last = nc.tensor.transpose(PS[:, STAGE, c * P:(c + 1) * P], s.attn[:, c, :], ident[:, :])
                elif name == "wo":
                    for c in range(TILES):
                        last = nc.tensor.matmul(PS[:, STAGE, c * P:(c + 1) * P], s.attn_t[:, c * P:(c + 1) * P],
                                                w_o[:, :], start=True, stop=True)
                last.then_inc(s.stage_written.sem, 1)

            def before():
                stage = s.stage("before", 0)
                for name in s.FRONT:
                    step(stage, name, 0, 0)
                for n in range(2 * 2 * TILES):
                    row_scores(0, 0, n, True)
                step(stage, "max0", 0, 0)

            def turn(t, b, kind):
                stage = s.stage(kind, t)
                for n in range(N):
                    g, u = n // nu, n % nu
                    if u == 0:
                        pe.wait_ge(s.max_placed[g].sem, s.max_placed[g].at(t, 16 * GH))
                    for j in range(GH):
                        i = GH * n + j
                        if i >= 2 or kind != "first":
                            pe.wait_ge(s.exp_done.sem, s.exp_done.at(t, i - 1))
                        for k, q0, at, width in units[u]:
                            last = nc.tensor.matmul(PS[:, ST + j % 2, at:at + width],
                                                    s.qkt[:, b, g, 1, k * P:(k + 1) * P],
                                                    s.q_alone[:, b, GH * g + j, q0:q0 + width], start=True, stop=True)
                        last.then_inc(s.scores.sem, 1)
                        for m in s.fills(i):
                            if m < ROWS:
                                row_scores(t, b, m, False)
                            elif kind != "last":
                                row_scores(t + 1, 1 - b, m - ROWS, False)
                        for name in s.slot(i, kind):
                            if name in s.FRONT or name == "max0":
                                step(stage, name, t + 1, 1 - b)
                            elif name in s.TAIL:
                                step(stage, name, t - 1, 1 - b)
                            else:
                                step(stage, name, t, b)
                        if j == GH - 1:
                            if n:
                                products(t, b, n - 1)
                            elif kind != "first":
                                products(t - 1, 1 - b, N - 1)

            def after():
                products(BATCH - 1, 1, N - 1)
                stage = s.stage("after", BATCH)
                for name in s.TAIL:
                    step(stage, name, BATCH - 1, 1)

            over_turns(pe, before, turn, after)


def scale_shift(nc, link, target, source, gain, offset):
    rows = [P, TILES, D]
    link(nc.vector.tensor_tensor(target[:, :, :], source[:, :, :], gain[:, :].unsqueeze(1).to_broadcast(rows), ALU.mult))
    link(nc.vector.tensor_tensor(target[:, :, :], target[:, :, :], offset[:, :].unsqueeze(1).to_broadcast(rows), ALU.add))


def add_normalised(nc, link, s, turn, x):
    for c in range(TILES):
        last = nc.vector.tensor_tensor(x(c), x(c), s.y_norm[:, c, :], ALU.add)
    link(last)


def keep_norm1(core):
    def result(nc, link, s, turn, x):
        rows = [P, TILES, D]
        gain, offset = core.ln1_g[:, :].unsqueeze(1), core.ln1_b[:, :].unsqueeze(1)
        link(nc.vector.tensor_tensor(s.y[:, :, :], s.y_norm[:, :, :], gain.to_broadcast(rows), ALU.mult))
        link(nc.vector.tensor_tensor(core.X1[:, bass.ds(turn * TILES, TILES), :], s.y[:, :, :],
                                     offset.to_broadcast(rows), ALU.add))
    return result


def gelu_ffn(core, name, tag):
    nc, X, PS, ident = core.nc, core.X, core.PS, core.ident
    TURNED, DOWN, TOKENS = 4, 4, 5
    with ExitStack() as ctx:
        sb = lambda n, shape, dtype=F32: core.sbuf(f"{name}_{n}", shape, dtype, ctx)
        sig = lambda n, per=1: core.semaphore(f"{tag}_{n}", per)
        norm, norm_h, norm_y = (NormState(core, sb, sig, n) for n in ("front", "hidden", "tail"))
        row_sums = sb("row_sums", [P, 2])
        threshold = sb("threshold", [P, 2, 2])
        above, below = sb("above", [P, 2, FF]), sb("below", [P, 2, FF])
        w_up, w_down = sb("w_up", [P, FF]), sb("w_down", [P, FC, D])
        xn, xt = sb("xn", [P, TILES, D]), sb("xt", [P, SEQ])
        hidden, hidden_n = sb("h", [P, TILES, FF]), sb("h_norm", [P, TILES, FF])
        hidden_t = sb("h_t", [P, FC, SEQ])
        y, y_norm = sb("y", [P, TILES, D]), sb("y_norm", [P, TILES, D])
        link_signal, links = sig("link"), 8
        setup = sig("setup", 5)
        sums_spread, turned_w, weights_ready = sig("sums_spread"), sig("turned_w"), sig("weights_ready", 2)
        xn_ready, xt_summed, xt_ready = sig("xn_ready"), sig("xt_summed"), sig("xt_ready")
        up_summed, gelu_done, hidden_ready = sig("up_summed", TILES), sig("gelu_done", TILES), sig("hidden_ready")
        hidden_turned, hidden_t_ready = sig("hidden_turned", FC), sig("hidden_t_ready", FC)
        down_summed, y_read = sig("down_summed"), sig("y_read")
        block = ctx.enter_context(nc.Block())

        @block.gpsimd
        def _(pool):
            def turn(t, kind):
                if kind != "last":
                    norm.power(nc, pool, t + 1)
                norm_h.power(nc, pool, t)
                if kind != "first":
                    norm_y.power(nc, pool, t - 1)

            one_by_one(pool, lambda: norm.power(nc, pool, 0), turn, lambda: norm_y.power(nc, pool, BATCH - 1))

        @block.vector
        def _(dve):
            dve.wait_ge(core.weights_b.sem, core.weights_b.per_turn)
            raw = (core.w_fc[:, :, :], core.w_proj[:, :, :])
            for i, weight in enumerate(raw):
                nc.vector.tensor_reduce(row_sums[:, i:i + 1], weight, AX.XY, ALU.add,
                                        apply_absolute_value=True).then_inc(setup.sem, 1)
            dve.wait_ge(sums_spread.sem, 1)
            for i, sign in enumerate((0.5, -0.5)):
                nc.vector.tensor_scalar(threshold[:, :, i], PS[:, 0, 0:2], sign / (D * FF), sign * 1e-6, ALU.mult,
                                        ALU.add).then_inc(setup.sem, 1)
            dve.wait_ge(setup.sem, 4)
            for i, weight in enumerate(raw):
                flat = weight.rearrange("p a d -> p (a d)")
                nc.vector.tensor_scalar(above[:, i, :], flat, threshold[:, i, 0:1], None, ALU.is_gt)
                last = nc.vector.tensor_scalar(below[:, i, :], flat, threshold[:, i, 1:2], None, ALU.is_lt)
            last.then_inc(setup.sem, 1)
            dve.wait_ge(setup.sem, 5)
            nc.vector.tensor_tensor(above[:, :, :], above[:, :, :], below[:, :, :], ALU.subtract).then_inc(
                weights_ready.sem, 1)
            counted = [0]

            def x_of(t):
                return lambda c: X[:, t * TILES + c, :]

            def apply_norm(t):
                if not (isinstance(t, int) and t == 0):
                    dve.wait_ge(xt_summed.sem, xt_summed.at(t, 0))
                norm.apply(nc, dve, t, x_of(t), lambda c: xn[:, c, :]).then_inc(xn_ready.sem, 1)

            def read_y(link, t):
                dve.wait_ge(down_summed.sem, down_summed.at(t, 1))
                nc.vector.tensor_copy(y[:, :, :].rearrange("p c d -> p (c d)"), PS[:, DOWN, :]).then_inc(y_read.sem, 1)
                dve.wait_ge(y_read.sem, y_read.at(t, 1))
                norm_y.statistics(nc, link, lambda c: y[:, c, :], 1e-5)

            def add_y(link, t):
                link(norm_y.apply(nc, dve, t, lambda c: y[:, c, :], lambda c: y_norm[:, c, :]))
                for c in range(TILES):
                    last = nc.vector.tensor_tensor(x_of(t)(c), x_of(t)(c), y_norm[:, c, :], ALU.add)
                link(last)

            def hidden_layer(t):
                norm_h.apply(nc, dve, t, lambda c: hidden[:, c, :], lambda c: hidden_n[:, c, :]).then_inc(
                    hidden_ready.sem, 1)

            def before():
                chain = Chain(dve, link_signal, 0)
                norm.statistics(nc, chain.link, x_of(0), 1e-5)
                apply_norm(0)
                counted[0] = chain.count

            def turn(t, kind):
                chain = Chain(dve, link_signal, counted[0] + (0 if kind == "first" else (t - 1) * links))
                if kind != "last":
                    norm.statistics(nc, chain.link, x_of(t + 1), 1e-5)
                    apply_norm(t + 1)
                dve.wait_ge(gelu_done.sem, gelu_done.at(t, TILES))
                norm_h.statistics(nc, chain.link, lambda c: hidden[:, c, :], 1e-5, FF)
                if kind != "first":
                    read_y(chain.link, t - 1)
                hidden_layer(t)
                if kind != "first":
                    add_y(chain.link, t - 1)
                if kind == "first":
                    counted[0] += chain.count
                elif kind == "mid":
                    assert chain.count == links, (chain.count, links)
                else:
                    counted[0] += (BATCH - 2) * links + chain.count

            def after():
                chain = Chain(dve, link_signal, counted[0])
                read_y(chain.link, BATCH - 1)
                add_y(chain.link, BATCH - 1)

            one_by_one(dve, before, turn, after)

        @block.scalar
        def _(act):
            act.wait_ge(turned_w.sem, 1)
            nc.scalar.activation(w_up[:, :], PS[:, 1, :], ACT.Copy)
            nc.scalar.activation(w_down[:, :, :].rearrange("p a d -> p (a d)"), PS[:, 2, :], ACT.Copy).then_inc(
                weights_ready.sem, 1)

            def keep_xt(t):
                act.wait_ge(xt_summed.sem, xt_summed.at(t, 1))
                nc.scalar.activation(xt[:, :], PS[:, TOKENS, :], ACT.Copy).then_inc(xt_ready.sem, 1)

            def turn(t, kind):
                for c in range(TILES):
                    if c == 0 and kind != "first":
                        act.wait_ge(hidden_ready.sem, hidden_ready.at(t, 0))
                    act.wait_ge(up_summed.sem, up_summed.at(t, c + 1))
                    nc.scalar.activation(hidden[:, c, :], PS[:, c, :], ACT.Gelu).then_inc(gelu_done.sem, 1)
                if kind != "last":
                    keep_xt(t + 1)

                for f in range(FC):
                    act.wait_ge(hidden_turned.sem, hidden_turned.at(t, f + 1))
                    nc.scalar.activation(hidden_t[:, f, :], PS[:, TURNED + f, :], ACT.Identity,
                                         bias=core.ln_b[:, f:f + 1], scale=core.ln_w[:, f:f + 1]).then_inc(
                        hidden_t_ready.sem, 1)

            one_by_one(act, lambda: keep_xt(0), turn, lambda: None)

        @block.tensor
        def _(pe):
            pe.wait_ge(core.constants_ready.sem, core.constants_ready.per_turn)
            pe.wait_ge(setup.sem, 2)
            nc.tensor.matmul(PS[:, 0, 0:2], core.ones[:, :], row_sums[:, :], start=True, stop=True).then_inc(
                sums_spread.sem, 1)
            pe.wait_ge(weights_ready.sem, 1)
            for i in range(2):
                for a in range(FC):
                    last = nc.tensor.transpose(PS[:, 1 + i, a * P:(a + 1) * P], above[:, i, a * P:(a + 1) * P],
                                               ident[:, :])
            last.then_inc(turned_w.sem, 1)
            pe.wait_ge(weights_ready.sem, 2)

            def turn_tokens(t):
                pe.wait_ge(xn_ready.sem, xn_ready.at(t, 1))
                for c in range(TILES):
                    last = nc.tensor.transpose(PS[:, TOKENS, c * P:(c + 1) * P], xn[:, c, :], ident[:, :])
                last.then_inc(xt_summed.sem, 1)

            def up(t):
                pe.wait_ge(xt_ready.sem, xt_ready.at(t, 1))
                for c in range(TILES):
                    nc.tensor.matmul(PS[:, c, :], xt[:, c * P:(c + 1) * P], w_up[:, :], start=True,
                                     stop=True).then_inc(up_summed.sem, 1)

            def turn_hidden(t):
                pe.wait_ge(hidden_ready.sem, hidden_ready.at(t, 1))
                for f in range(FC):
                    for c in range(TILES):
                        last = nc.tensor.transpose(PS[:, TURNED + f, c * P:(c + 1) * P],
                                                   hidden_n[:, c, f * P:(f + 1) * P], ident[:, :])
                    last.then_inc(hidden_turned.sem, 1)

            def down(t):
                pe.wait_ge(hidden_t_ready.sem, hidden_t_ready.at(t, FC))
                for c in range(TILES):
                    for f in range(FC):
                        last = nc.tensor.matmul(PS[:, DOWN, c * P:(c + 1) * P], hidden_t[:, f, c * P:(c + 1) * P],
                                                w_down[:, f, :], start=f == 0, stop=f == FC - 1)
                last.then_inc(down_summed.sem, 1)

            def turn(t, kind):
                up(t)
                if kind != "first":
                    down(t - 1)
                if kind != "last":
                    turn_tokens(t + 1)
                    pe.wait_ge(xt_ready.sem, xt_ready.at(t, 2))
                if kind != "first":
                    pe.wait_ge(y_read.sem, y_read.at(t, 0))
                turn_hidden(t)

            one_by_one(pe, lambda: turn_tokens(0), turn, lambda: down(BATCH - 1))


def expert_ffn(core, name, tag, stored, out):
    nc, X, X1, PS, ident = core.nc, core.X, core.X1, core.PS, core.ident
    UP, TURN, DOWN = 3, 3, 4
    BLOCKS = EXPERTS * FC
    with ExitStack() as ctx:
        sb = lambda n, shape, dtype=F32: core.sbuf(f"{name}_{n}", shape, dtype, ctx)
        sig = lambda n, per=1: core.semaphore(f"{tag}_{n}", per)
        norm2, norm = NormState(core, sb, sig, "norm2"), NormState(core, sb, sig, "final")
        now, xt = sb("now", [P, TILES, D]), sb("xt", [P, SEQ])
        key_terms, keys, scaled_floor = sb("key_terms", [P, TILES, D]), sb("keys", [P, TILES]), sb("scaled", [P, TILES])
        whole, rounded = sb("whole", [P, TILES], mybir.dt.int32), sb("rounded", [P, TILES])
        over, floor, chosen = sb("over", [P, TILES]), sb("floor", [P, TILES]), sb("chosen", [P, TILES])
        gate = sb("gate", [P, EXPERTS, TILES])
        hidden = sb("hidden", [P, 4, SEQ])
        experts = sb("experts", [P, TILES, EXPERTS, D])
        total, normed, y_norm = sb("total", [P, TILES, D]), sb("normed", [P, TILES, D]), sb("y_norm", [P, TILES, D])
        link_signal, links = sig("link"), 27
        now_ready, xt_summed, xt_ready = sig("now_ready"), sig("xt_summed"), sig("xt_ready")
        up_summed, hidden_ready, hidden_used = (sig(n, BLOCKS) for n in ("up_summed", "hidden_ready", "hidden_used"))
        down_read, finished = sig("down_read"), sig("finished")
        block = ctx.enter_context(nc.Block())

        @block.sync
        def _(sp):
            with sp.Fori(0, BATCH) as turn:
                sp.wait_ge(finished.sem, finished.at(turn, 1))
                sp.dma_start(out[bass.ds(turn, 1)].rearrange("b (c p) d -> p (b c) d", p=P),
                             X[:, bass.ds(turn * TILES, TILES), :]).then_inc(stored.sem, 16)
            sp.wait_ge(stored.sem, 16 * BATCH)

        @block.gpsimd
        def _(pool):
            with pool.Fori(0, BATCH) as turn:
                norm2.power(nc, pool, turn)
                norm.power(nc, pool, turn)

        @block.vector
        def _(dve):
            dve.wait_ge(core.weights_e.sem, core.weights_e.per_turn)
            counted = [0]

            def fetch(t):
                if not (isinstance(t, int) and t == 0):
                    dve.wait_ge(xt_summed.sem, xt_summed.at(t, 0))
                nc.vector.tensor_copy(now[:, :, :], X1[:, bass.ds(t * TILES, TILES), :]).then_inc(now_ready.sem, 1)

            def read_experts(t):
                dve.wait_ge(hidden_used.sem, hidden_used.at(t, BLOCKS))
                for c in range(TILES):
                    last = nc.vector.tensor_tensor(experts[:, c, :, :].rearrange("p e d -> p (e d)"),
                                                   PS[:, DOWN + c, :], core.b2[:, :], ALU.add)
                last.then_inc(down_read.sem, 1)

            def make_keys(link, t):
                dve.wait_ge(now_ready.sem, now_ready.at(t, 1))
                for c in range(TILES):
                    last = nc.vector.tensor_tensor(key_terms[:, c, :], now[:, c, :], core.router_w[:, :], ALU.mult)
                link(last)
                link(nc.vector.tensor_reduce(keys[:, :], key_terms[:, :, :], AX.X, ALU.add))
                link(nc.vector.tensor_scalar(keys[:, :], keys[:, :], core.router_b[:, 0:1], None, ALU.add))

            def take_floor(link, value):
                link(nc.vector.tensor_copy(whole[:, :], value))
                link(nc.vector.tensor_copy(rounded[:, :], whole[:, :]))
                link(nc.vector.tensor_tensor(over[:, :], rounded[:, :], value, ALU.is_gt))

            def choose(link):
                take_floor(link, keys[:, :])
                link(nc.vector.tensor_tensor(floor[:, :], rounded[:, :], over[:, :], ALU.subtract))
                link(nc.vector.tensor_scalar(scaled_floor[:, :], floor[:, :], 1.0 / EXPERTS, None, ALU.mult))
                take_floor(link, scaled_floor[:, :])
                link(nc.vector.tensor_tensor(chosen[:, :], rounded[:, :], over[:, :], ALU.subtract))
                link(nc.vector.tensor_scalar(chosen[:, :], chosen[:, :], float(EXPERTS), None, ALU.mult))
                link(nc.vector.tensor_tensor(chosen[:, :], floor[:, :], chosen[:, :], ALU.subtract))
                for e in range(EXPERTS):
                    last = nc.vector.tensor_scalar(gate[:, e, :], chosen[:, :], float(e), None, ALU.is_equal)
                link(last)

            def finish(link, t):
                dve.wait_ge(down_read.sem, down_read.at(t, 1))
                for e in range(EXPERTS):
                    for c in range(TILES):
                        before = X1[:, t * TILES + c, :] if e == 0 else total[:, c, :]
                        last = nc.vector.scalar_tensor_tensor(out=total[:, c, :], in0=experts[:, c, e, :],
                                                              scalar=gate[:, e, c:c + 1], in1=before, op0=ALU.mult,
                                                              op1=ALU.add)
                    link(last)
                norm2.statistics(nc, link, lambda c: total[:, c, :], 1e-5)
                link(norm2.apply(nc, dve, t, lambda c: total[:, c, :], lambda c: normed[:, c, :]))
                scale_shift(nc, link, total, normed, core.ln2_g, core.ln2_b)
                norm.statistics(nc, link, lambda c: total[:, c, :], 1e-5)
                link(norm.apply(nc, dve, t, lambda c: total[:, c, :], lambda c: y_norm[:, c, :]))
                x = lambda c: X[:, t * TILES + c, :]
                for c in range(TILES):
                    last = nc.vector.tensor_tensor(x(c), x(c), y_norm[:, c, :], ALU.add)
                last.then_inc(finished.sem, 1)

            def turn(t, kind):
                chain = Chain(dve, link_signal, counted[0] + (0 if kind == "first" else (t - 1) * links))
                if kind != "first":
                    read_experts(t - 1)
                make_keys(chain.link, t)
                if kind != "last":
                    fetch(t + 1)
                if kind != "first":
                    finish(chain.link, t - 1)
                choose(chain.link)
                if kind == "first":
                    counted[0] += chain.count
                elif kind == "mid":
                    assert chain.count == links, (chain.count, links)
                else:
                    counted[0] += (BATCH - 2) * links + chain.count

            def after():
                read_experts(BATCH - 1)
                finish(Chain(dve, link_signal, counted[0]).link, BATCH - 1)

            one_by_one(dve, lambda: fetch(0), turn, after)

        @block.scalar
        def _(act):
            act.wait_ge(core.weights_e.sem, core.weights_e.per_turn)

            def keep_xt(t):
                act.wait_ge(xt_summed.sem, xt_summed.at(t, 1))
                nc.scalar.activation(xt[:, :], PS[:, TURN, :], ACT.Copy).then_inc(xt_ready.sem, 1)

            def turn(t, kind):
                for n in range(BLOCKS):
                    act.wait_ge(up_summed.sem, up_summed.at(t, n + 1))
                    nc.scalar.activation(hidden[:, n % 4, :], PS[:, n % UP, :], ACT.Relu,
                                         bias=core.b1[:, n:n + 1]).then_inc(hidden_ready.sem, 1)
                if kind != "last":
                    keep_xt(t + 1)

            one_by_one(act, lambda: keep_xt(0), turn, lambda: None)

        @block.tensor
        def _(pe):
            pe.wait_ge(core.weights_e.sem, core.weights_e.per_turn)

            def turn_tokens(t):
                pe.wait_ge(now_ready.sem, now_ready.at(t, 1))
                for c in range(TILES):
                    last = nc.tensor.transpose(PS[:, TURN, c * P:(c + 1) * P], now[:, c, :], ident[:, :])
                last.then_inc(xt_summed.sem, 1)

            def up(n):
                nc.tensor.matmul(PS[:, n % UP, :], core.w1[:, n // FC, n % FC * P:(n % FC + 1) * P], xt[:, :],
                                 start=True, stop=True).then_inc(up_summed.sem, 1)

            def down(t, n):
                e, f = n // FC, n % FC
                pe.wait_ge(hidden_ready.sem, hidden_ready.at(t, n + 1))
                for c in range(TILES):
                    last = nc.tensor.matmul(PS[:, DOWN + c, e * D:(e + 1) * D], hidden[:, n % 4, c * P:(c + 1) * P],
                                            core.w2[:, e, f, :], start=f == 0, stop=f == FC - 1)
                last.then_inc(hidden_used.sem, 1)

            def turn(t, kind):
                pe.wait_ge(xt_ready.sem, xt_ready.at(t, 1))
                up(0)
                up(1)
                for n in range(BLOCKS):
                    if n + 2 < BLOCKS:
                        up(n + 2)
                    if n == 0 and kind != "first":
                        pe.wait_ge(down_read.sem, down_read.at(t, 0))
                    if n + 2 == BLOCKS and kind != "last":
                        turn_tokens(t + 1)
                    down(t, n)

            one_by_one(pe, lambda: turn_tokens(0), turn, lambda: None)


def one_by_one(engine, before, turn, after):
    before()
    turn(0, "first")
    with engine.Fori(0, BATCH - 2) as i:
        turn(i + 1, "mid")
    turn(BATCH - 1, "last")
    after()


class Wide:
    NU = 3
    SUBS = 2 * NU
    HELD = 4
    AHEAD = 3
    UNITS = [[(0, 0, 0, 512)], [(1, 128, 0, 384), (3, 384, 384, 128)], [(2, 256, 0, 256)]]

    def __init__(self, core, name, tag, ctx):
        sb = lambda n, shape, dtype=F32: core.sbuf(f"{name}_{n}", shape, dtype, ctx)
        sig = lambda n, per=1: core.semaphore(f"{tag}_{n}", per)
        held, nu = self.HELD, self.NU
        self.norm = NormState(core, sb, sig, "front")
        self.norm1, self.norm2 = NormState(core, sb, sig, "tail1"), NormState(core, sb, sig, "tail2")
        self.pool_carrier = sb("pool_carrier", [P, 1])
        self.xn, self.xt, self.residual = sb("xn", [P, TILES, D]), sb("xt", [P, SEQ]), sb("residual", [P, TILES, D])
        self.v = sb("v", [P, held, TILES, 2, HD64])
        self.part_high, self.part_low = sb("part_high", [P, 2, 2, SEQ], BF16), sb("part_low", [P, 2, 2, SEQ], BF16)
        self.q = sb("q", [P, 2, held, 2, SEQ], BF16)
        self.k = sb("k", [P, 2, held, 2, SEQ], BF16)
        self.neg_max = sb("neg_max", [P, PAIRS, TILES, 2])
        self.max_parts = sb("max_parts", [P, PAIRS, TILES, 2, 2], BF16)
        self.max_t = sb("max_t", [4, PAIRS, SEQ], BF16)
        self.probs = sb("probs", [P, nu * 2, SEQ])
        self.sums = sb("sums", [P, 2, 2, SEQ])
        self.inverse = sb("inverse", [P, SEQ])
        self.y, self.y_norm = sb("y", [P, TILES, D]), sb("y_norm", [P, TILES, D])
        self.cleared, self.ready = sig("cleared"), sig("ready")
        self.link = sig("link")
        self.links = PAIRS + 3 + 2 + 3 + 2 + 2
        self.stage_written, self.stage_read = sig("stage_written"), sig("stage_read")
        self.xn_ready = sig("xn_ready")
        self.high_ready = sig("high_ready", 2 * PAIRS)
        self.placed = [sig(f"placed{p}", 10 * 16) for p in range(PAIRS)]
        self.row_scores, self.row_max = sig("row_scores", PAIRS * TILES * 2), sig("row_max", PAIRS * TILES * 2)
        self.max_ready = sig("max_ready", PAIRS)
        self.max_placed = [sig(f"max_placed{p}", 32) for p in range(PAIRS)]
        self.scores, self.exp_done = sig("scores", PAIRS * nu * 2), sig("exp_done", PAIRS * nu * 2)
        self.added, self.sums_done = sig("added", PAIRS * 4), sig("sums_done", PAIRS)
        self.masked, self.pv_done = sig("masked", PAIRS * nu), sig("pv_done", PAIRS * nu)
        self.inverted, self.out_t_ready = sig("inverted", PAIRS * TILES), sig("out_t_ready", PAIRS)

    NORMS = {(1, 5): "y_norm1", (2, 2): "y_scale", (2, 4): "y_norm2", (3, 0): "y_add", (3, 2): "norm", (3, 5): "xn"}
    AFTER = ["wo", "y_norm1", "y_scale", "y_norm2", "y_add"]
    UNSTAGED = ["y_norm1", "y_scale", "y_norm2", "y_add", "norm", "xn"]

    def before(self):
        steps = [("norm", 0), ("xn", 0), ("xt", 0)]
        for p in range(self.AHEAD):
            steps += [("q", p), ("k", p), ("v", p)]
        return steps + [("max", 0)]

    def beside(self, p, sub, kind):
        names = []
        if sub in (0, 1, 4):
            ahead = p + self.AHEAD
            names.append(({0: "q", 1: "k", 4: "v"}[sub], ahead // PAIRS, ahead % PAIRS))
        if sub == 3:
            names.append(("max", (p + 1) // PAIRS, (p + 1) % PAIRS))
        if (p, sub) == (1, 5):
            names.append(("wo", -1, 0))
        if (p, sub) == (4, 5):
            names.append(("xt", 1, 0))
        if (p, sub) in self.NORMS:
            name = self.NORMS[p, sub]
            names.append((name, -1 if name[0] == "y" else 1, 0))
        return [s for s in names if not (s[1] < 0 and kind == "first") and not (s[1] > 0 and kind == "last")]

    def staged(self, kind):
        if kind == "before":
            steps = self.before()
        elif kind == "after":
            steps = [(name, 0) for name in self.AFTER]
        else:
            steps = [(name, p) for pair in range(PAIRS) for sub in range(self.SUBS)
                     for name, _, p in self.beside(pair, sub, kind)]
        return [name + str(p) for name, p in steps if name not in self.UNSTAGED]

    def stage(self, kind, t):
        count = lambda k: len(self.staged(k))
        base = 0
        if kind in ("mid", "last", "after"):
            base = count("before") + count("first") + (t - 1) * count("mid")
        if kind == "first":
            base = count("before")
        if kind == "after":
            base += count("last") - count("mid")
        return Stage(self.stage_written, self.stage_read, self.staged(kind), base)

    def fills(self, p, sub):
        per_pair = 2 * TILES
        due = lambda s: (p + 2) * per_pair + s * per_pair // self.SUBS
        return range(due(sub), due(sub + 1))


def wide_attention(core, name, tag):
    nc, X, PS, ident, ident_b = core.nc, core.X, core.PS, core.ident, core.ident_b
    PB = PS.bitcast(BF16)
    w_q, w_k, w_v = core.wide_w
    scale = float(HD64) ** -0.5
    ST, OUT, SUMS, STAGE = 2, 4, 6, 7
    FILLS = PAIRS * TILES * 2
    out_t = core.X1[:, :, :].rearrange("p (a c) d -> p a (c d)", a=PAIRS)

    with ExitStack() as ctx:
        s = Wide(core, name, tag, ctx)
        units, nu, held = s.UNITS, s.NU, s.HELD
        block = ctx.enter_context(nc.Block())

        @block.sync
        def _(sp):
            halves = slice(0, HD64), slice(HD64, P)

            def place(stage, p):
                at = p % held
                stage.after(sp, f"q{p}")
                for a in range(2):
                    own, other = halves[a], halves[1 - a]
                    high, low = s.part_high[own, 0, p % 2, :], s.part_low[own, 0, p % 2, :]
                    sp.dma_start(s.q[own, :, at, a, :], high.unsqueeze(1).to_broadcast([HD64, 2, SEQ])).then_inc(
                        s.placed[p].sem, 16)
                    sp.dma_start(s.q[other, 0, at, a, :], low).then_inc(s.placed[p].sem, 16)
                stage.after(sp, f"k{p}")
                for a in range(2):
                    own, other = halves[a], halves[1 - a]
                    high, low = s.part_high[own, 1, p % 2, :], s.part_low[own, 1, p % 2, :]
                    sp.dma_start(s.k[own, 0, at, a, :], high).then_inc(s.placed[p].sem, 16)
                    sp.dma_start(s.k[other, 0, at, a, :], high).then_inc(s.placed[p].sem, 16)
                    sp.dma_start(s.k[own, 1, at, a, :], low).then_inc(s.placed[p].sem, 16)

            def step(stage, name, t, p):
                if name == "k":
                    place(stage, p)
                elif name == "max":
                    stage.after(sp, f"max{p}")
                    at = p % held
                    sp.dma_start(s.q[HD64:HD64 + 2, 1, at, 0, :], s.max_t[0:2, p, :]).then_inc(s.max_placed[p].sem, 16)
                    sp.dma_start(s.q[0:2, 1, at, 1, :], s.max_t[2:4, p, :]).then_inc(s.max_placed[p].sem, 16)

            def before():
                stage = s.stage("before", 0)
                sp.wait_ge(s.ready.sem, 1)
                for name, p in s.before():
                    step(stage, name, 0, p)

            def turn(t, kind):
                stage = s.stage(kind, t)
                for pair in range(PAIRS):
                    for sub in range(s.SUBS):
                        for name, ahead, p in s.beside(pair, sub, kind):
                            step(stage, name, t + ahead, p)

            one_by_one(sp, before, turn, lambda: None)

        @block.gpsimd
        def _(pool):
            nc.gpsimd.memset(s.q[:, 1, :, :, :], 0.0)
            nc.gpsimd.memset(s.k[:, 1, :, :, :], 0.0).then_inc(s.cleared.sem, 1)
            pool.wait_ge(s.cleared.sem, 1)
            nc.gpsimd.memset(s.k[HD64:HD64 + 2, 1, :, 0, :], 1.0).then_inc(s.cleared.sem, 1)
            pool.wait_ge(s.cleared.sem, 2)
            nc.gpsimd.memset(s.k[0:2, 1, :, 1, :], 1.0).then_inc(s.ready.sem, 1)
            pool.wait_ge(s.ready.sem, 1)

            def add_up(t, p, u, kind):
                total, probs = s.sums[:, p % 2, :, :], s.probs
                added = [(0, P)] if u == 0 else [(P, SEQ), (3 * P, SEQ)] if u == 1 else [(2 * P, SEQ)]
                sources = {0: [(0, 0)], 1: [(2, 0), (2, 3 * P)], 2: [(4, 0)]}[u]
                for k, ((first, end), (slot, at)) in enumerate(zip(added, sources)):
                    if u == 0 and not (kind == "first" and p < 2):
                        pool.wait_ge(s.sums_done.sem, s.sums_done.at(t, p - 1))
                    if u == 0:
                        nc.gpsimd.tensor_tensor(s.pool_carrier[:, :], core.minus_half[:, 0:1],
                                                core.minus_half[:, 0:1], ALU.add)
                        last = nc.gpsimd.affine_select(out=total[:, :, 0:P], in_=probs[:, 0:2, 0:P],
                                                       compare_op=ALU.is_ge, fill=0.0, base=0,
                                                       pattern=[[0, 2], [1, P]], channel_multiplier=-1)
                    else:
                        before = probs[:, 0:2, P:SEQ] if (u, k) == (1, 0) else total[:, :, first:end]
                        if (u, k) != (1, 0):
                            pool.wait_ge(s.added.sem, s.added.at(t, 4 * p + u + k))
                        last = nc.gpsimd.tensor_tensor(total[:, :, first:end], before,
                                                       probs[:, slot:slot + 2, at:at + end - first], ALU.add)
                    last.then_inc(s.added.sem, 1)

            def turn(t, kind):
                for n in range(PAIRS * nu):
                    p, u = n // nu, n % nu
                    first = n == 0 and kind == "first"
                    pool.wait_ge(s.exp_done.sem, s.exp_done.at(t, 2 * (n + 1)))
                    if not first:
                        pool.wait_ge(s.added.sem, s.added.at(t, (0, 1, 3)[u] + 4 * p))
                    nc.gpsimd.tensor_tensor(s.pool_carrier[:, :], core.minus_half[:, 0:1], core.minus_half[:, 0:1],
                                            ALU.add)
                    heads = slice(2 * u, 2 * u + 2)
                    for _, _, at, _ in units[u]:
                        square = s.probs[:, heads, at:at + P]
                        last = nc.gpsimd.affine_select(out=square, in_=square, compare_op=ALU.is_ge, fill=0.0,
                                                       base=0, pattern=[[0, 2], [1, P]], channel_multiplier=-1)
                    last.then_inc(s.masked.sem, 1)
                    pool.wait_ge(s.masked.sem, s.masked.at(t, n + 1))
                    add_up(t, p, u, kind)
                    for sub in (n % nu * 2, n % nu * 2 + 1):
                        for name, ahead, _ in s.beside(n // nu, sub, kind):
                            if name in ("norm", "y_norm1", "y_norm2"):
                                norm = {"norm": s.norm, "y_norm1": s.norm1, "y_norm2": s.norm2}[name]
                                norm.power(nc, pool, t + ahead)

            def after():
                s.norm1.power(nc, pool, BATCH - 1)
                s.norm2.power(nc, pool, BATCH - 1)

            one_by_one(pool, lambda: s.norm.power(nc, pool, 0), turn, after)

        @block.vector
        def _(dve):
            dve.wait_ge(core.weights_c.sem, core.weights_c.per_turn)
            counted = [0]

            def row_max(chain, t, n):
                p, c, a = n // (2 * TILES), n // 2 % TILES, n % 2
                dve.wait_ge(s.row_scores.sem, s.row_scores.at(t, n + 1))
                nc.vector.tensor_reduce(s.neg_max[:, p, c, a:a + 1], PS[:, n % 2, 0:P * (c + 1)], AX.X, ALU.max,
                                        negate=True).then_inc(s.row_max.sem, 1)
                if n % (2 * TILES) == 2 * TILES - 1:
                    dve.wait_ge(s.row_max.sem, s.row_max.at(t, n + 1))
                    chain.link(nc.vector.tensor_copy(s.max_parts[:, p, :, :, 0], s.neg_max[:, p, :, :]))
                    nc.vector.tensor_tensor(s.max_parts[:, p, :, :, 1], s.neg_max[:, p, :, :],
                                            s.max_parts[:, p, :, :, 0], ALU.subtract).then_inc(s.max_ready.sem, 1)

            def invert(t, p, c):
                first = isinstance(t, int) and t * PAIRS + p == 0
                if c == 0:
                    dve.wait_ge(s.sums_done.sem, s.sums_done.at(t, p + 1))
                    if not first:
                        dve.wait_ge(s.out_t_ready.sem, s.out_t_ready.at(t, p))
                nc.vector.reciprocal(s.inverse[:, c * P:(c + 1) * P], PS[:, SUMS, c * P:(c + 1) * P]).then_inc(
                    s.inverted.sem, 1)

            def keep_products(t, p):
                dve.wait_ge(s.inverted.sem, s.inverted.at(t, TILES * (p + 1)))
                nc.vector.tensor_tensor(out_t[:, p, :], PS[:, OUT + p % 2, :], s.inverse[:, :], ALU.mult).then_inc(
                    s.out_t_ready.sem, 1)

            def finish_pair(pair, sub, t, kind):
                back, c = {3: (1, 0), 4: (1, 1), 5: (1, 2), 0: (2, 3), 1: (2, TILES)}.get(sub, (0, 0))
                if back and (pair >= back or kind != "first"):
                    t_of, p = (t, pair - back) if pair >= back else (t - 1, pair - back + PAIRS)
                    if c < TILES:
                        invert(t_of, p, c)
                    else:
                        keep_products(t_of, p)

            def step(chain, stage, name, t, p):
                x = lambda c: X[:, t * TILES + c, :]
                link = chain.link
                if name == "norm":
                    if not (isinstance(t, int) and t == 0):
                        link(nc.vector.tensor_copy(s.residual[:, :, :], s.xn[:, :, :]))
                    s.norm.statistics(nc, link, x, 1e-5)
                elif name == "xn":
                    s.norm.apply(nc, dve, t, x, lambda c: s.xn[:, c, :]).then_inc(s.xn_ready.sem, 1)
                elif name in ("q", "k"):
                    n = 2 * p + (name == "k")
                    dve.wait_ge(s.high_ready.sem, s.high_ready.at(t, n + 1))
                    nc.vector.tensor_tensor(s.part_low[:, n % 2, p % 2, :], PS[:, STAGE, :],
                                            s.part_high[:, n % 2, p % 2, :], ALU.subtract).then_inc(
                                                s.stage_read.sem, 1)
                elif name == "wo":
                    stage.drain(dve, "wo0")
                    residual = s.xn if isinstance(t, int) and t == BATCH - 1 else s.residual
                    nc.vector.tensor_tensor(s.y[:, :, :], PS[:, STAGE, :].rearrange("p (c d) -> p c d", d=D),
                                            residual[:, :, :], ALU.add).then_inc(s.stage_read.sem, 1)
                elif name == "y_norm1":
                    stage.after(dve, "wo0")
                    s.norm1.statistics(nc, link, lambda c: s.y[:, c, :], 1e-3)
                elif name == "y_scale":
                    link(s.norm1.apply(nc, dve, t, lambda c: s.y[:, c, :], lambda c: s.y_norm[:, c, :]))
                    scale_shift(nc, link, s.y, s.y_norm, core.wide_gamma, core.wide_beta)
                elif name == "y_norm2":
                    s.norm2.statistics(nc, link, lambda c: s.y[:, c, :], 1e-5)
                elif name == "y_add":
                    link(s.norm2.apply(nc, dve, t, lambda c: s.y[:, c, :], lambda c: s.y_norm[:, c, :]))
                    for c in range(TILES):
                        last = nc.vector.tensor_tensor(x(c), x(c), s.y_norm[:, c, :], ALU.add)
                    link(last)

            def before():
                chain = Chain(dve, s.link, 0)
                stage = s.stage("before", 0)
                for name, p in s.before()[:-1]:
                    step(chain, stage, name, 0, p)
                for n in range(2 * 2 * TILES):
                    row_max(chain, 0, n)
                counted[0] = chain.count

            def turn(t, kind):
                chain = Chain(dve, s.link, counted[0] + (0 if kind == "first" else (t - 1) * s.links))
                stage = s.stage(kind, t)
                for pair in range(PAIRS):
                    for sub in range(s.SUBS):
                        for n in s.fills(pair, sub):
                            if n < FILLS:
                                row_max(chain, t, n)
                            elif kind != "last":
                                row_max(chain, t + 1, n - FILLS)
                        for name, ahead, p in s.beside(pair, sub, kind):
                            step(chain, stage, name, t + ahead, p)
                        finish_pair(pair, sub, t, kind)
                if kind == "first":
                    counted[0] += chain.count
                elif kind == "mid":
                    assert chain.count == s.links, (chain.count, s.links)
                else:
                    counted[0] += (BATCH - 2) * s.links + chain.count

            def after():
                chain = Chain(dve, s.link, counted[0])
                invert(BATCH - 1, PAIRS - 2, TILES - 1)
                keep_products(BATCH - 1, PAIRS - 2)
                for c in range(TILES):
                    invert(BATCH - 1, PAIRS - 1, c)
                keep_products(BATCH - 1, PAIRS - 1)
                for name in s.AFTER:
                    step(chain, s.stage("after", BATCH), name, BATCH - 1, 0)

            one_by_one(dve, before, turn, after)

        @block.scalar
        def _(act):
            def step(stage, name, t, p):
                early = isinstance(t, int)
                if name == "xt":
                    stage.drain(act, "xt0")
                    nc.scalar.activation(s.xt[:, :], PS[:, STAGE, :], ACT.Copy).then_inc(s.stage_read.sem, 1)
                elif name in ("q", "k"):
                    n = 2 * p + (name == "k")
                    stage.drain(act, name + str(p))
                    if p >= 2:
                        act.wait_ge(s.placed[p - 2].sem, s.placed[p - 2].at(t, 10 * 16))
                    elif not (early and t == 0):
                        act.wait_ge(s.placed[p - 2].sem, s.placed[p - 2].at(t, 0))
                    nc.scalar.activation(s.part_high[:, n % 2, p % 2, :], PS[:, STAGE, :], ACT.Copy).then_inc(
                        s.high_ready.sem, 1)
                elif name == "v":
                    stage.drain(act, f"v{p}")
                    if not (early and t * PAIRS + p < held):
                        act.wait_ge(s.pv_done.sem, s.pv_done.at(t, nu * (p - held + 1)))
                    nc.scalar.activation(s.v[:, p % held, :, :, :].rearrange("p c a e -> p (c a e)"),
                                         PS[:, STAGE, :], ACT.Copy).then_inc(s.stage_read.sem, 1)
                elif name == "max":
                    stage.drain(act, f"max{p}")
                    nc.scalar.activation(s.max_t[:, p, :], PB[0:4, STAGE, 0:SEQ], ACT.Copy).then_inc(
                        s.stage_read.sem, 1)

            def before():
                stage = s.stage("before", 0)
                for name, p in s.before():
                    step(stage, name, 0, p)

            def turn(t, kind):
                stage = s.stage(kind, t)
                for pair in range(PAIRS):
                    for sub in range(s.SUBS):
                        n, i = pair * nu + sub // 2, pair * s.SUBS + sub
                        width = sum(w for _, _, _, w in units[n % nu])
                        if n >= nu or kind != "first":
                            act.wait_ge(s.pv_done.sem, s.pv_done.at(t, n - nu + 1))
                            act.wait_ge(s.added.sem, s.added.at(t, 4 * (pair - 1) + (3, 3, 4)[sub // 2]))
                        act.wait_ge(s.scores.sem, s.scores.at(t, i + 1))
                        nc.scalar.activation(s.probs[:, sub, 0:width], PS[:, ST + i % 2, 0:width], ACT.Exp,
                                             scale=scale).then_inc(s.exp_done.sem, 1)
                        for name, ahead, p in s.beside(pair, sub, kind):
                            step(stage, name, t + ahead, p)

            one_by_one(act, before, turn, lambda: None)

        @block.tensor
        def _(pe):
            pe.wait_ge(core.constants_ready.sem, core.constants_ready.per_turn)
            pe.wait_ge(core.weights_c.sem, core.weights_c.per_turn)

            def row_scores(t, n, first):
                p, c, a = n // (2 * TILES), n // 2 % TILES, n % 2
                if n % (2 * TILES) == 0:
                    pe.wait_ge(s.placed[p].sem, s.placed[p].at(t, 10 * 16))
                if n >= 2 or not first:
                    pe.wait_ge(s.row_max.sem, s.row_max.at(t, n - 1))
                keys, at = P * (c + 1), p % held
                nc.tensor.matmul(PS[:, n % 2, 0:keys], s.q[:, 0, at, a, c * P:(c + 1) * P], s.k[:, 0, at, a, 0:keys],
                                 start=True, stop=False)
                nc.tensor.matmul(PS[:, n % 2, keys - P:keys], ident_b[:, :], core.mask[:, :], start=False,
                                 stop=True).then_inc(s.row_scores.sem, 1)

            def products(t, n):
                p, u = n // nu, n % nu
                start = isinstance(t, int) and t == 0
                pe.wait_ge(s.masked.sem, s.masked.at(t, n + 1))
                if u == 0 and not (start and p < 2):
                    pe.wait_ge(s.out_t_ready.sem, s.out_t_ready.at(t, p - 1))
                for i, (k, q0, at, width) in enumerate(units[u]):
                    for a in range(2):
                        last = nc.tensor.matmul(PS[HD64 * a:HD64 * (a + 1), OUT + p % 2, q0:q0 + width],
                                                s.v[:, p % held, k, a, :], s.probs[:, u * 2 + a, at:at + width],
                                                start=u == 0 and i == 0, stop=u == nu - 1 and i == len(units[u]) - 1)
                last.then_inc(s.pv_done.sem, 1)

            def sum_rows(t, p):
                pe.wait_ge(s.added.sem, s.added.at(t, 4 * (p + 1)))
                if not (isinstance(t, int) and t == 0 and p == 0):
                    pe.wait_ge(s.inverted.sem, s.inverted.at(t, TILES * p))
                for a in range(2):
                    last = nc.tensor.matmul(PS[HD64 * a:HD64 * (a + 1), SUMS, :], core.ones[:, 0:HD64],
                                            s.sums[:, p % 2, a, :], start=True, stop=True)
                last.then_inc(s.sums_done.sem, 1)

            def step(stage, name, t, p):
                if name in s.UNSTAGED:
                    return
                stage.fill(pe, name + str(p))
                if name == "xt":
                    pe.wait_ge(s.xn_ready.sem, s.xn_ready.at(t, 1))
                    for c in range(TILES):
                        last = nc.tensor.transpose(PS[:, STAGE, c * P:(c + 1) * P], s.xn[:, c, :], ident[:, :])
                elif name in ("q", "k"):
                    weight = w_q if name == "q" else w_k
                    last = nc.tensor.matmul(PS[:, STAGE, :], weight[:, 2 * p:2 * p + 2, :].rearrange("p h e -> p (h e)"),
                                            s.xt[:, :], start=True, stop=True)
                elif name == "v":
                    for c in range(TILES):
                        last = nc.tensor.matmul(PS[:, STAGE, c * P:(c + 1) * P], s.xt[:, c * P:(c + 1) * P],
                                                w_v[:, 2 * p:2 * p + 2, :].rearrange("p h e -> p (h e)"), start=True,
                                                stop=True)
                elif name == "max":
                    pe.wait_ge(s.max_ready.sem, s.max_ready.at(t, p + 1))
                    for c in range(TILES):
                        last = nc.tensor.transpose(PB[0:4, STAGE, c * P:(c + 1) * P],
                                                   s.max_parts[:, p, c, :, :].rearrange("p a r -> p (a r)"),
                                                   ident_b[:, :])
                elif name == "wo":
                    pe.wait_ge(s.out_t_ready.sem, s.out_t_ready.at(t, PAIRS))
                    for c in range(TILES):
                        for pair in range(PAIRS):
                            last = nc.tensor.matmul(PS[:, STAGE, c * P:(c + 1) * P],
                                                    out_t[:, pair, c * P:(c + 1) * P], core.wide_wo[:, pair, :],
                                                    start=pair == 0, stop=pair == PAIRS - 1)
                last.then_inc(s.stage_written.sem, 1)

            def before():
                stage = s.stage("before", 0)
                for name, p in s.before()[:-1]:
                    step(stage, name, 0, p)
                for n in range(2 * 2 * TILES):
                    row_scores(0, n, True)
                step(stage, "max", 0, 0)

            def turn(t, kind):
                stage = s.stage(kind, t)
                for pair in range(PAIRS):
                    pe.wait_ge(s.max_placed[pair].sem, s.max_placed[pair].at(t, 32))
                    for sub in range(s.SUBS):
                        n, a, i = pair * nu + sub // 2, sub % 2, pair * s.SUBS + sub
                        if i >= 2 or kind != "first":
                            pe.wait_ge(s.exp_done.sem, s.exp_done.at(t, i - 1))
                        for k, q0, at, width in units[n % nu]:
                            bank = PS[:, ST + i % 2, at:at + width]
                            for half in range(2):
                                last = nc.tensor.matmul(bank, s.k[:, half, pair % held, a, k * P:(k + 1) * P],
                                                        s.q[:, half, pair % held, a, q0:q0 + width],
                                                        start=half == 0, stop=half == 1)
                        last.then_inc(s.scores.sem, 1)
                        for m in s.fills(pair, sub):
                            if m < FILLS:
                                row_scores(t, m, False)
                            elif kind != "last":
                                row_scores(t + 1, m - FILLS, False)
                        for name, ahead, p in s.beside(pair, sub, kind):
                            step(stage, name, t + ahead, p)
                        if a:
                            if n:
                                products(t, n - 1)
                            elif kind != "first":
                                products(t - 1, PAIRS * nu - 1)
                        if sub == 2 and (pair or kind != "first"):
                            sum_rows(t if pair else t - 1, (pair - 1) % PAIRS)

            def after():
                products(BATCH - 1, PAIRS * nu - 1)
                sum_rows(BATCH - 1, PAIRS - 1)
                step(s.stage("after", BATCH), "wo", BATCH - 1, 0)

            one_by_one(pe, before, turn, after)


def broadcast_rows(vector):
    return vector.rearrange("(a n) -> a n", a=1).to_broadcast([P, vector.shape[0]])


class Net(Core):

    def __init__(self, nc, ctx, w, x_dram):
        super().__init__(nc, ctx)
        self.w, self.x_dram = w, x_dram
        self.PS = ctx.enter_context(nc.psum_tensor("banks", [P, 8, 512], F32))[:, :, :]
        self.X1 = self.sbuf("tokens1", [P, ALL_TILES, D])
        self.X = self.sbuf("tokens", [P, BATCH * TILES, D])
        self.ident = self.sbuf("ident", [P, P])
        self.ident_b = self.sbuf("ident_b", [P, P], BF16)
        self.mask = self.sbuf("mask", [P, P], BF16)
        self.minus_half = self.sbuf("minus_half", [P, TILES])
        self.constants_made = self.semaphore("constants_made")
        self.constants_ready = self.semaphore("constants_ready", 4)
        self.x_first = self.semaphore("x_first")
        self.x_rest = self.semaphore("x_rest")
        self.loads = []

        def load(signal, target, source):
            self.loads.append((target, source, signal))
            signal.per_turn += 16

        self.weights_a, self.biases_a = self.semaphore("weights_a", 0), self.semaphore("biases_a", 0)
        self.weights_b, self.weights_c = self.semaphore("weights_b", 0), self.semaphore("weights_c", 0)
        self.weights_d, self.biases_d = self.semaphore("weights_d", 0), self.semaphore("biases_d", 0)
        self.weights_e = self.semaphore("weights_e", 0)

        def narrow(tag, prefix, names, weights, biases):
            w_qkv = self.sbuf(f"w_qkv_{tag}", [P, 3 * D])
            b_qkv = self.sbuf(f"b_qkv_{tag}", [P, 3 * D])
            w_o, b_o = self.sbuf(f"w_o_{tag}", [P, D]), self.sbuf(f"b_o_{tag}", [P, D])
            for i, letter in enumerate("qkv"):
                load(weights, w_qkv[:, i * D:(i + 1) * D], w[f"{prefix}_{names[0]}{letter}"])
            load(weights, w_o[:, :], w[f"{prefix}_{names[0]}o"])
            for i, letter in enumerate("qkv"):
                load(biases, b_qkv[:, i * D:(i + 1) * D], broadcast_rows(w[f"{prefix}_b{letter}"]))
            load(biases, b_o[:, :], broadcast_rows(w[f"{prefix}_bo"]))
            return w_qkv, b_qkv, w_o, b_o

        self.ones = self.sbuf("ones", [P, P])
        self.narrow_a = narrow("a", "L0_attn", "w", self.weights_a, self.biases_a)
        self.first_loads = len(self.loads)
        self.w_fc = self.sbuf("w_fc", [P, FC, D])
        load(self.weights_b, self.w_fc[:, :, :], w["L0_ffn_W_fc"].rearrange("(a p) d -> p a d", p=P))
        self.w_proj = self.sbuf("w_proj", [P, FC, P])
        load(self.weights_b, self.w_proj[:, :, :], w["L0_ffn_W_proj"].rearrange("d (a p) -> d a p", p=P))
        self.ln_w, self.ln_b = self.sbuf("ln_w", [P, FC]), self.sbuf("ln_b", [P, FC])
        for tile, key in ((self.ln_w, "L0_ffn_ln_w"), (self.ln_b, "L0_ffn_ln_b")):
            load(self.weights_b, tile[:, :], w[key].rearrange("(a p) -> p a", p=P))
        self.wide_w = []
        for letter in "qkv":
            self.wide_w.append(self.sbuf(f"wide_w{letter}", [P, HEADS, HD64]))
            load(self.weights_c, self.wide_w[-1][:, :, :], w[f"L1_attn_W{letter}"].rearrange("h d e -> d h e"))
        self.wide_wo = self.sbuf("wide_wo", [P, PAIRS, D])
        load(self.weights_c, self.wide_wo[:, :, :], w["L1_attn_Wo"].rearrange("(a p) d -> p a d", p=P))
        self.wide_gamma, self.wide_beta = self.sbuf("wide_gamma", [P, D]), self.sbuf("wide_beta", [P, D])
        load(self.weights_c, self.wide_gamma[:, :], broadcast_rows(w["L1_attn_gamma"]))
        load(self.weights_c, self.wide_beta[:, :], broadcast_rows(w["L1_attn_beta"]))
        self.narrow_d = narrow("d", "L1_ffn", "W", self.weights_d, self.biases_d)
        self.ln1_g, self.ln1_b = self.sbuf("ln1_g", [P, D]), self.sbuf("ln1_b", [P, D])
        load(self.biases_d, self.ln1_g[:, :], broadcast_rows(w["L1_ffn_ln1_g"]))
        load(self.biases_d, self.ln1_b[:, :], broadcast_rows(w["L1_ffn_ln1_b"]))
        self.w1 = self.sbuf("w1", [P, EXPERTS, FF])
        load(self.weights_e, self.w1[:, :, :], w["L1_ffn_W1"].rearrange("e d f -> d e f"))
        self.w2 = self.sbuf("w2", [P, EXPERTS, FC, D])
        load(self.weights_e, self.w2[:, :, :, :], w["L1_ffn_W2"].rearrange("e (a p) d -> p e a d", p=P))
        self.b1 = self.sbuf("b1", [P, EXPERTS * FC])
        load(self.weights_e, self.b1[:, :], w["L1_ffn_b1"].rearrange("e (a p) -> p (e a)", p=P))
        self.b2 = self.sbuf("b2", [P, EXPERTS * D])
        load(self.weights_e, self.b2[:, :], broadcast_rows(w["L1_ffn_b2"].rearrange("e d -> (e d)")))
        self.router_w, self.router_b = self.sbuf("router_w", [P, D]), self.sbuf("router_b", [P, 1])
        load(self.weights_e, self.router_w[:, :], broadcast_rows(w["L1_ffn_router_w"].rearrange("d o -> (d o)")))
        load(self.weights_e, self.router_b[:, :], broadcast_rows(w["L1_ffn_router_b"]))
        self.ln2_g, self.ln2_b = self.sbuf("ln2_g", [P, D]), self.sbuf("ln2_b", [P, D])
        load(self.weights_e, self.ln2_g[:, :], broadcast_rows(w["L1_ffn_ln2_g"]))
        load(self.weights_e, self.ln2_b[:, :], broadcast_rows(w["L1_ffn_ln2_b"]))

    def load_first(self, sp):
        x = self.x_dram.rearrange("b (c p) d -> p b c d", p=P)
        tokens = self.X[:, :, :].rearrange("p (b c) d -> p b c d", c=TILES)
        sp.dma_start(tokens[:, 0], x[:, 0]).then_inc(self.x_first.sem, 16)
        for target, source, signal in self.loads[:self.first_loads]:
            sp.dma_start(target, source).then_inc(signal.sem, 16)
        sp.dma_start(tokens[:, 1:].rearrange("p b c d -> p (b c) d"),
                     x[:, 1:].rearrange("p b c d -> p (b c) d")).then_inc(self.x_rest.sem, 16)

    def load_rest(self, sp):
        for target, source, signal in self.loads[self.first_loads:]:
            with self.nc.allow_non_contiguous_dma(reason="short vectors laid out by feature"):
                sp.dma_start(target, source).then_inc(signal.sem, 16)

    def make_constants(self, pool):
        nc = self.nc
        nc.gpsimd.memset(self.ident[:, :], 0.0)
        nc.gpsimd.memset(self.ident_b[:, :], 0.0)
        nc.gpsimd.memset(self.mask[:, :], 0.0).then_inc(self.constants_made.sem, 1)
        pool.wait_ge(self.constants_made.sem, 1)
        for tile in (self.ident, self.ident_b):
            nc.gpsimd.affine_select(out=tile[:, :], in_=tile[:, :], compare_op=ALU.not_equal, fill=1.0, base=0,
                                    pattern=[[-1, P]], channel_multiplier=1).then_inc(self.constants_ready.sem, 1)
        nc.gpsimd.affine_select(out=self.mask[:, :], in_=self.mask[:, :], compare_op=ALU.is_ge, fill=MASKED, base=0,
                                pattern=[[-1, P]], channel_multiplier=1).then_inc(self.constants_ready.sem, 1)
        nc.gpsimd.memset(self.ones[:, :], 1.0)
        nc.gpsimd.memset(self.minus_half[:, :], -0.5).then_inc(self.constants_ready.sem, 1)


def build(nc, w, x_dram, out):
    with ExitStack() as ctx:
        core = Net(nc, ctx, w, x_dram)
        stored = core.semaphore("stored")
        with nc.Block() as block:
            @block.sync
            def _(sp):
                core.load_first(sp)

            @block.gpsimd
            def _(pool):
                core.make_constants(pool)

        narrow_attention(core, "first", "a", True, *core.narrow_a, (core.weights_a, core.biases_a), add_normalised)
        gelu_ffn(core, "rounded", "b")
        wide_attention(core, "wide", "c")
        narrow_attention(core, "last", "d", False, *core.narrow_d, (core.weights_d, core.biases_d), keep_norm1(core))
        expert_ffn(core, "experts", "e", stored, out)


def kernel(**inputs):
    import numpy as _np
    import concourse.bacc as _bacc
    from concourse import mybir as _mybir
    from concourse.bass_utils import run_bass_kernel_spmd as _run

    nc = _bacc.Bacc("TRN2", target_bir_lowering=False, num_devices=1)
    arrays, handles = {}, {}
    for name, value in inputs.items():
        a = _np.ascontiguousarray(value)
        arrays[f"in_{name}"] = a
        handles[name] = nc.dram_tensor(f"in_{name}", a.shape, _mybir.dt.from_np(a.dtype), kind="ExternalInput").ap()
    out = nc.dram_tensor("out", (BATCH, SEQ, D), F32, kind="ExternalOutput").ap()
    build(nc, handles, handles["L0_attn_x"], out)
    r = _run(nc, [arrays], core_ids=[0])
    return r.results[0]["out"]
```
